# Optimizing a Trainium2 kernel written in Bass

```python
import numpy as np
import jax
import jax.numpy as jnp

def _softmax(x, axis=-1):
    return jax.nn.softmax(x, axis=axis)

def _gelu(x):
    return jax.nn.gelu(x, approximate=True)

def _silu(x):
    return jax.nn.silu(x)

def _sigmoid(x):
    return jax.nn.sigmoid(x)

def _layernorm(x, axis=-1, eps=1e-05):
    m = jnp.mean(x, axis=axis, keepdims=True)
    v = jnp.var(x, axis=axis, keepdims=True)
    return (x - m) / jnp.sqrt(v + eps)

def _scatter_add(tgt, idx, src, axis=0):
    return tgt.at[idx].add(src)

def _segment_sum(src, seg, n):
    return jax.ops.segment_sum(src, seg, n)
kernel_name = 'mk_lm_tower_d4_tok_ids768_r4_9aa925'

def setup_inputs(seed: int=0):
    np.random.seed(seed)
    _w = jnp.asarray

    def _rec_inputs():
        import jax
        import jax.numpy as jnp
        _rk = jax.random.key(seed)
        x = jax.random.randint(jax.random.fold_in(_rk, 1), (8, 512), 0, 31999, jnp.int32)
        itok_BS_0_15 = jax.random.randint(jax.random.fold_in(_rk, 21), (8, 512), 0, 16, jnp.int32)
        itok_BS_0_3 = jax.random.randint(jax.random.fold_in(_rk, 22), (8, 512), 0, 4, jnp.int32)
        itok_BS_0_9999 = jax.random.randint(jax.random.fold_in(_rk, 23), (8, 512), 0, 2500, jnp.int32)
        itok_BS_0_2047 = jax.random.randint(jax.random.fold_in(_rk, 24), (8, 512), 0, 512, jnp.int32)
        fside_BS_age_tau = 49.5725 + 28.8366 * jax.random.normal(jax.random.fold_in(_rk, 25), (8, 512), jnp.float32)
        fside_BS_delays_tau = 49.8282 + 28.8637 * jax.random.normal(jax.random.fold_in(_rk, 26), (8, 512), jnp.float32)
        return (x, itok_BS_0_15, itok_BS_0_3, itok_BS_0_9999, itok_BS_0_2047, fside_BS_age_tau, fside_BS_delays_tau)
    x, itok_BS_0_15, itok_BS_0_3, itok_BS_0_9999, itok_BS_0_2047, fside_BS_age_tau, fside_BS_delays_tau = _rec_inputs()

    def _L0_tok_setup():
        import jax, jax.numpy as jnp
        import numpy as np
        B, S, H = (8, 512, 192)
        VOCAB, MODAL_V, SEG_V, NPI_V, MAX_POS = (8000, 16, 4, 2500, 512)
        LN_EPS = 1e-12

        def _sinusoidal_table(max_pos, hidden):
            pos = np.arange(max_pos, dtype=np.float32)[:, None]
            idx = np.arange(hidden, dtype=np.float32)[None, :]
            angle = pos / np.power(10000.0, 2.0 * idx / hidden)
            tab = np.where(np.arange(hidden)[None, :] % 2 == 0, np.sin(angle), np.cos(angle))
            return jnp.asarray(tab, dtype=jnp.float32)

        def _time2vec(tau, w, b, w0, b0):
            t = tau[..., None]
            v1 = jnp.sin(t * w[0] + b)
            v2 = t * w0[0] + b0
            return jnp.concatenate([v1, v2], axis=-1)

        def _layer_norm(x, gamma, beta, eps):
            mu = jnp.mean(x, axis=-1, keepdims=True)
            var = jnp.mean(jnp.square(x - mu), axis=-1, keepdims=True)
            return (x - mu) * jax.lax.rsqrt(var + eps) * gamma + beta
        key = jax.random.key(seed)
        ks = jax.random.split(key, 16)
        inp = {'word_ids': jax.random.randint(ks[0], (B, S), 0, VOCAB), 'modalities_ids': jax.random.randint(ks[1], (B, S), 0, MODAL_V), 'seg_ids': jax.random.randint(ks[2], (B, S), 0, SEG_V), 'npi_ids': jax.random.randint(ks[3], (B, S), 0, NPI_V), 'posi_ids': jnp.sort(jax.random.randint(ks[4], (B, S), 0, MAX_POS), axis=-1), 'age_tau': jax.random.uniform(ks[5], (B, S), dtype=jnp.float32) * 100.0, 'delays_tau': jax.random.uniform(ks[6], (B, S), dtype=jnp.float32) * 100.0, 'word_table': jax.random.normal(ks[7], (VOCAB, H), dtype=jnp.float32) * 0.02, 'modalities_table': jax.random.normal(ks[8], (MODAL_V, H), dtype=jnp.float32) * 0.02, 'seg_table': jax.random.normal(ks[9], (SEG_V, H), dtype=jnp.float32) * 0.02, 'npi_table': jax.random.normal(ks[10], (NPI_V, H), dtype=jnp.float32) * 0.02, 'posi_table': _sinusoidal_table(MAX_POS, H), 'age_w': jax.random.normal(ks[11], (1, H - 1), dtype=jnp.float32), 'age_b': jax.random.normal(ks[12], (H - 1,), dtype=jnp.float32), 'age_w0': jax.random.normal(ks[13], (1, 1), dtype=jnp.float32), 'age_b0': jax.random.normal(ks[14], (1,), dtype=jnp.float32), 'delay_w': jax.random.normal(ks[15], (1, H - 1), dtype=jnp.float32), 'delay_b': jax.random.normal(jax.random.fold_in(key, 100), (H - 1,), dtype=jnp.float32), 'delay_w0': jax.random.normal(jax.random.fold_in(key, 101), (1, 1), dtype=jnp.float32), 'delay_b0': jax.random.normal(jax.random.fold_in(key, 102), (1,), dtype=jnp.float32), 'ln_gamma': jnp.ones((H,), dtype=jnp.float32), 'ln_beta': jnp.zeros((H,), dtype=jnp.float32)}
        return inp
    _L0_tok_all = _L0_tok_setup()
    _L0_tok_in = {k: v for k, v in _L0_tok_all.items() if k in ('word_table', 'modalities_table', 'seg_table', 'npi_table', 'posi_table', 'age_w', 'age_b', 'age_w0', 'age_b0', 'delay_w', 'delay_b', 'delay_w0', 'delay_b0', 'ln_gamma', 'ln_beta')}
    del _L0_tok_all

    def _L0_attn_setup():
        import jax, jax.numpy as jnp
        import numpy as np
        HEADS = 12
        DIM_HEAD = 64
        SCALE = DIM_HEAD ** (-0.5)
        LN_EPS = 1e-05

        def _ternary(w):
            s = jnp.mean(jnp.abs(w))
            return jnp.clip(jnp.round(w / (s + 1e-08)), -1.0, 1.0) * s

        def _sparsify(x, sparsity):
            thr = jnp.quantile(jnp.abs(x), sparsity, axis=-1, keepdims=True)
            return jnp.where(jnp.abs(x) >= thr, x, 0.0)
        key = jax.random.key(seed)
        ks = jax.random.split(key, 4)
        b, n, dim = (16, 256, 192)
        inner = HEADS * DIM_HEAD
        return {'x': jax.random.normal(ks[0], (b, n, dim), dtype=jnp.float32), 'gamma': jnp.ones((dim,), jnp.float32), 'beta': jnp.zeros((dim,), jnp.float32), 'w_qkv': jax.random.normal(ks[1], (3 * inner, dim), jnp.float32) * 0.02, 'w_out': jax.random.normal(ks[2], (dim, inner), jnp.float32) * 0.02, 'b_out': jnp.zeros((dim,), jnp.float32), 'sparsity': jnp.float32(0.5)}
    _L0_attn_all = _L0_attn_setup()
    _L0_attn_in = {k: v for k, v in _L0_attn_all.items() if k in ('gamma', 'beta', 'w_qkv', 'w_out', 'b_out', 'sparsity')}
    del _L0_attn_all

    def _L0_ffn_setup():
        import jax, jax.numpy as jnp
        import numpy as np
        ACT_SCALE = 0.02
        W_SCALE = 0.01
        EFF_SCALE = ACT_SCALE * W_SCALE
        B, S, D, M = (8, 1024, 192, 192)
        key = jax.random.key(seed)
        kx, kw, kb = jax.random.split(key, 3)
        x = jax.random.normal(kx, (B, S, D), dtype=jnp.float32)
        weight_t = jax.random.randint(kw, (D, M), -128, 128, dtype=jnp.int32).astype(jnp.int8)
        bias = jax.random.normal(kb, (M,), dtype=jnp.float32)
        return {'x': x, 'weight_t': weight_t, 'bias': bias}
    _L0_ffn_all = _L0_ffn_setup()
    _L0_ffn_in = {k: v for k, v in _L0_ffn_all.items() if k in ('weight_t', 'bias')}
    del _L0_ffn_all

    def _L1_attn_setup():
        import jax, jax.numpy as jnp
        import numpy as np
        import math
        B, N, C = (8, 1024, 192)
        H = 12
        DH = C // H
        M = 64
        LN_EPS = 1e-05

        def _phi(t, random_features):
            norm_sq = 0.5 * jnp.sum(t * t, axis=-1, keepdims=True)
            proj = jnp.einsum('bhnd,md->bhnm', t, random_features)
            return jnp.exp(proj - norm_sq) * (1.0 / math.sqrt(M))
        key = jax.random.key(seed)
        ks = jax.random.split(key, 7)
        x = jax.random.normal(ks[0], (B, N, C), dtype=jnp.float32)
        W_qkv = jax.random.normal(ks[1], (C, 3 * C), dtype=jnp.float32) * (1.0 / math.sqrt(C))
        W_proj = jax.random.normal(ks[2], (C, C), dtype=jnp.float32) * (1.0 / math.sqrt(C))
        b_proj = jnp.zeros((C,), dtype=jnp.float32)
        gamma = jnp.ones((C,), dtype=jnp.float32)
        beta = jnp.zeros((C,), dtype=jnp.float32)
        random_features = jax.random.normal(ks[3], (M, DH), dtype=jnp.float32) / math.sqrt(DH)
        return {'x': x, 'W_qkv': W_qkv, 'W_proj': W_proj, 'b_proj': b_proj, 'gamma': gamma, 'beta': beta, 'random_features': random_features}
    _L1_attn_all = _L1_attn_setup()
    _L1_attn_in = {k: v for k, v in _L1_attn_all.items() if k in ('W_qkv', 'W_proj', 'b_proj', 'gamma', 'beta', 'random_features')}
    del _L1_attn_all

    def _L1_ffn_setup():
        import jax, jax.numpy as jnp
        import numpy as np
        B, S, H, I = (4, 512, 192, 384)
        E, K = (3, 2)
        INIT = 0.02

        def _expert(x, gw, uw, dw):
            return jax.nn.silu(x @ gw) * (x @ uw) @ dw
        key = jax.random.key(seed)
        ks = jax.random.split(key, 8)
        f32 = jnp.float32
        return {'x': jax.random.normal(ks[0], (B, S, H), f32), 'shared_gate': jax.random.normal(ks[1], (H, I), f32) * INIT, 'shared_up': jax.random.normal(ks[2], (H, I), f32) * INIT, 'shared_down': jax.random.normal(ks[3], (I, H), f32) * INIT, 'routed_gate': jax.random.normal(ks[4], (E, H, I), f32) * INIT, 'routed_up': jax.random.normal(ks[5], (E, H, I), f32) * INIT, 'routed_down': jax.random.normal(ks[6], (E, I, H), f32) * INIT, 'router_w': jax.random.normal(ks[7], (H, E), f32) * INIT, 'routing_bias': jnp.zeros((E,), f32)}
    _L1_ffn_all = _L1_ffn_setup()
    _L1_ffn_in = {k: v for k, v in _L1_ffn_all.items() if k in ('shared_gate', 'shared_up', 'shared_down', 'routed_gate', 'routed_up', 'routed_down', 'router_w', 'routing_bias')}
    del _L1_ffn_all

    def _L2_attn_setup():
        import jax, jax.numpy as jnp
        import numpy as np
        HIDDEN = 192
        NUM_HEADS = 12
        HEAD_DIM = 64

        def _xavier(key, shape):
            fan_in, fan_out = (shape[1], shape[0])
            limit = float(np.sqrt(6.0 / (fan_in + fan_out)))
            return jax.random.uniform(key, shape, jnp.float32, -limit, limit)
        key = jax.random.key(seed)
        k1, k2, k3 = jax.random.split(key, 3)
        B, N = (4, 512)
        x = jax.random.normal(k1, (B, N, HIDDEN), dtype=jnp.float32)
        qkv_w = _xavier(k2, (3 * NUM_HEADS * HEAD_DIM, HIDDEN))
        qkv_b = jnp.zeros((3 * NUM_HEADS * HEAD_DIM,), jnp.float32)
        proj_w = _xavier(k3, (HIDDEN, NUM_HEADS * HEAD_DIM))
        proj_b = jnp.zeros((HIDDEN,), jnp.float32)
        return {'x': x, 'qkv_w': qkv_w, 'qkv_b': qkv_b, 'proj_w': proj_w, 'proj_b': proj_b}
    _L2_attn_all = _L2_attn_setup()
    _L2_attn_in = {k: v for k, v in _L2_attn_all.items() if k in ('qkv_w', 'qkv_b', 'proj_w', 'proj_b')}
    del _L2_attn_all

    def _L2_ffn_setup():
        import jax, jax.numpy as jnp
        import numpy as np
        B, T, H, F, E = (128, 32, 192, 768, 3)
        key = jax.random.key(seed)
        ks = jax.random.split(key, 4)
        s = 0.02
        return {'x': jax.random.normal(ks[0], (B, T, H), jnp.float32), 'Wg': jax.random.normal(ks[1], (E, H), jnp.float32) * s, 'W1': jax.random.normal(ks[2], (E, H, F), jnp.float32) * s, 'b1': jnp.zeros((E, F), jnp.float32), 'W2': jax.random.normal(ks[3], (E, F, H), jnp.float32) * s, 'b2': jnp.zeros((E, H), jnp.float32)}
    _L2_ffn_all = _L2_ffn_setup()
    _L2_ffn_in = {k: v for k, v in _L2_ffn_all.items() if k in ('Wg', 'W1', 'b1', 'W2', 'b2')}
    del _L2_ffn_all

    def _L3_attn_setup():
        import jax, jax.numpy as jnp
        import numpy as np
        B, S, D, H, E = (8, 196, 192, 12, 8)
        HD = D // H
        FF = 4 * D
        EPS = 1e-05

        def _layernorm(x, g, b):
            mu = jnp.mean(x, axis=-1, keepdims=True)
            var = jnp.var(x, axis=-1, keepdims=True)
            return (x - mu) * jax.lax.rsqrt(var + EPS) * g + b

        def _rotate_half(x):
            x1, x2 = jnp.split(x, 2, axis=-1)
            return jnp.concatenate((-x2, x1), axis=-1)

        def _rope(seq_len):
            inv_freq = 1.0 / 10000.0 ** (jnp.arange(0, HD, 2, dtype=jnp.float32) / HD)
            freqs = jnp.arange(seq_len, dtype=jnp.float32)[:, None] * inv_freq[None, :]
            emb = jnp.concatenate((freqs, freqs), axis=-1)
            return emb[None, :, None, :]

        def _attention(x, Wq, bq, Wk, bk, Wv, bv):
            b, s, _ = x.shape
            q = (x @ Wq + bq).reshape(b, s, H, HD)
            k = (x @ Wk + bk).reshape(b, s, 1, HD)
            v = (x @ Wv + bv).reshape(b, s, 1, HD)
            k = jnp.broadcast_to(k, (b, s, H, HD))
            v = jnp.broadcast_to(v, (b, s, H, HD))
            pe = _rope(s)
            cos, sin = (jnp.cos(pe), jnp.sin(pe))
            q = q * cos + _rotate_half(q) * sin
            k = k * cos + _rotate_half(k) * sin
            scale = HD ** (-0.5)
            attn = jnp.einsum('bshd,bsgd->bshg', q, k) * scale
            attn = jax.nn.softmax(attn, axis=-1)
            out = jnp.einsum('bshg,bsgd->bshd', attn, v)
            return out.reshape(b, s, H * HD)

        def _moe(x, Wg, bg, W1, b1, W2, b2):
            b, s, d = x.shape
            xt = x.reshape(-1, d)
            gates = jax.nn.softmax(xt @ Wg + bg, axis=-1)
            top1 = jnp.argmax(gates, axis=-1)
            out = jnp.zeros_like(xt)
            for e in range(E):
                h = jax.nn.gelu(xt @ W1[e] + b1[e], approximate=False)
                y = h @ W2[e] + b2[e]
                out = jnp.where((top1 == e)[:, None], y, out)
            return out.reshape(b, s, d)
        key = jax.random.key(seed)
        ks = jax.random.split(key, 12)
        s = 0.02
        inp = {'x': jax.random.normal(ks[0], (B, S, D), jnp.float32), 'ln1_g': jnp.ones((D,), jnp.float32), 'ln1_b': jnp.zeros((D,), jnp.float32), 'Wq': jax.random.normal(ks[1], (D, D), jnp.float32) * s, 'bq': jnp.zeros((D,), jnp.float32), 'Wk': jax.random.normal(ks[2], (D, HD), jnp.float32) * s, 'bk': jnp.zeros((HD,), jnp.float32), 'Wv': jax.random.normal(ks[3], (D, HD), jnp.float32) * s, 'bv': jnp.zeros((HD,), jnp.float32), 'ln2_g': jnp.ones((D,), jnp.float32), 'ln2_b': jnp.zeros((D,), jnp.float32), 'Wg': jax.random.normal(ks[4], (D, E), jnp.float32) * s, 'bg': jnp.zeros((E,), jnp.float32), 'W1': jax.random.normal(ks[5], (E, D, FF), jnp.float32) * s, 'b1': jnp.zeros((E, FF), jnp.float32), 'W2': jax.random.normal(ks[6], (E, FF, D), jnp.float32) * s, 'b2': jnp.zeros((E, D), jnp.float32)}
        return inp
    _L3_attn_all = _L3_attn_setup()
    _L3_attn_in = {k: v for k, v in _L3_attn_all.items() if k in ('ln1_g', 'ln1_b', 'Wq', 'bq', 'Wk', 'bk', 'Wv', 'bv', 'ln2_g', 'ln2_b', 'Wg', 'bg', 'W1', 'b1', 'W2', 'b2')}
    del _L3_attn_all

    def _L3_ffn_setup():
        import jax, jax.numpy as jnp
        import numpy as np
        B, S, D, F, E = (8, 512, 192, 768, 16)
        CAP = 64
        EPS = 1e-06

        def _switch_moe_block(x, ln_w, w_router, wi, wo):
            var = jnp.mean(jnp.square(x.astype(jnp.float32)), axis=-1, keepdims=True)
            normed = (x * jax.lax.rsqrt(var + EPS)).astype(x.dtype) * ln_w
            logits = jnp.einsum('bsd,de->bse', normed.astype(jnp.float32), w_router.astype(jnp.float32))
            probs = jax.nn.softmax(logits, axis=-1)
            expert_idx = jnp.argmax(probs, axis=-1)
            onehot = jax.nn.one_hot(expert_idx, E, dtype=jnp.float32)
            priority = jnp.cumsum(onehot, axis=1)
            keep = onehot * (priority <= CAP)
            pos = (priority - 1.0).astype(jnp.int32)
            dispatch = keep[..., None] * jax.nn.one_hot(pos, CAP, dtype=jnp.float32)
            expert_in = jnp.einsum('bsec,bsd->becd', dispatch, normed)
            h = jax.nn.relu(jnp.einsum('becd,edf->becf', expert_in, wi))
            expert_out = jnp.einsum('becf,efd->becd', h, wo)
            combined = jnp.einsum('bsec,becd->bsd', dispatch, expert_out)
            routed = jnp.sum(dispatch, axis=(2, 3)) > 0
            next_states = jnp.where(routed[..., None], combined.astype(x.dtype), normed)
            router_prob = jnp.max(probs, axis=-1, keepdims=True).astype(x.dtype)
            return x + router_prob * next_states
        key = jax.random.key(seed)
        k_x, k_r, k_wi, k_wo = jax.random.split(key, 4)
        x = jax.random.normal(k_x, (B, S, D), dtype=jnp.float32)
        ln_w = jnp.ones((D,), dtype=jnp.float32)
        w_router = jax.random.normal(k_r, (D, E), dtype=jnp.float32) * 0.02
        wi = jax.random.normal(k_wi, (E, D, F), dtype=jnp.float32) * D ** (-0.5)
        wo = jax.random.normal(k_wo, (E, F, D), dtype=jnp.float32) * F ** (-0.5)
        return {'x': x, 'ln_w': ln_w, 'w_router': w_router, 'wi': wi, 'wo': wo}
    _L3_ffn_all = _L3_ffn_setup()
    _L3_ffn_in = {k: v for k, v in _L3_ffn_all.items() if k in ('ln_w', 'w_router', 'wi', 'wo')}
    del _L3_ffn_all
    return {'x': x, 'itok_BS_0_15': itok_BS_0_15, 'itok_BS_0_3': itok_BS_0_3, 'itok_BS_0_9999': itok_BS_0_9999, 'itok_BS_0_2047': itok_BS_0_2047, 'fside_BS_age_tau': fside_BS_age_tau, 'fside_BS_delays_tau': fside_BS_delays_tau, 'L0_tok_word_table': _L0_tok_in['word_table'], 'L0_tok_modalities_table': _L0_tok_in['modalities_table'], 'L0_tok_seg_table': _L0_tok_in['seg_table'], 'L0_tok_npi_table': _L0_tok_in['npi_table'], 'L0_tok_posi_table': _L0_tok_in['posi_table'], 'L0_tok_age_w': _L0_tok_in['age_w'], 'L0_tok_age_b': _L0_tok_in['age_b'], 'L0_tok_age_w0': _L0_tok_in['age_w0'], 'L0_tok_age_b0': _L0_tok_in['age_b0'], 'L0_tok_delay_w': _L0_tok_in['delay_w'], 'L0_tok_delay_b': _L0_tok_in['delay_b'], 'L0_tok_delay_w0': _L0_tok_in['delay_w0'], 'L0_tok_delay_b0': _L0_tok_in['delay_b0'], 'L0_tok_ln_gamma': _L0_tok_in['ln_gamma'], 'L0_tok_ln_beta': _L0_tok_in['ln_beta'], 'L0_attn_gamma': _L0_attn_in['gamma'], 'L0_attn_beta': _L0_attn_in['beta'], 'L0_attn_w_qkv': _L0_attn_in['w_qkv'], 'L0_attn_w_out': _L0_attn_in['w_out'], 'L0_attn_b_out': _L0_attn_in['b_out'], 'L0_attn_sparsity': _L0_attn_in['sparsity'], 'L0_ffn_weight_t': _L0_ffn_in['weight_t'], 'L0_ffn_bias': _L0_ffn_in['bias'], 'L1_attn_W_qkv': _L1_attn_in['W_qkv'], 'L1_attn_W_proj': _L1_attn_in['W_proj'], 'L1_attn_b_proj': _L1_attn_in['b_proj'], 'L1_attn_gamma': _L1_attn_in['gamma'], 'L1_attn_beta': _L1_attn_in['beta'], 'L1_attn_random_features': _L1_attn_in['random_features'], 'L1_ffn_shared_gate': _L1_ffn_in['shared_gate'], 'L1_ffn_shared_up': _L1_ffn_in['shared_up'], 'L1_ffn_shared_down': _L1_ffn_in['shared_down'], 'L1_ffn_routed_gate': _L1_ffn_in['routed_gate'], 'L1_ffn_routed_up': _L1_ffn_in['routed_up'], 'L1_ffn_routed_down': _L1_ffn_in['routed_down'], 'L1_ffn_router_w': _L1_ffn_in['router_w'], 'L1_ffn_routing_bias': _L1_ffn_in['routing_bias'], 'L2_attn_qkv_w': _L2_attn_in['qkv_w'], 'L2_attn_qkv_b': _L2_attn_in['qkv_b'], 'L2_attn_proj_w': _L2_attn_in['proj_w'], 'L2_attn_proj_b': _L2_attn_in['proj_b'], 'L2_ffn_Wg': _L2_ffn_in['Wg'], 'L2_ffn_W1': _L2_ffn_in['W1'], 'L2_ffn_b1': _L2_ffn_in['b1'], 'L2_ffn_W2': _L2_ffn_in['W2'], 'L2_ffn_b2': _L2_ffn_in['b2'], 'L3_attn_ln1_g': _L3_attn_in['ln1_g'], 'L3_attn_ln1_b': _L3_attn_in['ln1_b'], 'L3_attn_Wq': _L3_attn_in['Wq'], 'L3_attn_bq': _L3_attn_in['bq'], 'L3_attn_Wk': _L3_attn_in['Wk'], 'L3_attn_bk': _L3_attn_in['bk'], 'L3_attn_Wv': _L3_attn_in['Wv'], 'L3_attn_bv': _L3_attn_in['bv'], 'L3_attn_ln2_g': _L3_attn_in['ln2_g'], 'L3_attn_ln2_b': _L3_attn_in['ln2_b'], 'L3_attn_Wg': _L3_attn_in['Wg'], 'L3_attn_bg': _L3_attn_in['bg'], 'L3_attn_W1': _L3_attn_in['W1'], 'L3_attn_b1': _L3_attn_in['b1'], 'L3_attn_W2': _L3_attn_in['W2'], 'L3_attn_b2': _L3_attn_in['b2'], 'L3_ffn_ln_w': _L3_ffn_in['ln_w'], 'L3_ffn_w_router': _L3_ffn_in['w_router'], 'L3_ffn_wi': _L3_ffn_in['wi'], 'L3_ffn_wo': _L3_ffn_in['wo']}

def reference(x, itok_BS_0_15, itok_BS_0_3, itok_BS_0_9999, itok_BS_0_2047, fside_BS_age_tau, fside_BS_delays_tau, L0_tok_word_table, L0_tok_modalities_table, L0_tok_seg_table, L0_tok_npi_table, L0_tok_posi_table, L0_tok_age_w, L0_tok_age_b, L0_tok_age_w0, L0_tok_age_b0, L0_tok_delay_w, L0_tok_delay_b, L0_tok_delay_w0, L0_tok_delay_b0, L0_tok_ln_gamma, L0_tok_ln_beta, L0_attn_gamma, L0_attn_beta, L0_attn_w_qkv, L0_attn_w_out, L0_attn_b_out, L0_attn_sparsity, L0_ffn_weight_t, L0_ffn_bias, L1_attn_W_qkv, L1_attn_W_proj, L1_attn_b_proj, L1_attn_gamma, L1_attn_beta, L1_attn_random_features, L1_ffn_shared_gate, L1_ffn_shared_up, L1_ffn_shared_down, L1_ffn_routed_gate, L1_ffn_routed_up, L1_ffn_routed_down, L1_ffn_router_w, L1_ffn_routing_bias, L2_attn_qkv_w, L2_attn_qkv_b, L2_attn_proj_w, L2_attn_proj_b, L2_ffn_Wg, L2_ffn_W1, L2_ffn_b1, L2_ffn_W2, L2_ffn_b2, L3_attn_ln1_g, L3_attn_ln1_b, L3_attn_Wq, L3_attn_bq, L3_attn_Wk, L3_attn_bk, L3_attn_Wv, L3_attn_bv, L3_attn_ln2_g, L3_attn_ln2_b, L3_attn_Wg, L3_attn_bg, L3_attn_W1, L3_attn_b1, L3_attn_W2, L3_attn_b2, L3_ffn_ln_w, L3_ffn_w_router, L3_ffn_wi, L3_ffn_wo):
    import jax
    import jax.numpy as jnp

    def _L0_tok_ref(word_ids, modalities_ids, seg_ids, npi_ids, posi_ids, age_tau, delays_tau, word_table, modalities_table, seg_table, npi_table, posi_table, age_w, age_b, age_w0, age_b0, delay_w, delay_b, delay_w0, delay_b0, ln_gamma, ln_beta):
        import jax, jax.numpy as jnp
        import numpy as np
        B, S, H = (8, 512, 192)
        VOCAB, MODAL_V, SEG_V, NPI_V, MAX_POS = (8000, 16, 4, 2500, 512)
        LN_EPS = 1e-12

        def _sinusoidal_table(max_pos, hidden):
            pos = np.arange(max_pos, dtype=np.float32)[:, None]
            idx = np.arange(hidden, dtype=np.float32)[None, :]
            angle = pos / np.power(10000.0, 2.0 * idx / hidden)
            tab = np.where(np.arange(hidden)[None, :] % 2 == 0, np.sin(angle), np.cos(angle))
            return jnp.asarray(tab, dtype=jnp.float32)

        def _time2vec(tau, w, b, w0, b0):
            t = tau[..., None]
            v1 = jnp.sin(t * w[0] + b)
            v2 = t * w0[0] + b0
            return jnp.concatenate([v1, v2], axis=-1)

        def _layer_norm(x, gamma, beta, eps):
            mu = jnp.mean(x, axis=-1, keepdims=True)
            var = jnp.mean(jnp.square(x - mu), axis=-1, keepdims=True)
            return (x - mu) * jax.lax.rsqrt(var + eps) * gamma + beta
        word_e = word_table[word_ids]
        seg_e = seg_table[seg_ids]
        modal_e = modalities_table[modalities_ids]
        npi_e = npi_table[npi_ids]
        posi_e = posi_table[posi_ids]
        age_e = _time2vec(age_tau, age_w, age_b, age_w0, age_b0)
        delay_e = _time2vec(delays_tau, delay_w, delay_b, delay_w0, delay_b0)
        emb = word_e + seg_e + posi_e + modal_e + delay_e + age_e + npi_e
        emb = _layer_norm(emb, ln_gamma, ln_beta, LN_EPS)
        return emb

    def _L0_attn_ref(x, gamma, beta, w_qkv, w_out, b_out, sparsity):
        import jax, jax.numpy as jnp
        import numpy as np
        HEADS = 12
        DIM_HEAD = 64
        SCALE = DIM_HEAD ** (-0.5)
        LN_EPS = 1e-05

        def _ternary(w):
            s = jnp.mean(jnp.abs(w))
            return jnp.clip(jnp.round(w / (s + 1e-08)), -1.0, 1.0) * s

        def _sparsify(x, sparsity):
            thr = jnp.quantile(jnp.abs(x), sparsity, axis=-1, keepdims=True)
            return jnp.where(jnp.abs(x) >= thr, x, 0.0)
        b, n, dim = x.shape
        mu = jnp.mean(x, axis=-1, keepdims=True)
        var = jnp.mean((x - mu) ** 2, axis=-1, keepdims=True)
        xn = (x - mu) * jax.lax.rsqrt(var + LN_EPS) * gamma + beta
        qkv = jnp.einsum('bnd,ed->bne', _sparsify(xn, sparsity), _ternary(w_qkv))
        q, k, v = jnp.split(qkv, 3, axis=-1)

        def heads(t):
            return t.reshape(b, n, HEADS, DIM_HEAD).transpose(0, 2, 1, 3)
        q, k, v = (heads(q), heads(k), heads(v))
        dots = jnp.einsum('bhid,bhjd->bhij', q, k) * SCALE
        attn = jax.nn.softmax(dots, axis=-1)
        out = jnp.einsum('bhij,bhjd->bhid', attn, v)
        out = out.transpose(0, 2, 1, 3).reshape(b, n, HEADS * DIM_HEAD)
        out = jnp.einsum('bne,de->bnd', _sparsify(out, sparsity), _ternary(w_out)) + b_out
        return out

    def _L0_ffn_ref(x, weight_t, bias):
        import jax, jax.numpy as jnp
        import numpy as np
        ACT_SCALE = 0.02
        W_SCALE = 0.01
        EFF_SCALE = ACT_SCALE * W_SCALE
        B, S, D, M = (8, 1024, 192, 192)
        orig_shape = x.shape
        x_flat = x.reshape(-1, orig_shape[-1])
        x_int8 = jnp.clip(jnp.round(x_flat / ACT_SCALE), -128, 127).astype(jnp.int8)
        acc_i32 = jnp.matmul(x_int8, weight_t, preferred_element_type=jnp.int32)
        out = acc_i32.astype(jnp.float32) * jnp.float32(EFF_SCALE) + bias
        return out.reshape(orig_shape[:-1] + (M,))

    def _L1_attn_ref(x, W_qkv, W_proj, b_proj, gamma, beta, random_features):
        import jax, jax.numpy as jnp
        import numpy as np
        import math
        B, N, C = (8, 1024, 192)
        H = 12
        DH = C // H
        M = 64
        LN_EPS = 1e-05

        def _phi(t, random_features):
            norm_sq = 0.5 * jnp.sum(t * t, axis=-1, keepdims=True)
            proj = jnp.einsum('bhnd,md->bhnm', t, random_features)
            return jnp.exp(proj - norm_sq) * (1.0 / math.sqrt(M))
        b, n, c = x.shape
        qkv = (x @ W_qkv).reshape(b, n, 3, H, DH)
        qkv = jnp.transpose(qkv, (2, 0, 3, 1, 4))
        q, k, v = (qkv[0], qkv[1], qkv[2])
        q_p = _phi(q, random_features)
        k_p = _phi(k, random_features)
        kv = jnp.einsum('bhnm,bhnd->bhmd', k_p, v)
        out = jnp.einsum('bhnm,bhmd->bhnd', q_p, kv)
        k_sum = jnp.sum(k_p, axis=2)
        normalizer = jnp.einsum('bhnm,bhm->bhn', q_p, k_sum)[..., None]
        out = out / (normalizer + 1e-06)
        x_attn = jnp.transpose(out, (0, 2, 1, 3)).reshape(b, n, c)
        x_attn = x_attn @ W_proj + b_proj
        y = x + x_attn
        mu = jnp.mean(y, axis=-1, keepdims=True)
        var = jnp.mean(jnp.square(y - mu), axis=-1, keepdims=True)
        return (y - mu) * jax.lax.rsqrt(var + LN_EPS) * gamma + beta

    def _L1_ffn_ref(x, shared_gate, shared_up, shared_down, routed_gate, routed_up, routed_down, router_w, routing_bias):
        import jax, jax.numpy as jnp
        import numpy as np
        B, S, H, I = (4, 512, 192, 384)
        E, K = (3, 2)
        INIT = 0.02

        def _expert(x, gw, uw, dw):
            return jax.nn.silu(x @ gw) * (x @ uw) @ dw
        shared_out = _expert(x, shared_gate, shared_up, shared_down)
        routing_probs = jax.nn.sigmoid(x @ router_w + routing_bias)
        scores, indices = jax.lax.top_k(routing_probs, K)
        scores = scores / scores.sum(axis=-1, keepdims=True)
        combine_w = (jax.nn.one_hot(indices, E, dtype=x.dtype) * scores[..., None]).sum(axis=-2)
        g = jnp.einsum('bsh,ehi->ebsi', x, routed_gate)
        u = jnp.einsum('bsh,ehi->ebsi', x, routed_up)
        h = jax.nn.silu(g) * u
        out_e = jnp.einsum('ebsi,eih->ebsh', h, routed_down)
        combined = jnp.einsum('ebsh,bse->bsh', out_e, combine_w)
        return shared_out + combined

    def _L2_attn_ref(x, qkv_w, qkv_b, proj_w, proj_b):
        import jax, jax.numpy as jnp
        import numpy as np
        HIDDEN = 192
        NUM_HEADS = 12
        HEAD_DIM = 64

        def _xavier(key, shape):
            fan_in, fan_out = (shape[1], shape[0])
            limit = float(np.sqrt(6.0 / (fan_in + fan_out)))
            return jax.random.uniform(key, shape, jnp.float32, -limit, limit)
        B, N, _ = x.shape
        nh, H = (NUM_HEADS, HEAD_DIM)
        qkv = jnp.einsum('bnd,od->bno', x, qkv_w) + qkv_b
        q, k, v = jnp.split(qkv, 3, axis=-1)

        def heads(t):
            return t.reshape(B, N, nh, H).transpose(0, 2, 1, 3)
        q, k, v = (heads(q), heads(k), heads(v))
        scores = jnp.einsum('bhnd,bhmd->bhnm', q, k) / jnp.sqrt(jnp.float32(H))
        attn = jax.nn.softmax(scores, axis=-1)
        out = jnp.einsum('bhnm,bhmd->bhnd', attn, v)
        out = out.transpose(0, 2, 1, 3).reshape(B, N, nh * H)
        out = jnp.einsum('bnk,ok->bno', out, proj_w) + proj_b
        return out

    def _L2_ffn_ref(x, Wg, W1, b1, W2, b2):
        import jax, jax.numpy as jnp
        import numpy as np
        B, T, H, F, E = (128, 32, 192, 768, 3)
        scores = jax.nn.softmax(jnp.mean(x, axis=1) @ Wg.T, axis=-1)
        _, idx = jax.lax.top_k(scores, 1)
        sel = idx[:, 0]
        h = jax.nn.gelu(jnp.einsum('bth,ehf->betf', x, W1) + b1[None, :, None, :], approximate=False)
        y = jnp.einsum('betf,efh->beth', h, W2) + b2[None, :, None, :]
        w = scores * jax.nn.one_hot(sel, E, dtype=scores.dtype)
        out = jnp.einsum('beth,be->bth', y, w)
        return out

    def _L3_attn_ref(x, ln1_g, ln1_b, Wq, bq, Wk, bk, Wv, bv, ln2_g, ln2_b, Wg, bg, W1, b1, W2, b2):
        import jax, jax.numpy as jnp
        import numpy as np
        B, S, D, H, E = (8, 196, 192, 12, 8)
        HD = D // H
        FF = 4 * D
        EPS = 1e-05

        def _layernorm(x, g, b):
            mu = jnp.mean(x, axis=-1, keepdims=True)
            var = jnp.var(x, axis=-1, keepdims=True)
            return (x - mu) * jax.lax.rsqrt(var + EPS) * g + b

        def _rotate_half(x):
            x1, x2 = jnp.split(x, 2, axis=-1)
            return jnp.concatenate((-x2, x1), axis=-1)

        def _rope(seq_len):
            inv_freq = 1.0 / 10000.0 ** (jnp.arange(0, HD, 2, dtype=jnp.float32) / HD)
            freqs = jnp.arange(seq_len, dtype=jnp.float32)[:, None] * inv_freq[None, :]
            emb = jnp.concatenate((freqs, freqs), axis=-1)
            return emb[None, :, None, :]

        def _attention(x, Wq, bq, Wk, bk, Wv, bv):
            b, s, _ = x.shape
            q = (x @ Wq + bq).reshape(b, s, H, HD)
            k = (x @ Wk + bk).reshape(b, s, 1, HD)
            v = (x @ Wv + bv).reshape(b, s, 1, HD)
            k = jnp.broadcast_to(k, (b, s, H, HD))
            v = jnp.broadcast_to(v, (b, s, H, HD))
            pe = _rope(s)
            cos, sin = (jnp.cos(pe), jnp.sin(pe))
            q = q * cos + _rotate_half(q) * sin
            k = k * cos + _rotate_half(k) * sin
            scale = HD ** (-0.5)
            attn = jnp.einsum('bshd,bsgd->bshg', q, k) * scale
            attn = jax.nn.softmax(attn, axis=-1)
            out = jnp.einsum('bshg,bsgd->bshd', attn, v)
            return out.reshape(b, s, H * HD)

        def _moe(x, Wg, bg, W1, b1, W2, b2):
            b, s, d = x.shape
            xt = x.reshape(-1, d)
            gates = jax.nn.softmax(xt @ Wg + bg, axis=-1)
            top1 = jnp.argmax(gates, axis=-1)
            out = jnp.zeros_like(xt)
            for e in range(E):
                h = jax.nn.gelu(xt @ W1[e] + b1[e], approximate=False)
                y = h @ W2[e] + b2[e]
                out = jnp.where((top1 == e)[:, None], y, out)
            return out.reshape(b, s, d)
        res = x
        h = _layernorm(x, ln1_g, ln1_b)
        h = _attention(h, Wq, bq, Wk, bk, Wv, bv)
        x = res + h
        res = x
        h = _layernorm(x, ln2_g, ln2_b)
        h = _moe(h, Wg, bg, W1, b1, W2, b2)
        return res + h

    def _L3_ffn_ref(x, ln_w, w_router, wi, wo):
        import jax, jax.numpy as jnp
        import numpy as np
        B, S, D, F, E = (8, 512, 192, 768, 16)
        CAP = 64
        EPS = 1e-06

        def _switch_moe_block(x, ln_w, w_router, wi, wo):
            var = jnp.mean(jnp.square(x.astype(jnp.float32)), axis=-1, keepdims=True)
            normed = (x * jax.lax.rsqrt(var + EPS)).astype(x.dtype) * ln_w
            logits = jnp.einsum('bsd,de->bse', normed.astype(jnp.float32), w_router.astype(jnp.float32))
            probs = jax.nn.softmax(logits, axis=-1)
            expert_idx = jnp.argmax(probs, axis=-1)
            onehot = jax.nn.one_hot(expert_idx, E, dtype=jnp.float32)
            priority = jnp.cumsum(onehot, axis=1)
            keep = onehot * (priority <= CAP)
            pos = (priority - 1.0).astype(jnp.int32)
            dispatch = keep[..., None] * jax.nn.one_hot(pos, CAP, dtype=jnp.float32)
            expert_in = jnp.einsum('bsec,bsd->becd', dispatch, normed)
            h = jax.nn.relu(jnp.einsum('becd,edf->becf', expert_in, wi))
            expert_out = jnp.einsum('becf,efd->becd', h, wo)
            combined = jnp.einsum('bsec,becd->bsd', dispatch, expert_out)
            routed = jnp.sum(dispatch, axis=(2, 3)) > 0
            next_states = jnp.where(routed[..., None], combined.astype(x.dtype), normed)
            router_prob = jnp.max(probs, axis=-1, keepdims=True).astype(x.dtype)
            return x + router_prob * next_states
        return _switch_moe_block(x, ln_w, w_router, wi, wo)
    h = _L0_tok_ref(x, itok_BS_0_15, itok_BS_0_3, itok_BS_0_9999, itok_BS_0_2047, fside_BS_age_tau, fside_BS_delays_tau, L0_tok_word_table, L0_tok_modalities_table, L0_tok_seg_table, L0_tok_npi_table, L0_tok_posi_table, L0_tok_age_w, L0_tok_age_b, L0_tok_age_w0, L0_tok_age_b0, L0_tok_delay_w, L0_tok_delay_b, L0_tok_delay_w0, L0_tok_delay_b0, L0_tok_ln_gamma, L0_tok_ln_beta)
    h = h + _L0_attn_ref(_layernorm(h, axis=-1), L0_attn_gamma, L0_attn_beta, L0_attn_w_qkv, L0_attn_w_out, L0_attn_b_out, L0_attn_sparsity)
    h = h + _L0_ffn_ref(_layernorm(h, axis=-1), L0_ffn_weight_t, L0_ffn_bias)
    h = h + _L1_attn_ref(_layernorm(h, axis=-1), L1_attn_W_qkv, L1_attn_W_proj, L1_attn_b_proj, L1_attn_gamma, L1_attn_beta, L1_attn_random_features)
    h = h + _L1_ffn_ref(_layernorm(h, axis=-1), L1_ffn_shared_gate, L1_ffn_shared_up, L1_ffn_shared_down, L1_ffn_routed_gate, L1_ffn_routed_up, L1_ffn_routed_down, L1_ffn_router_w, L1_ffn_routing_bias)
    h = h + _L2_attn_ref(_layernorm(h, axis=-1), L2_attn_qkv_w, L2_attn_qkv_b, L2_attn_proj_w, L2_attn_proj_b)
    h = h + _L2_ffn_ref(_layernorm(h, axis=-1), L2_ffn_Wg, L2_ffn_W1, L2_ffn_b1, L2_ffn_W2, L2_ffn_b2)
    h = h + _L3_attn_ref(_layernorm(h, axis=-1), L3_attn_ln1_g, L3_attn_ln1_b, L3_attn_Wq, L3_attn_bq, L3_attn_Wk, L3_attn_bk, L3_attn_Wv, L3_attn_bv, L3_attn_ln2_g, L3_attn_ln2_b, L3_attn_Wg, L3_attn_bg, L3_attn_W1, L3_attn_b1, L3_attn_W2, L3_attn_b2)
    h = h + _L3_ffn_ref(_layernorm(h, axis=-1), L3_ffn_ln_w, L3_ffn_w_router, L3_ffn_wi, L3_ffn_wo)
    return h

_drawn_inputs = setup_inputs


def setup_inputs(seed=0):
    import zlib

    import numpy as np

    out = dict(_drawn_inputs(seed))
    spreads = {'L0_tok_ln_gamma': (1.0, 0.2),
     'L0_tok_ln_beta': (0.0, 0.1),
     'L0_attn_gamma': (1.0, 0.2),
     'L0_attn_beta': (0.0, 0.307),
     'L0_attn_b_out': (0.0, 0.1),
     'L1_attn_b_proj': (0.0, 0.595),
     'L1_attn_gamma': (1.0, 0.539),
     'L1_attn_beta': (0.0, 0.516),
     'L1_ffn_routing_bias': (0.0, 0.8),
     'L2_attn_qkv_b': (0.0, 0.421),
     'L2_attn_proj_b': (0.0, 0.563),
     'L2_ffn_b1': (0.0, 0.8),
     'L2_ffn_b2': (0.0, 0.8),
     'L3_attn_ln1_g': (1.0, 0.6),
     'L3_attn_ln1_b': (0.0, 0.8),
     'L3_attn_bq': (0.0, 0.1),
     'L3_attn_bk': (0.0, 0.1),
     'L3_attn_bv': (0.0, 0.495),
     'L3_attn_ln2_g': (1.0, 0.6),
     'L3_attn_ln2_b': (0.0, 0.8),
     'L3_attn_bg': (0.0, 0.573),
     'L3_attn_b1': (0.0, 0.8),
     'L3_attn_b2': (0.0, 0.566),
     'L3_ffn_ln_w': (1.0, 0.6)}
    factors = {'L0_tok_word_table': 3.061,
     'L0_tok_modalities_table': 3.142,
     'L0_tok_seg_table': 3.241,
     'L0_tok_npi_table': 3.086,
     'L1_attn_random_features': 8.0,
     'L1_ffn_shared_gate': 8.0,
     'L1_ffn_shared_up': 8.0,
     'L1_ffn_shared_down': 8.0,
     'L1_ffn_routed_gate': 8.0,
     'L1_ffn_routed_up': 8.0,
     'L1_ffn_routed_down': 8.0,
     'L1_ffn_router_w': 8.0,
     'L2_ffn_Wg': 7.954,
     'L2_ffn_W1': 8.0,
     'L2_ffn_W2': 8.0,
     'L3_attn_Wg': 3.465,
     'L3_attn_W1': 5.149,
     'L3_attn_W2': 4.9,
     'L3_ffn_w_router': 7.14,
     'L3_ffn_wi': 8.0,
     'L3_ffn_wo': 7.954}
    for name, (base, spread) in spreads.items():
        noise = np.random.default_rng([zlib.crc32(name.encode()), seed]).standard_normal(out[name].shape)
        drawn = base * np.exp(spread * noise) if base else spread * noise
        out[name] = jnp.asarray(drawn.astype(out[name].dtype))
    for name, factor in factors.items():
        out[name] = (out[name] * factor).astype(out[name].dtype)
    return out
```

```python
from contextlib import ExitStack

import numpy as np

import concourse.bass as bass
from concourse import mybir

F32 = mybir.dt.float32
BF16 = mybir.dt.bfloat16
I32 = mybir.dt.int32
U32 = mybir.dt.uint32
I8 = mybir.dt.int8
ALU = mybir.AluOpType
ACT = mybir.ActivationFunctionType
AX = mybir.AxisListType

P = 128
B, S, D = 8, 512, 192
T = B * S
NT = T // P
TB = S // P
KC, KP = 2, D // 2
ROUND = 1.5 * 2 ** 23


class Chain:

    def __init__(self, eng, sem):
        self.eng, self.sem, self.n = eng, sem, 0

    def mark(self, ins):
        ins.then_inc(self.sem, 1)
        self.n += 1
        return self.n

    def wait(self, n=None):
        self.eng.wait_ge(self.sem, self.n if n is None else n)

    def close(self):
        self.wait()
        self.eng.sem_clear(self.sem)

    def link(self, ins):
        self.mark(ins)
        self.wait()


class Stage:

    def __init__(self, nc, ctx, name):
        self.nc, self.ctx, self.name, self.sems = nc, ctx, name, []
        ctx.callback(self.end)

    def sb(self, name, shape, dt=F32):
        return self.ctx.enter_context(self.nc.sbuf_tensor(f"{self.name}_{name}", shape, dt))

    def ps(self, name, shape, dt=F32):
        return self.ctx.enter_context(self.nc.psum_tensor(f"{self.name}_{name}", shape, dt))

    def sem(self, name):
        self.sems.append(self.nc.alloc_semaphore(f"{self.name}_{name}"))
        return self.sems[-1]

    def end(self):
        self.nc.clear_and_free_semaphores(self.sems)
        self.nc.all_engine_barrier()


def batch_tiles(h):
    return h.rearrange("(b t p) d -> b p t d", t=TB, p=P)


def bcast(ap, shape):
    return ap.broadcast_to(shape)


def make_identity(pool, chain, ident):
    chain.link(pool.memset(ident, 0.0))
    return pool.affine_select(out=ident, in_=ident, compare_op=ALU.not_equal, fill=1.0, base=0,
                              pattern=[[-1, ident.shape[1]]], channel_multiplier=1)


def norm_stats(dve, c, x, stats, mv, eps, veps):
    n = x.shape[1]
    for t in range(n):
        c.mark(dve.bn_stats(stats[:, t, :], x[:, t, :]))
    c.wait()
    for t in range(n):
        c.mark(dve.bn_aggr(mv[:, t, :], stats[:, t, :]))
    c.wait()
    return dve.tensor_scalar(veps, mv[:, :, 1], eps, None, ALU.add)


def norm_apply(dve, c, out, x, mv, rstd):
    for t in range(x.shape[1]):
        c.mark(dve.tensor_scalar(out[:, t, :], x[:, t, :], mv[:, t, 0:1], rstd[:, t:t + 1],
                                 ALU.subtract, ALU.mult))


def quant_linear_stage(nc, A, h_in, h_out):
    with ExitStack() as ctx:
        st = Stage(nc, ctx, "l0f")
        x = st.sb("x", [P, 2, TB, D])
        y = st.sb("y", [P, TB, D])
        q = st.sb("q", [P, TB, D], BF16)
        qT = st.sb("qT", [KP, KC, S], BF16)
        w8 = st.sb("w8", [KP, KC, D // 4], I32)
        w = st.sb("w", [KP, KC, D], BF16)
        bias = st.sb("bias", [P, D])
        o = st.sb("o", [P, 2, TB, D])
        ident = st.sb("ident", [P, P], BF16)
        stats = st.sb("stats", [P, TB, 6])
        mv = st.sb("mv", [P, TB, 2])
        veps = st.sb("veps", [P, TB])
        rstd = st.sb("rstd", [P, TB])
        mhalf = st.sb("mhalf", [P, TB])
        psT = st.ps("psT", [P, KC, 1024], BF16)
        psO = st.ps("psO", [P, TB, 512])
        s_x, s_out = [st.sem(f"x{u}") for u in range(2)], [st.sem(f"out{u}") for u in range(2)]
        s_w = st.sem("w")
        s_xfree, s_var, s_rstd, s_q, s_T, s_qT, s_y, s_o = (
            st.sem(n) for n in ("xfree", "var", "rstd", "q", "T", "qT", "y", "o"))
        s_ident, s_wb, s_dve, s_pool = st.sem("ident"), st.sem("wb"), st.sem("dve"), st.sem("pool")
        hi, ho = batch_tiles(h_in), batch_tiles(h_out)
        with nc.Block() as block:

            @block.sync
            def _(sp):
                sp.dma_start(w8[:], A["L0_ffn_weight_t"].rearrange("(c p) n -> p c n", p=KP)).then_inc(s_w, 16)
                sp.dma_start(bias[:], A["L0_ffn_bias"].partition_broadcast(P)).then_inc(s_w, 16)
                with sp.Fori(0, B // 2) as i:
                    for u in range(2):
                        b = i * 2 + u
                        sp.wait_ge(s_xfree, b + 1)
                        sp.dma_start(x[:, u], hi[b]).then_inc(s_x[u], 16)

            @block.gpsimd
            def _(pool):
                c = Chain(pool, s_pool)
                make_identity(pool, c, ident[:]).then_inc(s_ident, 1)
                c.link(pool.memset(mhalf[:], -0.5))
                with pool.Fori(0, B // 2) as i:
                    for u in range(2):
                        b = i * 2 + u
                        pool.wait_ge(s_var, b + 1)
                        pool.tensor_tensor(rstd[:], veps[:], mhalf[:], ALU.pow).then_inc(s_rstd, 1)

            @block.vector
            def _(dve):
                dve.sem_inc(s_xfree, 2)
                dve.wait_ge(s_w, 32)
                dve.tensor_copy(w[:], w8[:].bitcast(I8)).then_inc(s_wb, 1)
                with dve.Fori(0, B // 2) as i:
                    for u in range(2):
                        b = i * 2 + u
                        c = Chain(dve, s_dve)
                        xb, ob = x[:, u], o[:, u]
                        dve.wait_ge(s_x[u], (i + 1) * 16)
                        norm_stats(dve, c, xb, stats, mv, 1e-5, veps[:]).then_inc(s_var, 1)
                        dve.wait_ge(s_rstd, b + 1)
                        norm_apply(dve, c, y, xb, mv, rstd)
                        c.wait()
                        c.link(dve.tensor_scalar(y[:], y[:], 50.0, None, ALU.mult))
                        c.link(dve.tensor_scalar(y[:], y[:], ROUND, None, ALU.add))
                        c.link(dve.tensor_scalar(y[:], y[:], ROUND, -128.0, ALU.subtract, ALU.max))
                        dve.tensor_scalar(q[:], y[:], 127.0, None, ALU.min).then_inc(s_q, 1)
                        for k in range(KC):
                            dve.wait_ge(s_T, b * KC + k + 1)
                            dve.tensor_copy(qT[:, k, :], psT[0:KP, k, 0:S]).then_inc(s_qT, 1)
                        dve.wait_ge(s_y, b + 1)
                        dve.wait_ge(s_out[u], i * 16)
                        c.link(dve.tensor_scalar(ob, psO[:, :, 0:D], 0.02 * 0.01, None, ALU.mult))
                        c.link(dve.tensor_tensor(ob, ob, bcast(bias[:].unsqueeze(1), [P, TB, D]), ALU.add))
                        dve.tensor_tensor(ob, ob, xb, ALU.add).then_inc(s_o, 1)
                        dve.wait_ge(s_o, b + 1)
                        dve.sem_inc(s_xfree, 1)
                        c.close()

            @block.tensor
            def _(pe):
                pe.wait_ge(s_ident, 1)
                pe.wait_ge(s_wb, 1)
                with pe.Fori(0, B // 2) as i:
                    for u in range(2):
                        b = i * 2 + u
                        pe.wait_ge(s_q, b + 1)
                        for k in range(KC):
                            for t in range(TB):
                                m = pe.transpose(psT[0:KP, k, t * P:(t + 1) * P],
                                                 q[:, t, k * KP:(k + 1) * KP], ident[:])
                            m.then_inc(s_T, 1)
                        pe.wait_ge(s_qT, (b + 1) * KC)
                        for t in range(TB):
                            for k in range(KC):
                                m = pe.matmul(psO[:, t, 0:D], qT[:, k, t * P:(t + 1) * P], w[:, k, :],
                                              start=(k == 0), stop=(k == KC - 1))
                        m.then_inc(s_y, 1)

            @block.scalar
            def _(act):
                with act.Fori(0, B // 2) as i:
                    for u in range(2):
                        b = i * 2 + u
                        act.wait_ge(s_o, b + 1)
                        act.dma_start(ho[b], o[:, u]).then_inc(s_out[u], 16)
                for u in range(2):
                    act.wait_ge(s_out[u], B // 2 * 16)


SPLITS = 24


def select_dve(dve, c, w, K, nK, sems, base):
    ax, smax, lo, mid, cnt, tmp, junk = w["ax"], w["smax"], w["lo"], w["mid"], w["cnt"], w["tmp"], w["junk"]
    s_mid, s_cnt = sems
    c.mark(dve.memset(lo[:], 0.0))
    c.link(dve.tensor_reduce(smax[:], ax[:], AX.X, ALU.max))
    for i in range(1, SPLITS + 1):
        m = c.mark(dve.scalar_tensor_tensor(mid[:], smax[:], 2.0 ** -i, lo[:], ALU.mult, ALU.add))
        c.wait(m)
        dve.sem_inc(s_mid, 1)
        for t in range(2):
            c.mark(dve.tensor_scalar(junk[:, t], ax[:, t, :], mid[:, t:t + 1], None, ALU.is_ge, ALU.add,
                                     accum_out=cnt[:, t:t + 1]))
        c.wait()
        c.mark(dve.scalar_tensor_tensor(tmp[:, 0:2], cnt[:, 0:2], K, smax[:, 0:2], ALU.is_ge, ALU.mult))
        dve.wait_ge(s_cnt, (base + i) * 2)
        c.link(dve.scalar_tensor_tensor(tmp[:, 2:4], cnt[:, 2:4], nK, smax[:, 2:4], ALU.is_le, ALU.mult))
        c.link(dve.scalar_tensor_tensor(lo[:], tmp[:], 2.0 ** -i, lo[:], ALU.mult, ALU.add))


def select_act(act, w, sems, base):
    s_mid, s_cnt = sems
    for i in range(1, SPLITS + 1):
        act.wait_ge(s_mid, base + i)
        for t in (2, 3):
            act.activation(w["junk"][:, t], w["ax"][:, t, :], ACT.Sign, bias=w["mid"][:, t:t + 1], scale=-1.0,
                           accum_out=w["cnt"][:, t:t + 1]).then_inc(s_cnt, 1)


def kept_count(dve, c, w, n):
    sp, r, g, K, nK = (w[k][:] for k in ("sp", "kr", "kg", "K", "nK"))
    c.link(dve.tensor_scalar(sp, sp, float(n - 1), None, ALU.mult))
    c.link(dve.tensor_scalar(r, sp, ROUND, None, ALU.add))
    c.link(dve.tensor_scalar(r, r, ROUND, None, ALU.subtract))
    c.link(dve.tensor_tensor(g, sp, r, ALU.is_gt))
    c.link(dve.tensor_tensor(r, r, g, ALU.add))
    c.mark(dve.tensor_scalar(K, r, -1.0, float(n), ALU.mult, ALU.add))
    c.link(dve.tensor_scalar(nK, r, 2.0, -float(n), ALU.mult, ALU.add))


def select_buffers(st, width):
    w = {"ax": st.sb("ax", [P, TB, width]), "junk": st.sb("junk", [P, TB, width], BF16)}
    for k in ("smax", "lo", "mid", "cnt", "tmp"):
        w[k] = st.sb(k, [P, TB])
    for k in ("sp", "kr", "kg", "K", "nK"):
        w[k] = st.sb(k, [P, 1])
    return w


def attention_inputs_stage(nc, A, name, h_in, xT_d, affine=None, sparsity=None):
    with ExitStack() as ctx:
        st = Stage(nc, ctx, name)
        x = st.sb("x", [P, 2, TB, D])
        y = st.sb("y", [P, TB, D])
        xT = st.sb("xT", [KP, KC, S])
        gb = st.sb("gb", [P, 2, D])
        ident = st.sb("ident", [P, P])
        stats, mv = st.sb("stats", [P, TB, 6]), st.sb("mv", [P, TB, 2])
        veps, rstd, mhalf = st.sb("veps", [P, TB]), st.sb("rstd", [P, TB]), st.sb("mhalf", [P, TB])
        w = select_buffers(st, D) if sparsity is not None else None
        ps_t = st.ps("ps_t", [P, KC, S])
        s_x = [st.sem(f"x{u}") for u in range(2)]
        s_c, s_xfree, s_var, s_rstd, s_y, s_t, s_xT, s_out, s_mid, s_cnt, s_ident, s_dve, s_pool = (
            st.sem(n) for n in ("c", "xfree", "var", "rstd", "y", "t", "xT", "out", "mid", "cnt", "ident",
                                "dve", "pool"))
        hi = batch_tiles(h_in)
        norms = 2 if affine else 1
        with nc.Block() as block:

            @block.sync
            def _(sp):
                if affine:
                    for k in range(2):
                        sp.dma_start(gb[:, k, :], affine[k].partition_broadcast(P)).then_inc(s_c, 16)
                    sp.dma_start(w["sp"][:], sparsity.partition_broadcast(P)).then_inc(s_c, 16)
                with sp.Fori(0, B // 2) as i:
                    for u in range(2):
                        sp.wait_ge(s_xfree, i * 2 + u + 1)
                        sp.dma_start(x[:, u], hi[i * 2 + u]).then_inc(s_x[u], 16)

            @block.gpsimd
            def _(pool):
                c = Chain(pool, s_pool)
                make_identity(pool, c, ident[:]).then_inc(s_ident, 1)
                c.link(pool.memset(mhalf[:], -0.5))
                with pool.Fori(0, B * norms) as i:
                    pool.wait_ge(s_var, i + 1)
                    pool.tensor_tensor(rstd[:], veps[:], mhalf[:], ALU.pow).then_inc(s_rstd, 1)

            @block.vector
            def _(dve):
                dve.sem_inc(s_xfree, 2)
                if affine:
                    dve.wait_ge(s_c, 48)
                    c = Chain(dve, s_dve)
                    kept_count(dve, c, w, D)
                    c.close()
                with dve.Fori(0, B // 2) as i:
                    for u in range(2):
                        b = i * 2 + u
                        c = Chain(dve, s_dve)
                        dve.wait_ge(s_x[u], (i + 1) * 16)
                        norm_stats(dve, c, x[:, u], stats, mv, 1e-5, veps[:]).then_inc(s_var, 1)
                        dve.wait_ge(s_rstd, b * norms + 1)
                        dve.wait_ge(s_t, b)
                        norm_apply(dve, c, y, x[:, u], mv, rstd)
                        c.wait()
                        dve.sem_inc(s_xfree, 1)
                        if affine:
                            norm_stats(dve, c, y, stats, mv, 1e-5, veps[:]).then_inc(s_var, 1)
                            dve.wait_ge(s_rstd, b * norms + 2)
                            norm_apply(dve, c, y, y, mv, rstd)
                            c.wait()
                            c.link(dve.tensor_tensor(y[:], y[:], bcast(gb[:, 0:1, :], [P, TB, D]), ALU.mult))
                            c.link(dve.tensor_tensor(y[:], y[:], bcast(gb[:, 1:2, :], [P, TB, D]), ALU.add))
                            c.link(dve.scalar_tensor_tensor(w["ax"][:], y[:], -1.0, y[:], ALU.mult, ALU.max))
                            select_dve(dve, c, w, w["K"][:], w["nK"][:], (s_mid, s_cnt), b * SPLITS)
                            for t in range(TB):
                                c.mark(dve.scalar_tensor_tensor(y[:, t, :], w["ax"][:, t, :], w["lo"][:, t:t + 1],
                                                                y[:, t, :], ALU.is_ge, ALU.mult))
                            c.wait()
                        dve.sem_inc(s_y, 1)
                        dve.wait_ge(s_t, b + 1)
                        dve.wait_ge(s_out, b * 16)
                        dve.tensor_copy(xT[:], ps_t[0:KP, :, :]).then_inc(s_xT, 1)
                        c.close()

            @block.tensor
            def _(pe):
                pe.wait_ge(s_ident, 1)
                with pe.Fori(0, B) as b:
                    pe.wait_ge(s_y, b + 1)
                    pe.wait_ge(s_xT, b)
                    for k in range(KC):
                        for t in range(TB):
                            m = pe.transpose(ps_t[0:KP, k, t * P:(t + 1) * P], y[:, t, k * KP:(k + 1) * KP], ident[:])
                    m.then_inc(s_t, 1)

            @block.scalar
            def _(act):
                with act.Fori(0, B) as b:
                    if affine:
                        select_act(act, w, (s_mid, s_cnt), b * SPLITS)
                    act.wait_ge(s_xT, b + 1)
                    act.dma_start(xT_d[b], xT[:]).then_inc(s_out, 16)
                act.wait_ge(s_out, B * 16)


def ternary_stage(nc, A, name, pairs):
    with ExitStack() as ctx:
        st = Stage(nc, ctx, name)
        s_w, s_p, s_sum, s_out, s_dve, s_ones = (st.sem(n) for n in ("w", "p", "sum", "out", "dve", "ones"))
        work = []
        for k, (src, dst) in enumerate(pairs):
            p, n = src.shape
            work.append((st.sb(f"w{k}", [p, n]), st.sb(f"part{k}", [p, 1]), st.sb(f"s{k}", [p, 2]),
                         st.ps(f"sum{k}", [p, 1]), p, n))
        ones = st.sb("ones", [P, P])
        with nc.Block() as block:

            @block.sync
            def _(sp):
                for k, (src, dst) in enumerate(pairs):
                    sp.dma_start(work[k][0][:], src).then_inc(s_w, 16)
                    sp.wait_ge(s_w, 16 * (k + 1))

            @block.vector
            def _(dve):
                c = Chain(dve, s_dve)
                dve.memset(ones[:], 1.0).then_inc(s_ones, 1)
                for k, (w, part, sc, total, p, n) in enumerate(work):
                    dve.wait_ge(s_w, 16 * (k + 1))
                    dve.tensor_reduce(part[:], w[:], AX.X, ALU.add, apply_absolute_value=True).then_inc(s_p, 1)
                    dve.wait_ge(s_sum, k + 1)
                    c.link(dve.tensor_scalar(sc[:, 0:1], total[:], 1.0 / (p * n), None, ALU.mult))
                    c.link(dve.tensor_scalar(sc[:, 1:2], sc[:, 0:1], 1e-8, None, ALU.add))
                    c.link(dve.reciprocal(sc[:, 1:2], sc[:, 1:2]))
                    c.link(dve.tensor_scalar(w[:], w[:], sc[:, 1:2], None, ALU.mult))
                    c.link(dve.tensor_scalar(w[:], w[:], ROUND, None, ALU.add))
                    c.link(dve.tensor_scalar(w[:], w[:], ROUND, -1.0, ALU.subtract, ALU.max))
                    c.link(dve.tensor_scalar(w[:], w[:], 1.0, sc[:, 0:1], ALU.min, ALU.mult))

            @block.tensor
            def _(pe):
                pe.wait_ge(s_ones, 1)
                for k, (w, part, sc, total, p, n) in enumerate(work):
                    pe.wait_ge(s_p, k + 1)
                    pe.matmul(total[:], ones[0:p, 0:p], part[:], start=True, stop=True).then_inc(s_sum, 1)

            @block.scalar
            def _(act):
                for k, (src, dst) in enumerate(pairs):
                    act.wait_ge(s_dve, 7 * (k + 1))
                    act.dma_start(dst, work[k][0][:]).then_inc(s_out, 16)
                act.wait_ge(s_out, 16 * len(pairs))


def attention_stage(nc, A, name, xT_d, w_d, att_d, qkv_bias=None):
    H, DH = 12, 64
    NPAIR, INNER = H // 2, H * DH
    G = 2 * TB
    with ExitStack() as ctx:
        st = Stage(nc, ctx, name)
        W = st.sb("W", [KP, KC, 3 * INNER])
        xT = st.sb("xT", [KP, KC, S])
        qk = st.sb("qk", [P, 2, 2, S])
        v = st.sb("v", [P, 2, TB, P])
        prob = st.sb("prob", [P, 2, S])
        probT = st.sb("probT", [P, 2, S])
        o = st.sb("o", [P, 2, TB, 2, DH])
        nmax = st.sb("nmax", [P, 2])
        rsum = st.sb("rsum", [P, 2, TB, 2])
        rinv = st.sb("rinv", [P, TB, 2])
        ident = st.sb("ident", [P, P])
        bqk = st.sb("bqk", [P, 2, NPAIR])
        bv = st.sb("bv", [P, INNER])
        ps_qv, ps_k = st.ps("ps_qv", [P, S]), st.ps("ps_k", [P, S])
        ps_s, ps_t = st.ps("ps_s", [P, 2, S]), st.ps("ps_t", [P, 2, S])
        ps_o = st.ps("ps_o", [P, 2, TB, 2, DH])
        s_w, s_bias, s_bq, s_ident, s_x, s_pool = (st.sem(n) for n in ("w", "bias", "bq", "ident", "x", "pool"))
        s_qk, s_qkc, s_v, s_vc = (st.sem(n) for n in ("qk", "qkc", "v", "vc"))
        s_s, s_max, s_exp, s_t, s_tc, s_pv, s_o, s_dve = (
            st.sem(n) for n in ("s", "max", "exp", "t", "tc", "pv", "o", "dve"))
        s_out = [st.sem(f"out{u}") for u in range(2)]
        att = att_d.rearrange("(b t p) (n f) -> b n p t f", t=TB, p=P, n=NPAIR)
        with nc.Block() as block:

            @block.sync
            def _(sp):
                sp.dma_start(W[:], w_d).then_inc(s_w, 16)
                if qkv_bias is not None:
                    sp.dma_start(bqk[:], qkv_bias[0:2 * INNER].rearrange("(a n p) -> p a n", a=2, p=P),
                                 allow_slow_non_contiguous=True).then_inc(s_bias, 16)
                    sp.dma_start(bv[:], qkv_bias[2 * INNER:].partition_broadcast(P)).then_inc(s_bias, 16)
                sp.dma_start(xT[:], xT_d[0]).then_inc(s_x, 16)
                with sp.Fori(0, B) as b:
                    for n in range(NPAIR):
                        if n == NPAIR - 1:
                            sp.wait_ge(s_v, (b + 1) * NPAIR)
                            sp.dma_start(xT[:], xT_d[(b + 1) % B]).then_inc(s_x, 16)
                        sp.wait_ge(s_o, b * NPAIR + n + 1)
                        sp.dma_start(att[b, n], o[:, n % 2].rearrange("p t h d -> p t (h d)")).then_inc(s_out[n % 2], 16)
                for u in range(2):
                    sp.wait_ge(s_out[u], B * NPAIR // 2 * 16)
                sp.wait_ge(s_x, (B + 1) * 16)

            @block.gpsimd
            def _(pool):
                c = Chain(pool, s_pool)
                make_identity(pool, c, ident[:]).then_inc(s_ident, 1)

            @block.tensor
            def _(pe):

                def project_qk(j, n):
                    if n == 0:
                        pe.wait_ge(s_x, (j // NPAIR + 1) * 16 if isinstance(j, int) else first_x[0])
                    pe.wait_ge(s_vc, j)
                    for a, bank in ((0, ps_qv), (1, ps_k)):
                        for k in range(KC):
                            m = pe.matmul(bank[:], W[:, k, a * INNER + n * P:a * INNER + (n + 1) * P], xT[:, k, :],
                                          start=(k == 0), stop=(k == KC - 1))
                    m.then_inc(s_qk, 1)

                def project_v(j, n):
                    pe.wait_ge(s_qkc, j + 1)
                    for t in range(TB):
                        for k in range(KC):
                            m = pe.matmul(ps_qv[:, t * P:(t + 1) * P], xT[:, k, t * P:(t + 1) * P],
                                          W[:, k, 2 * INNER + n * P:2 * INNER + (n + 1) * P],
                                          start=(k == 0), stop=(k == KC - 1))
                    m.then_inc(s_v, 1)

                def score(n, g):
                    rows, q = slice(g // TB * DH, (g // TB + 1) * DH), g % TB
                    pe.matmul(ps_s[:, g % 2], qk[rows, n % 2, 0, q * P:(q + 1) * P], qk[rows, n % 2, 1, :],
                              start=True, stop=True).then_inc(s_s, 1)

                first_x = [None]
                pe.wait_ge(s_w, 16)
                pe.wait_ge(s_ident, 1)
                project_qk(0, 0)
                project_v(0, 0)
                score(0, 0)
                score(0, 1)
                with pe.Fori(0, B) as b:
                    first_x[0] = (b + 2) * 16
                    for n in range(NPAIR):
                        j = b * NPAIR + n
                        for g in range(G):
                            step = j * G + g
                            pe.wait_ge(s_exp, step + 1)
                            for k in range(TB):
                                m = pe.transpose(ps_t[:, g % 2, k * P:(k + 1) * P],
                                                 prob[:, g % 2, k * P:(k + 1) * P], ident[:])
                            m.then_inc(s_t, 1)
                            if g == 1:
                                project_qk(j + 1, (n + 1) % NPAIR)
                            if g == 2:
                                project_v(j + 1, (n + 1) % NPAIR)
                            score((n if g + 2 < G else n + 1) % NPAIR, (g + 2) % G)
                            pe.wait_ge(s_tc, step + 1)
                            if g == 0:
                                pe.wait_ge(s_vc, j + 1)
                            for k in range(TB):
                                m = pe.matmul(ps_o[:, n % 2, g % TB, g // TB, :], probT[:, g % 2, k * P:(k + 1) * P],
                                              v[:, n % 2, k, g // TB * DH:(g // TB + 1) * DH],
                                              start=(k == 0), stop=(k == TB - 1))
                            m.then_inc(s_pv, 1)

            @block.scalar
            def _(act):

                def copy_qk(j, u):
                    act.wait_ge(s_qk, j + 1)
                    if qkv_bias is None:
                        act.activation(qk[:, u, 0, :], ps_qv[:], ACT.Copy, scale=DH ** -0.5)
                        act.activation(qk[:, u, 1, :], ps_k[:], ACT.Copy).then_inc(s_qkc, 1)
                    else:
                        n = j % NPAIR
                        act.activation(qk[:, u, 0, :], ps_qv[:], ACT.Identity, scale=DH ** -0.5,
                                       bias=bqk[:, 0, bass.ds(n, 1)])
                        act.activation(qk[:, u, 1, :], ps_k[:], ACT.Identity,
                                       bias=bqk[:, 1, bass.ds(n, 1)]).then_inc(s_qkc, 1)

                def exponentials(step, u, g):
                    act.wait_ge(s_max, step + 1)
                    act.activation(prob[:, g % 2], ps_s[:, g % 2], ACT.Exp, bias=nmax[:, g % 2:g % 2 + 1],
                                   accum_out=rsum[:, u, g % TB, g // TB:g // TB + 1]).then_inc(s_exp, 1)

                if qkv_bias is not None:
                    act.wait_ge(s_bq, 1)
                copy_qk(0, 0)
                exponentials(0, 0, 0)
                with act.Fori(0, B * NPAIR // 2) as i:
                    for u in range(2):
                        j = i * 2 + u
                        for g in range(G):
                            step = j * G + g
                            if g == G - 1:
                                act.wait_ge(s_o, j)
                            act.wait_ge(s_t, step)
                            exponentials(step + 1, (u if g + 1 < G else 1 - u), (g + 1) % G)
                            if g == 1:
                                copy_qk(j + 1, 1 - u)

            @block.vector
            def _(dve):

                def maximum(step, g):
                    dve.wait_ge(s_s, step + 1)
                    dve.tensor_reduce(nmax[:, g % 2:g % 2 + 1], ps_s[:, g % 2], AX.X, ALU.max,
                                      negate=True).then_inc(s_max, 1)

                def copy_v(j, u):
                    dve.wait_ge(s_v, j + 1)
                    vb = v[:, u].rearrange("p t f -> p (t f)")
                    if qkv_bias is None:
                        dve.tensor_copy(vb, ps_qv[:]).then_inc(s_vc, 1)
                    else:
                        n = j % NPAIR
                        dve.tensor_tensor(v[:, u], ps_qv[:].rearrange("p (t f) -> p t f", t=TB),
                                          bcast(bv[:, bass.ds(n * P, P)].unsqueeze(1), [P, TB, P]),
                                          ALU.add).then_inc(s_vc, 1)

                def normalise(j, u, stored):
                    c = Chain(dve, s_dve)
                    dve.wait_ge(s_pv, (j + 1) * G)
                    c.link(dve.reciprocal(rinv[:], rsum[:, u]))
                    dve.wait_ge(s_out[u], stored * 16)
                    dve.tensor_tensor(o[:, u], ps_o[:, u], bcast(rinv[:].unsqueeze(3), [P, TB, 2, DH]),
                                      ALU.mult).then_inc(s_o, 1)
                    c.close()

                if qkv_bias is not None:
                    dve.wait_ge(s_bias, 32)
                    dve.tensor_scalar(bqk[:, 0, :], bqk[:, 0, :], DH ** -0.5, None, ALU.mult).then_inc(s_bq, 1)
                maximum(0, 0)
                copy_v(0, 0)
                with dve.Fori(0, B * NPAIR // 2) as i:
                    for u in range(2):
                        j = i * 2 + u
                        for g in range(G):
                            step = j * G + g
                            dve.wait_ge(s_exp, step)
                            maximum(step + 1, (g + 1) % G)
                            dve.wait_ge(s_t, step + 1)
                            dve.tensor_copy(probT[:, g % 2], ps_t[:, g % 2]).then_inc(s_tc, 1)
                            if g == 3:
                                copy_v(j + 1, 1 - u)
                        normalise(j, u, i)


def attention_output_stage(nc, A, name, att_d, w_d, bias, h_in, h_out, sparsity=None):
    INNER = att_d.shape[1]
    C = INNER // P
    with ExitStack() as ctx:
        st = Stage(nc, ctx, name)
        a = st.sb("a", [P, 2, TB, INNER])
        hx = st.sb("hx", [P, 2, TB, D])
        W = st.sb("W", [P, C, D])
        bo = st.sb("bo", [P, D])
        aT = st.sb("aT", [P, 2, C * P])
        o = st.sb("o", [P, 2, TB, D])
        ident = st.sb("ident", [P, P])
        w = select_buffers(st, INNER) if sparsity is not None else None
        ps_t = st.ps("ps_t", [P, 2, 2, S])
        ps_o = st.ps("ps_o", [P, TB, S])
        s_a = [st.sem(f"a{u}") for u in range(2)]
        s_out = [st.sem(f"out{u}") for u in range(2)]
        s_w, s_afree, s_m, s_t, s_tc, s_y, s_o, s_mid, s_cnt, s_ident, s_dve, s_pool = (
            st.sem(n) for n in ("w", "afree", "m", "t", "tc", "y", "o", "mid", "cnt", "ident", "dve", "pool"))
        ai = att_d.rearrange("(b t p) f -> b p t f", t=TB, p=P)
        hi, ho = batch_tiles(h_in), batch_tiles(h_out)
        HC = C * P // 2
        with nc.Block() as block:

            @block.sync
            def _(sp):
                sp.dma_start(W[:], w_d).then_inc(s_w, 16)
                sp.dma_start(bo[:], bias.partition_broadcast(P)).then_inc(s_w, 16)
                if sparsity is not None:
                    sp.dma_start(w["sp"][:], sparsity.partition_broadcast(P)).then_inc(s_w, 16)
                with sp.Fori(0, B // 2) as i:
                    for u in range(2):
                        b = i * 2 + u
                        sp.wait_ge(s_afree, b + 1)
                        sp.dma_start(a[:, u], ai[b]).then_inc(s_a[u], 16)
                        sp.dma_start(hx[:, u], hi[b]).then_inc(s_a[u], 16)

            @block.gpsimd
            def _(pool):
                c = Chain(pool, s_pool)
                make_identity(pool, c, ident[:]).then_inc(s_ident, 1)

            @block.vector
            def _(dve):
                dve.sem_inc(s_afree, 2)
                dve.wait_ge(s_w, 48 if sparsity is not None else 32)
                if sparsity is not None:
                    c = Chain(dve, s_dve)
                    kept_count(dve, c, w, INNER)
                    c.close()
                with dve.Fori(0, B // 2) as i:
                    for u in range(2):
                        b = i * 2 + u
                        c = Chain(dve, s_dve)
                        dve.wait_ge(s_a[u], (i + 1) * 32)
                        if sparsity is not None:
                            c.link(dve.scalar_tensor_tensor(w["ax"][:], a[:, u], -1.0, a[:, u], ALU.mult, ALU.max))
                            select_dve(dve, c, w, w["K"][:], w["nK"][:], (s_mid, s_cnt), b * SPLITS)
                            for t in range(TB):
                                c.mark(dve.scalar_tensor_tensor(a[:, u, t, :], w["ax"][:, t, :], w["lo"][:, t:t + 1],
                                                                a[:, u, t, :], ALU.is_ge, ALU.mult))
                            c.wait()
                        dve.sem_inc(s_m, 1)
                        for t in range(TB):
                            dve.wait_ge(s_t, b * TB + t + 1)
                            dve.tensor_copy(aT[:, t % 2].rearrange("p (a f) -> p a f", a=2),
                                            ps_t[:, t % 2, :, 0:HC]).then_inc(s_tc, 1)
                        c.mark(dve.tensor_tensor(hx[:, u], hx[:, u], bcast(bo[:].unsqueeze(1), [P, TB, D]), ALU.add))
                        c.wait()
                        dve.wait_ge(s_y, b + 1)
                        dve.wait_ge(s_out[u], i * 16)
                        dve.tensor_tensor(o[:, u], ps_o[:, :, 0:D], hx[:, u], ALU.add).then_inc(s_o, 1)
                        dve.wait_ge(s_o, b + 1)
                        dve.sem_inc(s_afree, 1)
                        c.close()

            @block.tensor
            def _(pe):
                pe.wait_ge(s_ident, 1)
                pe.wait_ge(s_w, 48 if sparsity is not None else 32)
                with pe.Fori(0, B // 2) as i:
                    for u in range(2):
                        b = i * 2 + u
                        pe.wait_ge(s_m, b + 1)

                        def turn(t):
                            for k in range(C):
                                m = pe.transpose(ps_t[:, t % 2, k * P // HC, k * P % HC:k * P % HC + P],
                                                 a[:, u, t, k * P:(k + 1) * P], ident[:])
                            m.then_inc(s_t, 1)

                        turn(0)
                        for t in range(TB):
                            if t + 1 < TB:
                                turn(t + 1)
                            pe.wait_ge(s_tc, b * TB + t + 1)
                            if t == 0:
                                pe.wait_ge(s_o, b)
                            for k in range(C):
                                m = pe.matmul(ps_o[:, t, 0:D], aT[:, t % 2, k * P:(k + 1) * P], W[:, k, :],
                                              start=(k == 0), stop=(k == C - 1))
                        m.then_inc(s_y, 1)

            @block.scalar
            def _(act):
                with act.Fori(0, B // 2) as i:
                    for u in range(2):
                        b = i * 2 + u
                        if sparsity is not None:
                            select_act(act, w, (s_mid, s_cnt), b * SPLITS)
                        act.wait_ge(s_o, b + 1)
                        act.dma_start(ho[b], o[:, u]).then_inc(s_out[u], 16)
                for u in range(2):
                    act.wait_ge(s_out[u], B // 2 * 16)


def embedding_stage(nc, A, h_in, h_out):
    V_WORD, V_MODAL, V_SEG, V_NPI, V_POS = 8000, 16, 4, 2500, 512
    WORD, NPI, POS, SEG, MODAL = range(5)
    IDS = [("x", V_WORD), ("itok_BS_0_9999", V_NPI), ("itok_BS_0_2047", V_POS), ("itok_BS_0_3", V_SEG),
           ("itok_BS_0_15", V_MODAL)]
    TWO_PI_HI = 6.28125
    TWO_PI_LO = 2 * np.pi - TWO_PI_HI
    PI = float(np.float32(np.pi)) * (1 - 2.0 ** -23)
    combined = nc.dram_tensor("d_seg_modal", (V_SEG * V_MODAL, D), F32).ap()
    tables = [A["L0_tok_word_table"], A["L0_tok_npi_table"], A["L0_tok_posi_table"], combined]
    NG = NT // TB
    with ExitStack() as ctx:
        st = Stage(nc, ctx, "emb")
        ids = st.sb("ids", [P, 5, NT], I32)
        idf = st.sb("idf", [P, 5, NT])
        neg = st.sb("neg", [P, 5, NT])
        rows = st.sb("rows", [P, 4, NT], I32)
        row = st.sb("row", [P, 2, 4, TB], I32)
        tau = st.sb("tau", [P, 2, NT])
        tg = st.sb("tg", [P, 2, TB])
        wb = st.sb("wb", [P, 2, 2, D])
        seg = st.sb("seg", [V_SEG * V_MODAL, D])
        modal = st.sb("modal", [V_SEG * V_MODAL, D])
        g = st.sb("g", [P, 2, 4, TB, D])
        arg = st.sb("arg", [P, TB, 2, D])
        turns = st.sb("turns", [P, TB, 2, D])
        wave = st.sb("wave", [P, TB, 2, D])
        e = st.sb("e", [P, TB, D])
        o = st.sb("o", [P, 2, TB, D])
        gb = st.sb("gb", [P, 2, D])
        stats, mv = st.sb("stats", [P, TB, 6]), st.sb("mv", [P, TB, 2])
        veps, rstd, mhalf = st.sb("veps", [P, TB]), st.sb("rstd", [P, TB]), st.sb("mhalf", [P, TB])
        s_g = [st.sem(f"g{u}") for u in range(2)]
        s_out = [st.sem(f"out{u}") for u in range(2)]
        s_c, s_cmb, s_cst, s_rows, s_gfree, s_arg, s_turns, s_red, s_wave, s_var, s_rstd, s_o, s_dve, s_pool, s_act = (
            st.sem(n) for n in ("c", "cmb", "cst", "rows", "gfree", "arg", "turns", "red", "wave", "var", "rstd", "o",
                                "dve", "pool", "act"))
        ho = h_out.rearrange("(p g t) d -> g p t d", p=P, t=TB)
        with nc.Block() as block:

            @block.sync
            def _(sp):
                for k, (name, _) in enumerate(IDS):
                    sp.dma_start(ids[:, k, :], A[name].rearrange("b (q t) -> (b q) t", t=NT)).then_inc(s_c, 16)
                for k, (tau_name, part) in enumerate((("fside_BS_age_tau", "age"), ("fside_BS_delays_tau", "delay"))):
                    sp.dma_start(tau[:, k, :], A[tau_name].rearrange("b (q t) -> (b q) t", t=NT)).then_inc(s_c, 16)
                    for a, name in enumerate(("w", "b")):
                        v = A[f"L0_tok_{part}_{name}"]
                        v0 = A[f"L0_tok_{part}_{name}0"]
                        v = v[0] if a == 0 else v
                        v0 = v0[0] if a == 0 else v0
                        sp.dma_start(wb[:, k, a, 0:D - 1], v.partition_broadcast(P)).then_inc(s_c, 16)
                        sp.dma_start(wb[:, k, a, D - 1:D], v0.partition_broadcast(P)).then_inc(s_c, 16)
                sp.dma_start(gb[:, 0, :], A["L0_tok_ln_gamma"].partition_broadcast(P)).then_inc(s_c, 16)
                sp.dma_start(gb[:, 1, :], A["L0_tok_ln_beta"].partition_broadcast(P)).then_inc(s_c, 16)
                for k in range(V_SEG):
                    sp.dma_start(seg[k * V_MODAL:(k + 1) * V_MODAL, :],
                                 A["L0_tok_seg_table"][k].partition_broadcast(V_MODAL)).then_inc(s_c, 16)
                    sp.dma_start(modal[k * V_MODAL:(k + 1) * V_MODAL, :],
                                 A["L0_tok_modalities_table"]).then_inc(s_c, 16)
                sp.wait_ge(s_cmb, 1)
                sp.dma_start(combined, seg[:]).then_inc(s_cst, 16)

            @block.gpsimd
            def _(pool):
                c = Chain(pool, s_pool)
                c.link(pool.memset(mhalf[:], -0.5))
                c.close()
                pool.wait_ge(s_rows, 1)
                pool.wait_ge(s_cst, 16)

                def gather(i, u):
                    c = Chain(pool, s_pool)
                    pool.wait_ge(s_gfree, i * 2 + u + 1)
                    c.link(pool.tensor_copy(row[:, u], rows[:, :, bass.ds((i * 2 + u) * TB, TB)]))
                    for k in range(4):
                        for t in range(TB):
                            pool.indirect_dma_start(
                                out=g[:, u, k, t, :], out_offset=None, in_=tables[k],
                                in_offset=bass.IndirectOffsetOnAxis(ap=row[:, u, k, t:t + 1], axis=0)).then_inc(s_g[u], 16)
                    c.close()

                gather(0, 0)
                with pool.Fori(0, NG // 2) as i:
                    for u in range(2):
                        if u == 0:
                            gather(i, 1)
                        else:
                            c = Chain(pool, s_pool)
                            pool.wait_ge(s_gfree, i * 2 + 3)
                            c.link(pool.tensor_copy(row[:, 0], rows[:, :, bass.ds((i * 2 + 2) % NG * TB, TB)]))
                            for k in range(4):
                                for t in range(TB):
                                    pool.indirect_dma_start(
                                        out=g[:, 0, k, t, :], out_offset=None, in_=tables[k],
                                        in_offset=bass.IndirectOffsetOnAxis(ap=row[:, 0, k, t:t + 1],
                                                                            axis=0)).then_inc(s_g[0], 16)
                            c.close()
                        pool.wait_ge(s_var, i * 2 + u + 1)
                        pool.tensor_tensor(rstd[:], veps[:], mhalf[:], ALU.pow).then_inc(s_rstd, 1)
                pool.wait_ge(s_g[0], (NG // 2 + 1) * 4 * TB * 16)

            @block.scalar
            def _(act):
                with act.Fori(0, NG // 2) as i:
                    for u in range(2):
                        n = i * 2 + u
                        c = Chain(act, s_act)
                        act.wait_ge(s_arg, n + 1)
                        c.link(act.activation(turns[:], arg[:], ACT.Copy, scale=float(1 / (2 * np.pi)), bias=ROUND))
                        act.activation(turns[:], turns[:], ACT.Copy, bias=-ROUND).then_inc(s_turns, 1)
                        act.wait_ge(s_red, n + 1)
                        act.activation(wave[:, :, :, 0:D - 1], turns[:, :, :, 0:D - 1], ACT.Sin).then_inc(s_wave, 1)
                        act.activation(wave[:, :, :, D - 1:D], arg[:, :, :, D - 1:D], ACT.Copy).then_inc(s_wave, 1)
                        c.close()
                        act.wait_ge(s_o, n + 1)
                        act.dma_start(ho[n], o[:, u]).then_inc(s_out[u], 16)
                for u in range(2):
                    act.wait_ge(s_out[u], NG // 2 * 16)

            @block.vector
            def _(dve):
                c = Chain(dve, s_dve)
                dve.wait_ge(s_c, 16 * 25)
                c.link(dve.tensor_copy(idf[:], ids[:]))
                for k, (_, size) in enumerate(IDS):
                    c.mark(dve.tensor_scalar(neg[:, k], idf[:, k], 0.0, float(size), ALU.is_lt, ALU.mult))
                c.wait()
                c.link(dve.tensor_tensor(idf[:], idf[:], neg[:], ALU.add))
                for k, (_, size) in enumerate(IDS):
                    c.mark(dve.tensor_scalar(idf[:, k], idf[:, k], 0.0, float(size - 1), ALU.max, ALU.min))
                c.wait()
                c.link(dve.scalar_tensor_tensor(idf[:, SEG], idf[:, SEG], float(V_MODAL), idf[:, MODAL], ALU.mult, ALU.add))
                c.link(dve.tensor_copy(rows[:], idf[:, 0:4]))
                dve.sem_inc(s_rows, 1)
                c.link(dve.tensor_tensor(seg[:], seg[:], modal[:], ALU.add))
                dve.sem_inc(s_cmb, 1)
                dve.sem_inc(s_gfree, 2)
                c.close()
                with dve.Fori(0, NG // 2) as i:
                    for u in range(2):
                        n = i * 2 + u
                        c = Chain(dve, s_dve)
                        c.link(dve.tensor_copy(tg[:], tau[:, :, bass.ds(n * TB, TB)]))
                        for k in range(2):
                            for t in range(TB):
                                c.mark(dve.scalar_tensor_tensor(arg[:, t, k, :], wb[:, k, 0, :], tg[:, k, t:t + 1],
                                                                wb[:, k, 1, :], ALU.mult, ALU.add))
                        c.wait()
                        dve.sem_inc(s_arg, 1)
                        ob, gu = o[:, u], g[:, u]
                        dve.wait_ge(s_g[u], (i + 1) * 4 * TB * 16)
                        dve.wait_ge(s_out[u], i * 16)
                        c.mark(dve.tensor_tensor(e[:], gu[:, WORD], gu[:, SEG], ALU.add))
                        c.link(dve.tensor_tensor(ob, gu[:, NPI], gu[:, POS], ALU.add))
                        dve.sem_inc(s_gfree, 1)
                        c.mark(dve.tensor_tensor(e[:], e[:], ob, ALU.add))
                        dve.wait_ge(s_turns, n + 1)
                        c.link(dve.scalar_tensor_tensor(wave[:], turns[:], -TWO_PI_HI, arg[:], ALU.mult, ALU.add))
                        c.link(dve.scalar_tensor_tensor(wave[:], turns[:], -TWO_PI_LO, wave[:], ALU.mult, ALU.add))
                        c.link(dve.tensor_scalar(turns[:], wave[:], PI, -PI, ALU.min, ALU.max))
                        dve.sem_inc(s_red, 1)
                        dve.wait_ge(s_wave, 2 * n + 2)
                        c.link(dve.tensor_tensor(e[:], e[:], wave[:, :, 0, :], ALU.add))
                        c.link(dve.tensor_tensor(e[:], e[:], wave[:, :, 1, :], ALU.add))
                        norm_stats(dve, c, e, stats, mv, 1e-12, veps[:]).then_inc(s_var, 1)
                        dve.wait_ge(s_rstd, n + 1)
                        norm_apply(dve, c, ob, e, mv, rstd)
                        c.wait()
                        c.link(dve.tensor_tensor(ob, ob, bcast(gb[:, 0:1, :], [P, TB, D]), ALU.mult))
                        c.link(dve.tensor_tensor(ob, ob, bcast(gb[:, 1:2, :], [P, TB, D]), ALU.add))
                        dve.sem_inc(s_o, 1)
                        c.close()


def stage_l1_attention(nc, A, h_in, h_out):
    H, DH, M = 12, 16, 64
    NP = H // 2
    HC = H // KC
    V1 = DH + 1
    with ExitStack() as ctx:
        st = Stage(nc, ctx, "l1a")
        x = st.sb("x", [P, 2, TB, D])
        y = st.sb("y", [P, TB, D])
        xT = st.sb("xT", [KP, KC, S])
        W = st.sb("W", [KP, KC, 3 * D])
        Wp = st.sb("Wp", [KP, KC, D])
        gb = st.sb("gb", [P, 3, D])
        feat = st.sb("feat", [KP, HC * M])
        half = st.sb("half", [KP, HC * M])
        kvmask = st.sb("kvmask", [P, 2 * V1])
        t1 = st.sb("t1", [KP, 2, KC, S])
        t2 = st.sb("t2", [KP, 2, KC, S])
        v1 = st.sb("v1", [P, TB, H, V1])
        kp = st.sb("kp", [P, TB, H * M])
        qp = st.sb("qp", [P, NP, S])
        kv = st.sb("kv", [P, NP, 2 * V1])
        den = st.sb("den", [P, TB, H])
        att = st.sb("att", [P, TB, H, DH])
        o = st.sb("o", [P, 2, TB, D])
        ident = st.sb("ident", [P, P])
        stats, mv = st.sb("stats", [P, TB, 6]), st.sb("mv", [P, TB, 2])
        veps, rstd, mhalf = st.sb("veps", [P, TB]), st.sb("rstd", [P, TB]), st.sb("mhalf", [P, TB])
        ps_t = st.ps("ps_t", [P, KC, S])
        ps_q = st.ps("ps_q", [P, KC, S])
        ps_e = st.ps("ps_e", [P, 2, S])
        ps_m = st.ps("ps_m", [P, 2, 256])
        ps_o = st.ps("ps_o", [P, 2, 256])
        s_x = [st.sem(f"x{u}") for u in range(2)]
        s_out = [st.sem(f"out{u}") for u in range(2)]
        names = ("c xfree var rstd y t tc q qc sq v vc e ec kv kvc num att proj o dve pool ident ones pr").split()
        (s_c, s_xfree, s_var, s_rstd, s_y, s_t, s_tc, s_q, s_qc, s_sq, s_v, s_vc, s_e, s_ec, s_kv, s_kvc, s_num,
         s_att, s_proj, s_o, s_dve, s_pool, s_ident, s_ones, s_pr) = (st.sem(n) for n in names)
        hi, ho = batch_tiles(h_in), batch_tiles(h_out)
        NE = 2 * TB + NP
        with nc.Block() as block:

            @block.sync
            def _(sp):
                loads = [(W[:], A["L1_attn_W_qkv"]), (Wp[:], A["L1_attn_W_proj"]),
                         (gb[:, 0, :], A["L1_attn_gamma"].partition_broadcast(P)),
                         (gb[:, 1, :], A["L1_attn_beta"].partition_broadcast(P)),
                         (gb[:, 2, :], A["L1_attn_b_proj"].partition_broadcast(P)),
                         (half[:], A["c_half"]), (kvmask[:], A["c_kvmask"])]
                for to, src in loads:
                    sp.dma_start(to, src).then_inc(s_c, 16)
                sp.wait_ge(s_ones, 1)
                for n in range(HC):
                    sp.dma_start(feat[n * DH:(n + 1) * DH, n * M:(n + 1) * M], A["L1_attn_random_features"]).then_inc(s_c, 16)
                with sp.Fori(0, B // 2) as i:
                    for u in range(2):
                        sp.wait_ge(s_xfree, i * 2 + u + 1)
                        sp.dma_start(x[:, u], hi[i * 2 + u]).then_inc(s_x[u], 16)

            @block.gpsimd
            def _(pool):
                c = Chain(pool, s_pool)
                make_identity(pool, c, ident[:]).then_inc(s_ident, 1)
                c.link(pool.memset(mhalf[:], -0.5))
                with pool.Fori(0, B * 2) as i:
                    pool.wait_ge(s_var, i + 1)
                    pool.tensor_tensor(rstd[:], veps[:], mhalf[:], ALU.pow).then_inc(s_rstd, 1)

            @block.tensor
            def _(pe):
                pe.wait_ge(s_ident, 1)
                pe.wait_ge(s_c, 16 * (7 + HC))

                def turn(src):
                    for k in range(KC):
                        for t in range(TB):
                            m = pe.transpose(ps_t[0:KP, k, t * P:(t + 1) * P], src(t, k), ident[:])
                    m.then_inc(s_t, 1)

                with pe.Fori(0, B) as b:
                    pe.wait_ge(s_y, b + 1)
                    pe.wait_ge(s_tc, 2 * b)
                    turn(lambda t, k: y[:, t, k * KP:(k + 1) * KP])
                    pe.wait_ge(s_tc, 2 * b + 1)
                    for a in range(2):
                        pe.wait_ge(s_qc, 2 * b + a)
                        for c in range(KC):
                            for k in range(KC):
                                m = pe.matmul(ps_q[0:KP, c, :], W[:, k, a * D + c * KP:a * D + (c + 1) * KP], xT[:, k, :],
                                              start=(k == 0), stop=(k == KC - 1))
                        m.then_inc(s_q, 1)
                    for r in range(2):
                        if r == 1:
                            pe.wait_ge(s_vc, 2 * b + 1)
                        for t in range(2):
                            for k in range(KC):
                                m = pe.matmul(ps_m[:, t, 0:D], xT[:, k, (2 * r + t) * P:(2 * r + t + 1) * P],
                                              W[:, k, 2 * D:3 * D], start=(k == 0), stop=(k == KC - 1))
                        m.then_inc(s_v, 1)
                    pe.wait_ge(s_qc, 2 * b + 2)
                    pe.wait_ge(s_sq, 2 * b + 2)
                    for n in range(2 * TB):
                        t, c = n // 2, n % 2
                        pe.wait_ge(s_ec, b * NE + n - 1) if n else None
                        pe.matmul(ps_e[:, n % 2, 0:HC * M], t1[:, 1, c, t * P:(t + 1) * P], feat[:], start=True, stop=False)
                        pe.matmul(ps_e[:, n % 2, 0:HC * M], t2[:, 1, c, t * P:(t + 1) * P], half[:], start=False,
                                  stop=True).then_inc(s_e, 1)
                    for p in range(NP):
                        c, cols = p // 3, slice(p % 3 * P, (p % 3 + 1) * P)
                        n = 2 * TB + p
                        pe.wait_ge(s_ec, b * NE + n - 1)
                        pe.matmul(ps_e[:, n % 2, :], feat[:, cols], t1[:, 0, c, :], start=True, stop=False)
                        pe.matmul(ps_e[:, n % 2, :], half[:, cols], t2[:, 0, c, :], start=False,
                                  stop=True).then_inc(s_e, 1)
                    pe.wait_ge(s_vc, 2 * b + 2)
                    for p in range(NP):
                        for t in range(TB):
                            m = pe.matmul(ps_m[:].rearrange("p a f -> p (a f)")[:, p * 2 * V1:(p + 1) * 2 * V1],
                                          kp[:, t, p * P:(p + 1) * P],
                                          v1[:, t, 2 * p:2 * p + 2, :].rearrange("p a f -> p (a f)"),
                                          start=(t == 0), stop=(t == TB - 1))
                    m.then_inc(s_kv, 1)
                    pe.wait_ge(s_kvc, b + 1)
                    pe.wait_ge(s_ec, (b + 1) * NE)
                    for r in range(2):
                        pe.wait_ge(s_att, 2 * b + r)
                        for t in range(2):
                            for p in range(NP):
                                m = pe.matmul(ps_o[:, t, p * 2 * V1:(p + 1) * 2 * V1],
                                              qp[:, p, (2 * r + t) * P:(2 * r + t + 1) * P], kv[:, p, :],
                                              start=True, stop=True)
                        m.then_inc(s_num, 1)
                    pe.wait_ge(s_att, 2 * b + 2)
                    turn(lambda t, k: att[:, t, k * HC:(k + 1) * HC, :].rearrange("p h d -> p (h d)"))
                    pe.wait_ge(s_tc, 2 * b + 2)
                    for r in range(2):
                        if r == 1:
                            pe.wait_ge(s_proj, 2 * b + 1)
                        for t in range(2):
                            for k in range(KC):
                                m = pe.matmul(ps_m[:, t, 0:D], xT[:, k, (2 * r + t) * P:(2 * r + t + 1) * P], Wp[:, k, :],
                                              start=(k == 0), stop=(k == KC - 1))
                        m.then_inc(s_pr, 1)

            @block.scalar
            def _(act):
                with act.Fori(0, B // 2) as i:
                    for u in range(2):
                        b = i * 2 + u
                        for a in range(2):
                            act.wait_ge(s_qc, 2 * b + a + 1)
                            act.activation(t2[:, a], t1[:, a], ACT.Square).then_inc(s_sq, 1)
                        for n in range(2 * TB):
                            act.wait_ge(s_e, b * NE + n + 1)
                            act.activation(kp[:, n // 2, n % 2 * HC * M:(n % 2 + 1) * HC * M], ps_e[:, n % 2, 0:HC * M],
                                           ACT.Exp).then_inc(s_ec, 1)
                        for p in range(NP):
                            n = 2 * TB + p
                            act.wait_ge(s_e, b * NE + n + 1)
                            act.activation(qp[:, p, :], ps_e[:, n % 2, :], ACT.Exp).then_inc(s_ec, 1)
                        act.wait_ge(s_o, b + 1)
                        act.dma_start(ho[b], o[:, u]).then_inc(s_out[u], 16)
                for u in range(2):
                    act.wait_ge(s_out[u], B // 2 * 16)

            @block.vector
            def _(dve):
                c = Chain(dve, s_dve)
                c.link(dve.memset(feat[:], 0.0))
                c.link(dve.memset(v1[:], 1.0))
                dve.sem_inc(s_ones, 1)
                dve.sem_inc(s_xfree, 2)
                c.close()
                dve.wait_ge(s_c, 16 * (7 + HC))
                with dve.Fori(0, B // 2) as i:
                    for u in range(2):
                        b = i * 2 + u
                        xb, ob = x[:, u], o[:, u]
                        c = Chain(dve, s_dve)
                        dve.wait_ge(s_x[u], (i + 1) * 16)
                        norm_stats(dve, c, xb, stats, mv, 1e-5, veps[:]).then_inc(s_var, 1)
                        dve.wait_ge(s_rstd, 2 * b + 1)
                        norm_apply(dve, c, y, xb, mv, rstd)
                        c.wait()
                        dve.sem_inc(s_y, 1)
                        dve.wait_ge(s_t, 2 * b + 1)
                        dve.tensor_copy(xT[:], ps_t[0:KP]).then_inc(s_tc, 1)
                        c.link(dve.tensor_tensor(y[:], y[:], bcast(gb[:, 2:3, :], [P, TB, D]), ALU.add))
                        for a in range(2):
                            dve.wait_ge(s_q, 2 * b + a + 1)
                            dve.tensor_copy(t1[:, a], ps_q[0:KP]).then_inc(s_qc, 1)
                        for r in range(2):
                            dve.wait_ge(s_v, 2 * b + r + 1)
                            dve.tensor_copy(v1[:, 2 * r:2 * r + 2, :, 0:DH],
                                            ps_m[:, :, 0:D].rearrange("p t (h d) -> p t h d", h=H)).then_inc(s_vc, 1)
                        dve.wait_ge(s_kv, b + 1)
                        dve.tensor_tensor(kv[:], ps_m[:].rearrange("p a f -> p (a f)")[:, 0:NP * 2 * V1]
                                          .rearrange("p (n f) -> p n f", n=NP),
                                          bcast(kvmask[:].unsqueeze(1), [P, NP, 2 * V1]), ALU.mult).then_inc(s_kvc, 1)
                        for r in range(2):
                            dve.wait_ge(s_num, 2 * b + r + 1)
                            frac = ps_o[:, :, 0:H * V1].rearrange("p t (h f) -> p t h f", h=H)
                            dn = den[:, 2 * r:2 * r + 2, :]
                            c.link(dve.tensor_scalar(dn, frac[:, :, :, DH], 1e-6, None, ALU.add))
                            c.link(dve.reciprocal(dn, dn))
                            dve.tensor_tensor(att[:, 2 * r:2 * r + 2], frac[:, :, :, 0:DH],
                                              bcast(dn.unsqueeze(3), [P, 2, H, DH]), ALU.mult).then_inc(s_att, 1)
                        dve.wait_ge(s_t, 2 * b + 2)
                        dve.tensor_copy(xT[:], ps_t[0:KP]).then_inc(s_tc, 1)
                        for r in range(2):
                            dve.wait_ge(s_pr, 2 * b + r + 1)
                            c.link(dve.tensor_tensor(y[:, 2 * r:2 * r + 2], y[:, 2 * r:2 * r + 2], ps_m[:, :, 0:D], ALU.add))
                            dve.sem_inc(s_proj, 1)
                        norm_stats(dve, c, y, stats, mv, 1e-5, veps[:]).then_inc(s_var, 1)
                        dve.wait_ge(s_rstd, 2 * b + 2)
                        dve.wait_ge(s_out[u], i * 16)
                        norm_apply(dve, c, ob, y, mv, rstd)
                        c.wait()
                        c.link(dve.tensor_tensor(ob, ob, bcast(gb[:, 0:1, :], [P, TB, D]), ALU.mult))
                        c.link(dve.tensor_tensor(ob, ob, bcast(gb[:, 1:2, :], [P, TB, D]), ALU.add))
                        c.link(dve.tensor_tensor(ob, ob, xb, ALU.add))
                        dve.sem_inc(s_o, 1)
                        dve.sem_inc(s_xfree, 1)
                        c.close()


def stage_l1_ffn(nc, A, h_in, h_out):
    E, I = 4, 384
    C = I // P
    N = E * C
    R = 3
    with ExitStack() as ctx:
        st = Stage(nc, ctx, "l1f")
        x = st.sb("x", [P, 2, TB, D])
        y = st.sb("y", [P, TB, D])
        xT = st.sb("xT", [KP, 2, KC, S])
        Wg, Wu = st.sb("Wg", [KP, E, KC, I]), st.sb("Wu", [KP, E, KC, I])
        Wd = st.sb("Wd", [P, E, C, D])
        Wr = st.sb("Wr", [KP, KC, R])
        rb = st.sb("rb", [P, R])
        sg = st.sb("sg", [P, 2, S])
        hT = st.sb("hT", [P, 2, C, S])
        pr = st.sb("pr", [P, TB, R])
        cmp = st.sb("cmp", [P, 3, TB])
        keep = st.sb("keep", [P, TB, R])
        tot = st.sb("tot", [P, TB])
        o = st.sb("o", [P, 2, TB, D])
        ident = st.sb("ident", [P, P])
        stats, mv = st.sb("stats", [P, TB, 6]), st.sb("mv", [P, TB, 2])
        veps, rstd, mhalf = st.sb("veps", [P, TB]), st.sb("rstd", [P, TB]), st.sb("mhalf", [P, TB])
        ps_t = st.ps("ps_t", [P, KC, S])
        ps_g, ps_u = st.ps("ps_g", [P, 2, S]), st.ps("ps_u", [P, 2, S])
        ps_d = st.ps("ps_d", [P, TB, 256])
        s_x = [st.sem(f"x{u}") for u in range(2)]
        s_out = [st.sem(f"out{u}") for u in range(2)]
        names = "c xfree var rstd y t tc r rl p g u sg h d acc o dve pool ident".split()
        (s_c, s_xfree, s_var, s_rstd, s_y, s_t, s_tc, s_r, s_rl, s_p, s_g, s_u, s_sg, s_h, s_d, s_acc, s_o,
         s_dve, s_pool, s_ident) = (st.sem(n) for n in names)
        hi, ho = batch_tiles(h_in), batch_tiles(h_out)
        with nc.Block() as block:

            @block.sync
            def _(sp):
                loads = [(Wg[:, 0], A["L1_ffn_shared_gate"]), (Wu[:, 0], A["L1_ffn_shared_up"]),
                         (Wg[:, 1:], A["L1_ffn_routed_gate"]), (Wu[:, 1:], A["L1_ffn_routed_up"]),
                         (Wd[:, 0], A["L1_ffn_shared_down"]), (Wd[:, 1:], A["L1_ffn_routed_down"]),
                         (Wr[:], A["L1_ffn_router_w"]), (rb[:], A["L1_ffn_routing_bias"].partition_broadcast(P))]
                sp.dma_start(x[:, 0], hi[0]).then_inc(s_x[0], 16)
                for to, src in loads:
                    sp.dma_start(to, src).then_inc(s_c, 16)
                with sp.Fori(0, B // 2) as i:
                    for u in range(2):
                        b = i * 2 + u
                        sp.wait_ge(s_xfree, b + 1)
                        sp.dma_start(x[:, 1 - u], hi[(b + 1) % B]).then_inc(s_x[1 - u], 16)

            @block.gpsimd
            def _(pool):
                c = Chain(pool, s_pool)
                make_identity(pool, c, ident[:]).then_inc(s_ident, 1)
                c.link(pool.memset(mhalf[:], -0.5))
                with pool.Fori(0, B + 1) as i:
                    pool.wait_ge(s_var, i + 1)
                    pool.tensor_tensor(rstd[:], veps[:], mhalf[:], ALU.pow).then_inc(s_rstd, 1)

            @block.tensor
            def _(pe):

                def turn(b, u):
                    pe.wait_ge(s_y, b + 1)
                    for k in range(KC):
                        for t in range(TB):
                            m = pe.transpose(ps_t[0:KP, k, t * P:(t + 1) * P], y[:, t, k * KP:(k + 1) * KP], ident[:])
                    m.then_inc(s_t, 1)

                def down(b, e):
                    pe.wait_ge(s_h, b * N + (e + 1) * C)
                    pe.wait_ge(s_acc, b * E + e)
                    if e == 0:
                        pe.wait_ge(s_rl, b + 1)
                    for t in range(TB):
                        for k in range(C):
                            m = pe.matmul(ps_d[:, t, 0:D], hT[:, e % 2, k, t * P:(t + 1) * P], Wd[:, e, k, :],
                                          start=(k == 0), stop=(k == C - 1))
                    m.then_inc(s_d, 1)

                pe.wait_ge(s_ident, 1)
                turn(0, 0)
                pe.wait_ge(s_c, 16 * 8)
                with pe.Fori(0, B // 2) as i:
                    for u in range(2):
                        b = i * 2 + u
                        pe.wait_ge(s_tc, b + 1)
                        pe.wait_ge(s_acc, b * E)
                        for t in range(TB):
                            for k in range(KC):
                                m = pe.matmul(ps_d[:, t, D:D + R], xT[:, u, k, t * P:(t + 1) * P], Wr[:, k, :],
                                              start=(k == 0), stop=(k == KC - 1))
                        m.then_inc(s_r, 1)
                        for n in range(N):
                            e, c = n // C, n % C
                            cols = slice(c * P, (c + 1) * P)
                            pe.wait_ge(s_h, b * N + n - 1) if n else None
                            for W, bank in ((Wg, ps_g), (Wu, ps_u)):
                                for k in range(KC):
                                    m = pe.matmul(bank[:, n % 2], W[:, e, k, cols], xT[:, u, k, :],
                                                  start=(k == 0), stop=(k == KC - 1))
                                m.then_inc(s_g if bank is ps_g else s_u, 1)
                            if c == 1 and e:
                                down(b, e - 1)
                        turn(b + 1, 1 - u)
                        down(b, E - 1)

            @block.scalar
            def _(act):
                with act.Fori(0, B // 2) as i:
                    for u in range(2):
                        b = i * 2 + u
                        act.wait_ge(s_rl, b + 1)
                        act.activation(pr[:], pr[:], ACT.Sigmoid).then_inc(s_p, 1)
                        for n in range(N):
                            act.wait_ge(s_g, b * N + n + 1)
                            act.wait_ge(s_h, b * N + n - 1) if n else None
                            act.activation(sg[:, n % 2], ps_g[:, n % 2], ACT.Silu).then_inc(s_sg, 1)
                        act.wait_ge(s_o, b + 1)
                        act.dma_start(ho[b], o[:, u]).then_inc(s_out[u], 16)
                for u in range(2):
                    act.wait_ge(s_out[u], B // 2 * 16)

            @block.vector
            def _(dve):

                def norm(c, b, i, u):
                    dve.wait_ge(s_x[u], (i + 1) * 16)
                    norm_stats(dve, c, x[:, u], stats, mv, 1e-5, veps[:]).then_inc(s_var, 1)
                    dve.wait_ge(s_rstd, b + 1)
                    norm_apply(dve, c, y, x[:, u], mv, rstd)
                    c.wait()
                    dve.sem_inc(s_y, 1)

                def weights(c):
                    p0, p1, p2 = (pr[:, :, e] for e in range(R))
                    c20, c21, c10 = (cmp[:, k, :] for k in range(3))
                    k0, k1, k2 = (keep[:, :, e] for e in range(R))
                    c.mark(dve.tensor_tensor(c20, p2, p0, ALU.is_gt))
                    c.mark(dve.tensor_tensor(c21, p2, p1, ALU.is_gt))
                    c.link(dve.tensor_tensor(c10, p1, p0, ALU.is_gt))
                    c.mark(dve.tensor_tensor(k2, c20, c21, ALU.max))
                    c.mark(dve.tensor_tensor(k1, c21, c21, ALU.mult))
                    c.mark(dve.tensor_tensor(k0, c20, c10, ALU.mult))
                    c.wait()
                    c.link(dve.tensor_scalar(k1, k1, -1.0, 1.0, ALU.mult, ALU.add))
                    c.mark(dve.tensor_tensor(k1, k1, c10, ALU.max))
                    c.link(dve.tensor_scalar(k0, k0, -1.0, 1.0, ALU.mult, ALU.add))
                    c.link(dve.tensor_tensor(pr[:], pr[:], keep[:], ALU.mult))
                    c.link(dve.tensor_reduce(tot[:], pr[:], AX.X, ALU.add))
                    c.link(dve.reciprocal(tot[:], tot[:]))
                    c.link(dve.tensor_tensor(pr[:], pr[:], bcast(tot[:].unsqueeze(2), [P, TB, R]), ALU.mult))

                def accumulate(c, b, e, i, u):
                    dve.wait_ge(s_d, b * E + e + 1)
                    if e == 0:
                        dve.wait_ge(s_out[u], i * 16)
                        c.link(dve.tensor_tensor(o[:, u], ps_d[:, :, 0:D], x[:, u], ALU.add))
                    else:
                        for t in range(TB):
                            c.mark(dve.scalar_tensor_tensor(o[:, u, t, :], ps_d[:, t, 0:D], pr[:, t, e - 1:e],
                                                            o[:, u, t, :], ALU.mult, ALU.add))
                        c.wait()
                    dve.sem_inc(s_acc, 1)

                dve.sem_inc(s_xfree, 1)
                c = Chain(dve, s_dve)
                norm(c, 0, 0, 0)
                dve.wait_ge(s_t, 1)
                dve.tensor_copy(xT[:, 0], ps_t[0:KP]).then_inc(s_tc, 1)
                c.close()
                dve.wait_ge(s_c, 16 * 8)
                with dve.Fori(0, B // 2) as i:
                    for u in range(2):
                        b = i * 2 + u
                        c = Chain(dve, s_dve)
                        dve.wait_ge(s_r, b + 1)
                        c.link(dve.tensor_tensor(pr[:], ps_d[:, :, D:D + R], bcast(rb[:].unsqueeze(1), [P, TB, R]), ALU.add))
                        dve.sem_inc(s_rl, 1)
                        for n in range(N):
                            e = n // C
                            dve.wait_ge(s_sg, b * N + n + 1)
                            dve.wait_ge(s_u, b * N + n + 1)
                            dve.tensor_tensor(hT[:, e % 2, n % C, :], sg[:, n % 2], ps_u[:, n % 2], ALU.mult).then_inc(s_h, 1)
                            if n == 1:
                                dve.wait_ge(s_p, b + 1)
                                weights(c)
                            if n % C == 2 and e:
                                accumulate(c, b, e - 1, i, u)
                            if n == 6:
                                norm(c, b + 1, (i if u == 0 else i + 1), 1 - u)
                        dve.wait_ge(s_t, b + 2)
                        dve.tensor_copy(xT[:, 1 - u], ps_t[0:KP]).then_inc(s_tc, 1)
                        accumulate(c, b, E - 1, i, u)
                        dve.sem_inc(s_o, 1)
                        dve.sem_inc(s_xfree, 1)
                        c.close()


def top1(dve, act_turn, c, logits, shape, m, oh, val, rank, best, ex, prob):
    N, E = shape
    full = [P, N, E]
    c.link(dve.tensor_reduce(m[:], logits, AX.X, ALU.max))
    c.mark(dve.tensor_tensor(ex[:], logits, bcast(m[:].unsqueeze(2), full), ALU.subtract))
    c.link(dve.tensor_tensor(oh[:], logits, bcast(m[:].unsqueeze(2), full), ALU.is_ge))
    act_turn()
    c.link(dve.tensor_tensor(val[:], oh[:], bcast(rank[:, 0:E].unsqueeze(1), full), ALU.mult))
    c.link(dve.tensor_reduce(best[:], val[:], AX.X, ALU.max))
    c.link(dve.tensor_tensor(oh[:], val[:], bcast(best[:].unsqueeze(2), full), ALU.is_equal))
    c.link(dve.tensor_reduce(prob[:], ex[:], AX.X, ALU.add))
    c.link(dve.reciprocal(prob[:], prob[:]))


def grouped_ffn_stage(nc, A, name, xs_d, ys_d, eid_d, w1_d, w2_d, b1_d, b2_d, func, NG, TG):
    F, C = 768, 6
    N = TG * P
    with ExitStack() as ctx:
        st = Stage(nc, ctx, name)
        eid = st.sb("eid", [1, NG + 1], I32)
        w1 = st.sb("w1", [KP, 2, KC, F])
        w2 = st.sb("w2", [P, 2, C, D])
        b1 = st.sb("b1", [P, 2, C])
        b2 = st.sb("b2", [P, 2, D])
        x = st.sb("x", [P, 2, TG, D])
        xT = st.sb("xT", [KP, 2, KC, N])
        hT = st.sb("hT", [P, 2, C, N])
        o = st.sb("o", [P, 2, TG, D])
        ident = st.sb("ident", [P, P])
        ps_t = st.ps("ps_t", [P, KC, S])
        ps_h = st.ps("ps_h", [P, 3, S])
        ps_y = st.ps("ps_y", [P, 2 if TG == 4 else 1, S])
        s_w = [st.sem(f"w{u}") for u in range(2)]
        s_x = [st.sem(f"x{u}") for u in range(2)]
        s_out = [st.sem(f"out{u}") for u in range(2)]
        names = "e t tc h hc y o pool ident".split()
        s_e, s_t, s_tc, s_h, s_hc, s_y, s_o, s_pool, s_ident = (st.sem(n) for n in names)
        xi = xs_d.rearrange("(g t p) d -> g p t d", t=TG, p=P)
        yo = ys_d.rearrange("(g t p) d -> g p t d", t=TG, p=P)
        nw = 2 + (b1_d is not None) * 2

        def y_bank(t):
            return ps_y[:, t // 2, t % 2 * 256:t % 2 * 256 + D]

        with nc.Block() as block:

            @block.sync
            def _(sp):

                def load(g, u):
                    e = sp.value_load(eid[0:1, bass.ds(g, 1)], min_val=0, max_val=w1_d.shape[0] - 1)
                    sp.dma_start(x[:, u], xi[g % NG]).then_inc(s_x[u], 16)
                    sp.dma_start(w1[:, u], w1_d[e]).then_inc(s_w[u], 16)
                    sp.dma_start(w2[:, u], w2_d[e]).then_inc(s_w[u], 16)
                    if b1_d is not None:
                        sp.dma_start(b1[:, u], b1_d[e]).then_inc(s_w[u], 16)
                        sp.dma_start(b2[:, u], b2_d[e].partition_broadcast(P)).then_inc(s_w[u], 16)

                sp.dma_start(eid[0:1, 0:NG], eid_d[0:1, 0:NG]).then_inc(s_e, 16)
                sp.dma_start(eid[0:1, NG:NG + 1], eid_d[0:1, 0:1]).then_inc(s_e, 16)
                sp.wait_ge(s_e, 32)
                load(0, 0)
                with sp.Fori(0, NG // 2) as i:
                    for u in range(2):
                        g = i * 2 + u
                        sp.wait_ge(s_o, g)
                        load(g + 1, 1 - u)
                sp.wait_ge(s_x[0], (NG // 2 + 1) * 16)
                sp.wait_ge(s_w[0], (NG // 2 + 1) * 16 * nw)

            @block.gpsimd
            def _(pool):
                c = Chain(pool, s_pool)
                make_identity(pool, c, ident[:]).then_inc(s_ident, 1)

            @block.tensor
            def _(pe):

                def turn(i, u):
                    pe.wait_ge(s_x[u], (i + 1) * 16)
                    for k in range(KC):
                        for t in range(TG):
                            m = pe.transpose(ps_t[0:KP, k, t * P:(t + 1) * P], x[:, u, t, k * KP:(k + 1) * KP], ident[:])
                    m.then_inc(s_t, 1)

                pe.wait_ge(s_ident, 1)
                turn(0, 0)
                with pe.Fori(0, NG // 2) as i:
                    for u in range(2):
                        g = i * 2 + u
                        pe.wait_ge(s_w[u], (i + 1) * 16 * nw)
                        pe.wait_ge(s_tc, g + 1)
                        for c in range(C):
                            pe.wait_ge(s_hc, g * C + c - 2) if c > 1 else None
                            for k in range(KC):
                                m = pe.matmul(ps_h[:, c % 3, 0:N], w1[:, u, k, c * P:(c + 1) * P], xT[:, u, k, :],
                                              start=(k == 0), stop=(k == KC - 1))
                            m.then_inc(s_h, 1)
                        turn(i if u == 0 else i + 1, 1 - u)
                        pe.wait_ge(s_hc, (g + 1) * C)
                        pe.wait_ge(s_o, g)
                        for t in range(TG):
                            for c in range(C):
                                m = pe.matmul(y_bank(t), hT[:, u, c, t * P:(t + 1) * P], w2[:, u, c, :],
                                              start=(c == 0), stop=(c == C - 1))
                        m.then_inc(s_y, 1)

            @block.scalar
            def _(act):
                with act.Fori(0, NG // 2) as i:
                    for u in range(2):
                        g = i * 2 + u
                        act.wait_ge(s_w[u], (i + 1) * 16 * nw)
                        for c in range(C):
                            act.wait_ge(s_h, g * C + c + 1)
                            bias = 0.0 if b1_d is None else b1[:, u, c:c + 1]
                            act.activation(hT[:, u, c, :], ps_h[:, c % 3, 0:N], func, bias=bias).then_inc(s_hc, 1)
                        act.wait_ge(s_o, g + 1)
                        act.dma_start(yo[g], o[:, u]).then_inc(s_out[u], 16)
                for u in range(2):
                    act.wait_ge(s_out[u], NG // 2 * 16)

            @block.vector
            def _(dve):

                def copy_x(g, u):
                    dve.wait_ge(s_t, g + 1)
                    dve.tensor_copy(xT[:, u], ps_t[0:KP, :, 0:N]).then_inc(s_tc, 1)

                copy_x(0, 0)
                with dve.Fori(0, NG // 2) as i:
                    for u in range(2):
                        g = i * 2 + u
                        copy_x(g + 1, 1 - u)
                        dve.wait_ge(s_y, g + 1)
                        dve.wait_ge(s_out[u], i * 16)
                        view = ps_y[:].rearrange("p a (b f) -> p (a b) f", b=2)[:, 0:TG, 0:D]
                        if b2_d is None:
                            dve.tensor_copy(o[:, u], view).then_inc(s_o, 1)
                        else:
                            dve.tensor_tensor(o[:, u], view, bcast(b2[:, u:u + 1, :], [P, TG, D]), ALU.add).then_inc(s_o, 1)


def l2_gate_stage(nc, A, h_in, xs_d, eid_d, prob_d):
    E = 3
    with ExitStack() as ctx:
        st = Stage(nc, ctx, "l2g")
        x = st.sb("x", [P, 2, TB, D])
        y = st.sb("y", [P, 2, TB, D])
        Wg = st.sb("Wg", [KP, KC, E])
        rank = st.sb("rank", [P, 16])
        mean = st.sb("mean", [KP, KC, P])
        ones = st.sb("ones", [P, P])
        lg, ex, oh, val = (st.sb(n, [P, B, E]) for n in ("lg", "ex", "oh", "val"))
        m, best, prob = (st.sb(n, [P, B]) for n in ("m", "best", "prob"))
        eid = st.sb("eid", [P, B], I32)
        stats, mv = st.sb("stats", [P, TB, 6]), st.sb("mv", [P, TB, 2])
        veps, rstd, mhalf = st.sb("veps", [P, TB]), st.sb("rstd", [P, TB]), st.sb("mhalf", [P, TB])
        ps_m, ps_l = st.ps("ps_m", [P, KC]), st.ps("ps_l", [P, E])
        s_x = [st.sem(f"x{u}") for u in range(2)]
        s_out = [st.sem(f"out{u}") for u in range(2)]
        names = "c xfree var rstd y m mc l lc ex exd fin pool dve fout".split()
        (s_c, s_xfree, s_var, s_rstd, s_y, s_m, s_mc, s_l, s_lc, s_ex, s_exd, s_fin, s_pool, s_dve,
         s_fout) = (st.sem(n) for n in names)
        hi, ho = batch_tiles(h_in), batch_tiles(xs_d)
        with nc.Block() as block:

            @block.sync
            def _(sp):
                sp.dma_start(Wg[:], A["L2_ffn_Wg"]).then_inc(s_c, 16)
                sp.dma_start(rank[:], A["c_rank"]).then_inc(s_c, 16)
                with sp.Fori(0, B // 2) as i:
                    for u in range(2):
                        sp.wait_ge(s_xfree, i * 2 + u + 1)
                        sp.dma_start(x[:, u], hi[i * 2 + u]).then_inc(s_x[u], 16)
                sp.wait_ge(s_fin, 1)
                sp.dma_start(eid_d, eid[0:1, :]).then_inc(s_fout, 16)
                sp.dma_start(prob_d, prob[:]).then_inc(s_fout, 16)
                sp.wait_ge(s_fout, 32)

            @block.gpsimd
            def _(pool):
                c = Chain(pool, s_pool)
                c.link(pool.memset(mhalf[:], -0.5))
                with pool.Fori(0, B) as i:
                    pool.wait_ge(s_var, i + 1)
                    pool.tensor_tensor(rstd[:], veps[:], mhalf[:], ALU.pow).then_inc(s_rstd, 1)

            @block.tensor
            def _(pe):
                pe.wait_ge(s_c, 32)
                with pe.Fori(0, B // 2) as i:
                    for u in range(2):
                        b = i * 2 + u
                        pe.wait_ge(s_y, b + 1)
                        for k in range(KC):
                            for t in range(TB):
                                mm = pe.matmul(ps_m[0:KP, k:k + 1], y[:, u, t, k * KP:(k + 1) * KP], ones[:, 0:1],
                                               start=(t == 0), stop=(t == TB - 1))
                        mm.then_inc(s_m, 1)
                        pe.wait_ge(s_mc, b + 1)
                        for k in range(KC):
                            mm = pe.matmul(ps_l[:], mean[:, k, :], Wg[:, k, :], start=(k == 0), stop=(k == KC - 1))
                        mm.then_inc(s_l, 1)

            @block.scalar
            def _(act):
                with act.Fori(0, B // 2) as i:
                    for u in range(2):
                        b = i * 2 + u
                        act.wait_ge(s_y, b + 1)
                        act.dma_start(ho[b], y[:, u]).then_inc(s_out[u], 16)
                act.wait_ge(s_ex, 1)
                act.activation(ex[:], ex[:], ACT.Exp).then_inc(s_exd, 1)
                for u in range(2):
                    act.wait_ge(s_out[u], B // 2 * 16)

            @block.vector
            def _(dve):
                c = Chain(dve, s_dve)
                c.link(dve.memset(ones[:], 1.0))
                dve.sem_inc(s_xfree, 2)
                c.close()
                dve.wait_ge(s_c, 32)
                with dve.Fori(0, B // 2) as i:
                    for u in range(2):
                        b = i * 2 + u
                        c = Chain(dve, s_dve)
                        dve.wait_ge(s_x[u], (i + 1) * 16)
                        norm_stats(dve, c, x[:, u], stats, mv, 1e-5, veps[:]).then_inc(s_var, 1)
                        dve.wait_ge(s_rstd, b + 1)
                        dve.wait_ge(s_out[u], i * 16)
                        norm_apply(dve, c, y[:, u], x[:, u], mv, rstd)
                        c.wait()
                        dve.sem_inc(s_y, 1)
                        dve.sem_inc(s_xfree, 1)
                        dve.wait_ge(s_m, b + 1)
                        c.mark(dve.tensor_scalar(mean[:], bcast(ps_m[0:KP].unsqueeze(2), [KP, KC, P]), 1.0 / S, None, ALU.mult))
                        c.wait()
                        dve.sem_inc(s_mc, 1)
                        dve.wait_ge(s_l, b + 1)
                        c.link(dve.tensor_copy(lg[:, bass.ds(b, 1), :], ps_l[:].unsqueeze(1)))
                        c.close()
                c = Chain(dve, s_dve)

                def act_turn():
                    dve.sem_inc(s_ex, 1)
                    dve.wait_ge(s_exd, 1)

                top1(dve, act_turn, c, lg[:], (B, E), m, oh, val, rank, best, ex, prob)
                c.link(dve.tensor_scalar(eid[:], best[:], -1.0, 16.0, ALU.mult, ALU.add))
                dve.sem_inc(s_fin, 1)
                c.close()


def l2_add_stage(nc, A, h_in, ys_d, prob_d, h_out):
    with ExitStack() as ctx:
        st = Stage(nc, ctx, "l2s")
        x, ys, o = (st.sb(n, [P, 2, TB, D]) for n in ("x", "ys", "o"))
        prob = st.sb("prob", [P, B])
        pb = st.sb("pb", [P, 1])
        s_x = [st.sem(f"x{u}") for u in range(2)]
        s_out = [st.sem(f"out{u}") for u in range(2)]
        s_c, s_free, s_o, s_dve = (st.sem(n) for n in ("c", "free", "o", "dve"))
        hi, yi, ho = batch_tiles(h_in), batch_tiles(ys_d), batch_tiles(h_out)
        with nc.Block() as block:

            @block.sync
            def _(sp):
                sp.dma_start(prob[:], prob_d).then_inc(s_c, 16)
                with sp.Fori(0, B // 2) as i:
                    for u in range(2):
                        b = i * 2 + u
                        sp.wait_ge(s_free, b + 1)
                        sp.dma_start(x[:, u], hi[b]).then_inc(s_x[u], 16)
                        sp.dma_start(ys[:, u], yi[b]).then_inc(s_x[u], 16)

            @block.vector
            def _(dve):
                dve.sem_inc(s_free, 2)
                dve.wait_ge(s_c, 16)
                with dve.Fori(0, B // 2) as i:
                    for u in range(2):
                        c = Chain(dve, s_dve)
                        c.link(dve.tensor_copy(pb[:], prob[:, bass.ds(i * 2 + u, 1)]))
                        dve.wait_ge(s_x[u], (i + 1) * 32)
                        dve.wait_ge(s_out[u], i * 16)
                        c.link(dve.scalar_tensor_tensor(o[:, u], ys[:, u], pb[:, 0:1], x[:, u], ALU.mult, ALU.add))
                        dve.sem_inc(s_o, 1)
                        dve.sem_inc(s_free, 1)
                        c.close()

            @block.scalar
            def _(act):
                with act.Fori(0, B // 2) as i:
                    for u in range(2):
                        b = i * 2 + u
                        act.wait_ge(s_o, b + 1)
                        act.dma_start(ho[b], o[:, u]).then_inc(s_out[u], 16)
                for u in range(2):
                    act.wait_ge(s_out[u], B // 2 * 16)


def stage_l2_ffn(nc, A, h_in, h_out):
    xs = nc.dram_tensor("d_l2f_xs", (T, D), F32).ap()
    ys = nc.dram_tensor("d_l2f_ys", (T, D), F32).ap()
    eid = nc.dram_tensor("d_l2f_eid", (1, B), I32).ap()
    prob = nc.dram_tensor("d_l2f_prob", (P, B), F32).ap()
    l2_gate_stage(nc, A, h_in, xs, eid, prob)
    grouped_ffn_stage(nc, A, "l2f", xs, ys, eid, A["L2_ffn_W1"], A["L2_ffn_W2"], A["L2_ffn_b1"], A["L2_ffn_b2"],
                      ACT.Gelu, B, TB)
    l2_add_stage(nc, A, h_in, ys, prob, h_out)


def l3_token_attention_stage(nc, A, h_in, x2_d):
    H, DH = 12, 16
    HF = DH // 2
    NQ = D + 2 * DH
    with ExitStack() as ctx:
        st = Stage(nc, ctx, "l3i")
        x = st.sb("x", [P, 2, TB, D])
        y = st.sb("y", [P, TB, D])
        z = st.sb("z", [P, TB, D])
        o = st.sb("o", [P, 2, TB, D])
        zT = st.sb("zT", [KP, KC, S])
        W = st.sb("W", [KP, KC, NQ])
        bias = st.sb("bias", [P, NQ])
        gb = st.sb("gb", [P, 2, D])
        qkv = st.sb("qkv", [P, TB, NQ])
        cos, sin, cosq, sinq = (st.sb(n, [P, TB, HF]) for n in ("cos", "sin", "cosq", "sinq"))
        ta, tb = st.sb("ta", [P, TB, H, HF]), st.sb("tb", [P, TB, H, HF])
        qr = st.sb("qr", [P, TB, H, DH])
        kr = st.sb("kr", [P, TB, DH])
        sc, mx, ex = (st.sb(n, [P, TB, H]) for n in ("sc", "mx", "ex"))
        ident = st.sb("ident", [P, P])
        stats, mv = st.sb("stats", [P, TB, 6]), st.sb("mv", [P, TB, 2])
        veps, rstd, mhalf = st.sb("veps", [P, TB]), st.sb("rstd", [P, TB]), st.sb("mhalf", [P, TB])
        ps_t = st.ps("ps_t", [P, KC, S])
        ps_p = st.ps("ps_p", [P, TB, 256])
        s_x = [st.sem(f"x{u}") for u in range(2)]
        s_out = [st.sem(f"out{u}") for u in range(2)]
        names = "c xfree var rstd z t tc p sc ex o dve pool ident".split()
        (s_c, s_xfree, s_var, s_rstd, s_z, s_t, s_tc, s_p, s_sc, s_ex, s_o, s_dve, s_pool,
         s_ident) = (st.sem(n) for n in names)
        hi, ho = batch_tiles(h_in), batch_tiles(x2_d)
        with nc.Block() as block:

            @block.sync
            def _(sp):
                loads = [(W[:, :, 0:D], A["L3_attn_Wq"]), (W[:, :, D:D + DH], A["L3_attn_Wk"]),
                         (W[:, :, D + DH:], A["L3_attn_Wv"]),
                         (bias[:, 0:D], A["L3_attn_bq"].partition_broadcast(P)),
                         (bias[:, D:D + DH], A["L3_attn_bk"].partition_broadcast(P)),
                         (bias[:, D + DH:], A["L3_attn_bv"].partition_broadcast(P)),
                         (gb[:, 0, :], A["L3_attn_ln1_g"].partition_broadcast(P)),
                         (gb[:, 1, :], A["L3_attn_ln1_b"].partition_broadcast(P)),
                         (cos[:], A["c_cos"]), (sin[:], A["c_sin"])]
                for to, src in loads:
                    sp.dma_start(to, src).then_inc(s_c, 16)
                with sp.Fori(0, B // 2) as i:
                    for u in range(2):
                        sp.wait_ge(s_xfree, i * 2 + u + 1)
                        sp.dma_start(x[:, u], hi[i * 2 + u]).then_inc(s_x[u], 16)

            @block.gpsimd
            def _(pool):
                c = Chain(pool, s_pool)
                make_identity(pool, c, ident[:]).then_inc(s_ident, 1)
                c.link(pool.memset(mhalf[:], -0.5))
                with pool.Fori(0, 2 * B) as i:
                    pool.wait_ge(s_var, i + 1)
                    pool.tensor_tensor(rstd[:], veps[:], mhalf[:], ALU.pow).then_inc(s_rstd, 1)

            @block.tensor
            def _(pe):
                pe.wait_ge(s_ident, 1)
                pe.wait_ge(s_c, 160)
                with pe.Fori(0, B) as b:
                    pe.wait_ge(s_z, b + 1)
                    for k in range(KC):
                        for t in range(TB):
                            m = pe.transpose(ps_t[0:KP, k, t * P:(t + 1) * P], z[:, t, k * KP:(k + 1) * KP], ident[:])
                    m.then_inc(s_t, 1)
                    pe.wait_ge(s_tc, b + 1)
                    for t in range(TB):
                        for k in range(KC):
                            m = pe.matmul(ps_p[:, t, 0:NQ], zT[:, k, t * P:(t + 1) * P], W[:, k, :],
                                          start=(k == 0), stop=(k == KC - 1))
                    m.then_inc(s_p, 1)

            @block.scalar
            def _(act):
                with act.Fori(0, B // 2) as i:
                    for u in range(2):
                        b = i * 2 + u
                        act.wait_ge(s_sc, b + 1)
                        act.activation(ex[:], sc[:], ACT.Exp).then_inc(s_ex, 1)
                        act.wait_ge(s_o, b + 1)
                        act.dma_start(ho[b], o[:, u]).then_inc(s_out[u], 16)
                for u in range(2):
                    act.wait_ge(s_out[u], B // 2 * 16)

            @block.vector
            def _(dve):
                c = Chain(dve, s_dve)
                dve.sem_inc(s_xfree, 2)
                dve.wait_ge(s_c, 160)
                c.mark(dve.tensor_scalar(cosq[:], cos[:], DH ** -0.5, None, ALU.mult))
                c.mark(dve.tensor_scalar(sinq[:], sin[:], DH ** -0.5, None, ALU.mult))
                c.close()
                hf = [P, TB, H, HF]
                with dve.Fori(0, B // 2) as i:
                    for u in range(2):
                        b = i * 2 + u
                        c = Chain(dve, s_dve)
                        dve.wait_ge(s_x[u], (i + 1) * 16)
                        norm_stats(dve, c, x[:, u], stats, mv, 1e-5, veps[:]).then_inc(s_var, 1)
                        dve.wait_ge(s_rstd, 2 * b + 1)
                        norm_apply(dve, c, y, x[:, u], mv, rstd)
                        c.wait()
                        dve.sem_inc(s_xfree, 1)
                        norm_stats(dve, c, y, stats, mv, 1e-5, veps[:]).then_inc(s_var, 1)
                        dve.wait_ge(s_rstd, 2 * b + 2)
                        norm_apply(dve, c, z, y, mv, rstd)
                        c.wait()
                        c.link(dve.tensor_tensor(z[:], z[:], bcast(gb[:, 0:1, :], [P, TB, D]), ALU.mult))
                        c.link(dve.tensor_tensor(z[:], z[:], bcast(gb[:, 1:2, :], [P, TB, D]), ALU.add))
                        dve.sem_inc(s_z, 1)
                        dve.wait_ge(s_t, b + 1)
                        dve.tensor_copy(zT[:], ps_t[0:KP]).then_inc(s_tc, 1)
                        dve.wait_ge(s_p, b + 1)
                        c.link(dve.tensor_tensor(qkv[:], ps_p[:, :, 0:NQ], bcast(bias[:].unsqueeze(1), [P, TB, NQ]), ALU.add))
                        q = qkv[:, :, 0:D].rearrange("p t (h a f) -> p t h a f", h=H, a=2)
                        k = qkv[:, :, D:D + DH].rearrange("p t (a f) -> p t a f", a=2)
                        q1, q2, k1, k2 = q[:, :, :, 0, :], q[:, :, :, 1, :], k[:, :, 0, :], k[:, :, 1, :]
                        cq, sq = (bcast(w[:].unsqueeze(2), hf) for w in (cosq, sinq))
                        c.mark(dve.tensor_tensor(ta[:], q1, cq, ALU.mult))
                        c.link(dve.tensor_tensor(tb[:], q2, sq, ALU.mult))
                        c.link(dve.tensor_tensor(qr[:, :, :, 0:HF], ta[:], tb[:], ALU.subtract))
                        c.mark(dve.tensor_tensor(ta[:], q2, cq, ALU.mult))
                        c.link(dve.tensor_tensor(tb[:], q1, sq, ALU.mult))
                        c.link(dve.tensor_tensor(qr[:, :, :, HF:DH], ta[:], tb[:], ALU.add))
                        c.mark(dve.tensor_tensor(ta[:, :, 0, :], k1, cos[:], ALU.mult))
                        c.link(dve.tensor_tensor(tb[:, :, 0, :], k2, sin[:], ALU.mult))
                        c.link(dve.tensor_tensor(kr[:, :, 0:HF], ta[:, :, 0, :], tb[:, :, 0, :], ALU.subtract))
                        c.mark(dve.tensor_tensor(ta[:, :, 0, :], k2, cos[:], ALU.mult))
                        c.link(dve.tensor_tensor(tb[:, :, 0, :], k1, sin[:], ALU.mult))
                        c.link(dve.tensor_tensor(kr[:, :, HF:DH], ta[:, :, 0, :], tb[:, :, 0, :], ALU.add))
                        c.link(dve.tensor_tensor(qr[:], qr[:], bcast(kr[:].unsqueeze(2), [P, TB, H, DH]), ALU.mult))
                        c.link(dve.tensor_reduce(sc[:], qr[:], AX.X, ALU.add))
                        c.link(dve.tensor_tensor(mx[:], sc[:], sc[:], ALU.max))
                        c.link(dve.tensor_tensor(sc[:], sc[:], mx[:], ALU.subtract))
                        dve.sem_inc(s_sc, 1)
                        dve.wait_ge(s_ex, b + 1)
                        c.link(dve.tensor_scalar(mx[:], ex[:], float(H), None, ALU.mult))
                        c.link(dve.reciprocal(mx[:], mx[:]))
                        c.link(dve.scalar_tensor_tensor(sc[:], ex[:], float(H), mx[:], ALU.mult, ALU.mult))
                        dve.wait_ge(s_out[u], i * 16)
                        v = qkv[:, :, D + DH:]
                        full = [P, TB, H, DH]
                        c.link(dve.tensor_tensor(qr[:], bcast(v.unsqueeze(2), full), bcast(sc[:].unsqueeze(3), full), ALU.mult))
                        c.link(dve.tensor_tensor(o[:, u], qr[:].rearrange("p t h d -> p t (h d)"), y[:], ALU.add))
                        dve.sem_inc(s_o, 1)
                        c.close()


def router_stage(nc, A, name, E, h_in, res_d, z_d, xs_d, eid_d, tok_d, w_router, NG, cap=None,
                 moe=None, switch=None):
    with ExitStack() as ctx:
        st = Stage(nc, ctx, name)
        x, o = st.sb("x", [P, 2, TB, D]), st.sb("o", [P, 2, TB, D])
        y = st.sb("y", [P, 2, TB, D])
        z = st.sb("z", [P, 2, TB, D])
        zT = st.sb("zT", [KP, KC, S])
        sq = st.sb("sq", [P, TB, D])
        gb = st.sb("gb", [P, 2, D])
        rb = st.sb("rb", [P, E])
        Wr = st.sb("Wr", [KP, KC, E])
        rank, upper = st.sb("rank", [P, 16]), st.sb("upper", [P, P])
        count = st.sb("count", [P, NG])
        ones, ident = st.sb("ones", [P, P]), st.sb("ident", [P, P])
        zeros = st.sb("zeros", [P, D])
        lg, ex, oh, val, tot, before, run = (st.sb(n, [P, NT, E]) for n in ("lg", "ex", "oh", "val", "tot", "before", "run"))
        m, best = st.sb("m", [P, NT]), st.sb("best", [P, NT])
        tok = st.sb("tok", [P, 3, NT])
        pos = st.sb("pos", [P, NT], I32)
        row = st.sb("row", [P, 2, TB], I32)
        zl = st.sb("zl", [P, 2, TB, D])
        ntile, start, swap = (st.sb(n, [P, E]) for n in ("ntile", "start", "swap"))
        ge = st.sb("ge", [P, NG, E])
        gsum = st.sb("gsum", [P, NG])
        eid = st.sb("eid", [P, NG], I32)
        stats, mv = st.sb("stats", [P, TB, 6]), st.sb("mv", [P, TB, 2])
        veps, rstd, mhalf = st.sb("veps", [P, TB]), st.sb("rstd", [P, TB]), st.sb("mhalf", [P, TB])
        ps_t = st.ps("ps_t", [P, KC, S])
        ps_l = st.ps("ps_l", [P, TB, E])
        ps_in, ps_tot = st.ps("ps_in", [P, NT, E]), st.ps("ps_tot", [P, NT, E])
        s_x = [st.sem(f"x{u}") for u in range(2)]
        s_out = [st.sem(f"out{u}") for u in range(2)]
        s_zl = [st.sem(f"zl{u}") for u in range(2)]
        s_sc = [st.sem(f"sc{u}") for u in range(2)]
        names = "c xfree var rstd z t tc l ex exd oh cnt pos fin zero zd scf dve pool ident fout zero2 lc".split()
        (s_c, s_xfree, s_var, s_rstd, s_z, s_t, s_tc, s_l, s_ex, s_exd, s_oh, s_cnt, s_pos, s_fin, s_zero, s_zd, s_scf,
         s_dve, s_pool, s_ident, s_fout, s_zero2, s_lc) = (st.sem(n) for n in names)
        hi, ro, zo = batch_tiles(h_in), batch_tiles(res_d), batch_tiles(z_d)
        loads = [(Wr[:], w_router), (rank[:], A["c_rank"]), (upper[:], A["c_upper"]), (count[:], A["c_count"][:, 0:NG])]
        if moe:
            y_d, gamma, beta, bias = moe
            loads += [(gb[:, 0, :], gamma.partition_broadcast(P)), (gb[:, 1, :], beta.partition_broadcast(P)),
                      (rb[:], bias.partition_broadcast(P))]
            yi = batch_tiles(y_d)
        else:
            loads += [(gb[:, 0, :], switch[0].partition_broadcast(P))]
        nx = 2 if moe else 1
        norms = 1 if moe else 2
        with nc.Block() as block:

            @block.sync
            def _(sp):
                for to, src in loads:
                    sp.dma_start(to, src).then_inc(s_c, 16)
                with sp.Fori(0, B // 2) as i:
                    for u in range(2):
                        b = i * 2 + u
                        sp.wait_ge(s_xfree, b + 1)
                        sp.dma_start(x[:, u], hi[b]).then_inc(s_x[u], 16)
                        if moe:
                            sp.dma_start(y[:, u], yi[b]).then_inc(s_x[u], 16)
                sp.wait_ge(s_zero, 1)
                sp.dma_start(xs_d.rearrange("(g p) d -> p g d", p=P),
                             bcast(zeros[:].unsqueeze(1), [P, NG, D])).then_inc(s_zd, 16)
                with sp.Fori(0, B // 2) as i:
                    for u in range(2):
                        b = i * 2 + u
                        sp.wait_ge(s_scf, b + 1)
                        if u == 0:
                            sp.wait_ge(s_zero2, 1)
                        sp.dma_start(zl[:, u], zo[b]).then_inc(s_zl[u], 16)
                sp.wait_ge(s_fin, 1)
                sp.dma_start(eid_d[0:1, 0:NG], eid[0:1, :]).then_inc(s_fout, 16)
                sp.dma_start(tok_d, tok[:]).then_inc(s_fout, 16)
                sp.wait_ge(s_fout, 32)

            @block.gpsimd
            def _(pool):
                c = Chain(pool, s_pool)
                make_identity(pool, c, ident[:]).then_inc(s_ident, 1)
                c.link(pool.memset(mhalf[:], -0.5))
                with pool.Fori(0, B * norms) as i:
                    pool.wait_ge(s_var, i + 1)
                    pool.tensor_tensor(rstd[:], veps[:], mhalf[:], ALU.pow).then_inc(s_rstd, 1)
                c.close()
                pool.sem_inc(s_scf, 2)
                pool.wait_ge(s_pos, 1)
                pool.wait_ge(s_zd, 16)
                with pool.Fori(0, B // 2) as i:
                    for u in range(2):
                        b = i * 2 + u
                        c = Chain(pool, s_pool)
                        pool.wait_ge(s_zl[u], (i + 1) * 16)
                        c.link(pool.tensor_copy(row[:, u], pos[:, bass.ds(b * TB, TB)]))
                        for t in range(TB):
                            pool.indirect_dma_start(out=xs_d, out_offset=bass.IndirectOffsetOnAxis(ap=row[:, u, t:t + 1], axis=0),
                                                    in_=zl[:, u, t, :], in_offset=None).then_inc(s_sc[u], 16)
                        pool.wait_ge(s_sc[u], (i + 1) * 16 * TB)
                        pool.sem_inc(s_scf, 1)
                        c.close()

            @block.tensor
            def _(pe):
                pe.wait_ge(s_ident, 1)
                pe.wait_ge(s_c, 16 * len(loads))
                with pe.Fori(0, B // 2) as i:
                    for u in range(2):
                        b = i * 2 + u
                        pe.wait_ge(s_z, b + 1)
                        for k in range(KC):
                            for t in range(TB):
                                mm = pe.transpose(ps_t[0:KP, k, t * P:(t + 1) * P], z[:, u, t, k * KP:(k + 1) * KP], ident[:])
                        mm.then_inc(s_t, 1)
                        pe.wait_ge(s_tc, b + 1)
                        for t in range(TB):
                            for k in range(KC):
                                mm = pe.matmul(ps_l[:, t, :], zT[:, k, t * P:(t + 1) * P], Wr[:, k, :],
                                               start=(k == 0), stop=(k == KC - 1))
                        mm.then_inc(s_l, 1)
                pe.wait_ge(s_oh, 1)
                flat = oh[:].rearrange("p t e -> p (t e)")
                pe.matmul(ps_in[:].rearrange("p t e -> p (t e)"), upper[:], flat, start=True, stop=True)
                pe.matmul(ps_tot[:].rearrange("p t e -> p (t e)"), ones[:], flat, start=True, stop=True).then_inc(s_cnt, 1)

            @block.scalar
            def _(act):
                with act.Fori(0, B // 2) as i:
                    for u in range(2):
                        b = i * 2 + u
                        act.wait_ge(s_z, b + 1)
                        act.dma_start(zo[b], z[:, u]).then_inc(s_out[u], 16)
                        act.dma_start(ro[b], o[:, u]).then_inc(s_out[u], 16)
                for u in range(2):
                    act.wait_ge(s_out[u], B // 2 * 32)
                act.sem_inc(s_zero2, 1)
                act.wait_ge(s_ex, 1)
                act.activation(ex[:], ex[:], ACT.Exp).then_inc(s_exd, 1)

            @block.vector
            def _(dve):
                c = Chain(dve, s_dve)
                c.mark(dve.memset(ones[:], 1.0))
                c.link(dve.memset(zeros[:], 0.0))
                dve.sem_inc(s_zero, 1)
                dve.sem_inc(s_xfree, 2)
                dve.wait_ge(s_c, 16 * len(loads))
                c.close()
                full = [P, TB, D]
                with dve.Fori(0, B // 2) as i:
                    for u in range(2):
                        b = i * 2 + u
                        xb, yb, zb, ob = x[:, u], y[:, u], z[:, u], o[:, u]
                        c = Chain(dve, s_dve)
                        dve.wait_ge(s_x[u], (i + 1) * 16 * nx)
                        dve.wait_ge(s_out[u], i * 32)
                        if moe:
                            norm_stats(dve, c, yb, stats, mv, 1e-5, veps[:]).then_inc(s_var, 1)
                            c.mark(dve.tensor_tensor(ob, xb, yb, ALU.add))
                            dve.wait_ge(s_rstd, b + 1)
                            norm_apply(dve, c, zb, yb, mv, rstd)
                            c.wait()
                            c.link(dve.tensor_tensor(zb, zb, bcast(gb[:, 0:1, :], full), ALU.mult))
                            c.link(dve.tensor_tensor(zb, zb, bcast(gb[:, 1:2, :], full), ALU.add))
                        else:
                            norm_stats(dve, c, xb, stats, mv, 1e-5, veps[:]).then_inc(s_var, 1)
                            dve.wait_ge(s_rstd, 2 * b + 1)
                            norm_apply(dve, c, yb, xb, mv, rstd)
                            c.wait()
                            c.mark(dve.tensor_tensor(ob, xb, yb, ALU.add))
                            c.link(dve.tensor_tensor(sq[:], yb, yb, ALU.mult))
                            c.link(dve.tensor_reduce(veps[:], sq[:], AX.X, ALU.add))
                            dve.tensor_scalar(veps[:], veps[:], 1.0 / D, 1e-6, ALU.mult, ALU.add).then_inc(s_var, 1)
                            dve.wait_ge(s_rstd, 2 * b + 2)
                            for t in range(TB):
                                c.mark(dve.tensor_scalar(zb[:, t, :], yb[:, t, :], rstd[:, t:t + 1], None, ALU.mult))
                            c.wait()
                            c.link(dve.tensor_tensor(zb, zb, bcast(gb[:, 0:1, :], full), ALU.mult))
                        dve.sem_inc(s_z, 1)
                        dve.sem_inc(s_xfree, 1)
                        dve.wait_ge(s_t, b + 1)
                        dve.tensor_copy(zT[:], ps_t[0:KP]).then_inc(s_tc, 1)
                        dve.wait_ge(s_l, b + 1)
                        to = lg[:, bass.ds(b * TB, TB), :]
                        if moe:
                            c.link(dve.tensor_tensor(to, ps_l[:], bcast(rb[:].unsqueeze(1), [P, TB, E]), ALU.add))
                        else:
                            c.link(dve.tensor_copy(to, ps_l[:]))
                        c.close()
                c = Chain(dve, s_dve)

                def act_turn():
                    dve.sem_inc(s_ex, 1)
                    dve.wait_ge(s_exd, 1)

                top1(dve, act_turn, c, lg[:], (NT, E), m, oh, val, rank, best, ex, tok[:, 1, :])
                dve.sem_inc(s_oh, 1)
                dve.wait_ge(s_cnt, 1)
                c.mark(dve.tensor_copy(tot[:], ps_tot[:]))
                c.link(dve.tensor_copy(run[:], ps_tot[:]))
                src, dst, s = run, before, 1
                while s < NT:
                    c.mark(dve.tensor_tensor(dst[:, s:, :], src[:, s:, :], src[:, 0:NT - s, :], ALU.add))
                    c.link(dve.tensor_copy(dst[:, 0:s, :], src[:, 0:s, :]))
                    src, dst, s = dst, src, 2 * s
                c.link(dve.tensor_copy(ntile[:], src[:, NT - 1, :]))
                c.link(dve.tensor_tensor(dst[:], src[:], tot[:], ALU.subtract))
                bef = dst
                c.link(dve.tensor_scalar(ntile[:], ntile[:], 1.0 / P, 0.5 - 1.0 / (2 * P), ALU.mult, ALU.add))
                c.link(dve.tensor_scalar(ntile[:], ntile[:], ROUND, None, ALU.add))
                c.link(dve.tensor_scalar(ntile[:], ntile[:], ROUND, None, ALU.subtract))
                c.link(dve.tensor_copy(start[:], ntile[:]))
                a, d, s = start, swap, 1
                while s < E:
                    c.mark(dve.tensor_tensor(d[:, s:], a[:, s:], a[:, 0:E - s], ALU.add))
                    c.link(dve.tensor_copy(d[:, 0:s], a[:, 0:s]))
                    a, d, s = d, a, 2 * s
                c.link(dve.tensor_tensor(ge[:], bcast(a[:].unsqueeze(1), [P, NG, E]),
                                         bcast(count[:].unsqueeze(2), [P, NG, E]), ALU.is_le))
                c.link(dve.tensor_reduce(gsum[:], ge[:], AX.X, ALU.add))
                c.link(dve.tensor_scalar(gsum[:], gsum[:], float(E - 1), None, ALU.min))
                c.link(dve.tensor_copy(eid[:], gsum[:]))
                c.link(dve.tensor_tensor(d[:], a[:], ntile[:], ALU.subtract))
                c.link(dve.tensor_scalar(d[:], d[:], float(P), None, ALU.mult))
                c.link(dve.tensor_tensor(tot[:], bef[:], ps_in[:], ALU.add))
                c.link(dve.tensor_tensor(val[:], tot[:], bcast(d[:].unsqueeze(1), [P, NT, E]), ALU.add))
                c.link(dve.tensor_tensor(val[:], val[:], oh[:], ALU.mult))
                c.link(dve.tensor_reduce(tok[:, 0, :], val[:], AX.X, ALU.add))
                c.link(dve.tensor_copy(pos[:], tok[:, 0, :]))
                dve.sem_inc(s_pos, 1)
                if cap is None:
                    c.link(dve.memset(tok[:, 2, :], 1.0))
                else:
                    by_batch = [P, B, TB, E]
                    tb = tot[:].rearrange("p (b t) e -> p b t e", t=TB)
                    bb = bef[:].rearrange("p (b t) e -> p b t e", t=TB)
                    vb = val[:].rearrange("p (b t) e -> p b t e", t=TB)
                    c.link(dve.tensor_tensor(vb, tb, bcast(bb[:, :, 0:1, :], by_batch), ALU.subtract))
                    c.link(dve.tensor_tensor(val[:], val[:], oh[:], ALU.mult))
                    c.link(dve.tensor_reduce(m[:], val[:], AX.X, ALU.add))
                    c.link(dve.tensor_scalar(tok[:, 2, :], m[:], float(cap), None, ALU.is_lt))
                dve.sem_inc(s_fin, 1)
                c.close()


def gather_stage(nc, A, name, res_d, ys_d, tok_d, h_out, z_d=None):
    with ExitStack() as ctx:
        st = Stage(nc, ctx, name)
        x, ys, z, o = (st.sb(n, [P, 2, TB, D]) for n in ("x", "ys", "z", "o"))
        tok = st.sb("tok", [P, 3, NT])
        cut = st.sb("cut", [P, 2, NT])
        pos = st.sb("pos", [P, NT], I32)
        row = st.sb("row", [P, 2, TB], I32)
        fac = st.sb("fac", [P, 2, TB])
        s_x = [st.sem(f"x{u}") for u in range(2)]
        s_g = [st.sem(f"g{u}") for u in range(2)]
        s_out = [st.sem(f"out{u}") for u in range(2)]
        s_c, s_pos, s_free, s_o, s_dve, s_pool = (st.sem(n) for n in ("c", "pos", "free", "o", "dve", "pool"))
        ri, ho = batch_tiles(res_d), batch_tiles(h_out)
        zi = batch_tiles(z_d) if z_d is not None else None
        nx = 1 if z_d is None else 2
        with nc.Block() as block:

            @block.sync
            def _(sp):
                sp.dma_start(tok[:], tok_d).then_inc(s_c, 16)
                with sp.Fori(0, B // 2) as i:
                    for u in range(2):
                        b = i * 2 + u
                        sp.wait_ge(s_free, b + 1)
                        sp.dma_start(x[:, u], ri[b]).then_inc(s_x[u], 16)
                        if z_d is not None:
                            sp.dma_start(z[:, u], zi[b]).then_inc(s_x[u], 16)

            @block.gpsimd
            def _(pool):
                pool.wait_ge(s_pos, 1)
                with pool.Fori(0, B // 2) as i:
                    for u in range(2):
                        b = i * 2 + u
                        c = Chain(pool, s_pool)
                        pool.wait_ge(s_free, b + 1)
                        c.link(pool.tensor_copy(row[:, u], pos[:, bass.ds(b * TB, TB)]))
                        for t in range(TB):
                            pool.indirect_dma_start(out=ys[:, u, t, :], out_offset=None, in_=ys_d,
                                                    in_offset=bass.IndirectOffsetOnAxis(ap=row[:, u, t:t + 1], axis=0)
                                                    ).then_inc(s_g[u], 16)
                        c.close()

            @block.vector
            def _(dve):
                c = Chain(dve, s_dve)
                dve.wait_ge(s_c, 16)
                c.link(dve.tensor_copy(pos[:], tok[:, 0, :]))
                dve.sem_inc(s_pos, 1)
                dve.sem_inc(s_free, 2)
                c.link(dve.tensor_tensor(cut[:, 0, :], tok[:, 1, :], tok[:, 2, :], ALU.mult))
                c.link(dve.tensor_tensor(cut[:, 1, :], tok[:, 1, :], cut[:, 0, :], ALU.subtract))
                c.close()
                with dve.Fori(0, B // 2) as i:
                    for u in range(2):
                        b = i * 2 + u
                        c = Chain(dve, s_dve)
                        dve.wait_ge(s_x[u], (i + 1) * 16 * nx)
                        dve.wait_ge(s_g[u], (i + 1) * 16 * TB)
                        dve.wait_ge(s_out[u], i * 16)
                        if z_d is None:
                            c.link(dve.tensor_tensor(o[:, u], x[:, u], ys[:, u], ALU.add))
                        else:
                            c.link(dve.tensor_copy(fac[:], cut[:, :, bass.ds(b * TB, TB)]))
                            for t in range(TB):
                                c.mark(dve.scalar_tensor_tensor(x[:, u, t, :], ys[:, u, t, :], fac[:, 0, t:t + 1],
                                                                x[:, u, t, :], ALU.mult, ALU.add))
                            c.wait()
                            for t in range(TB):
                                c.mark(dve.scalar_tensor_tensor(o[:, u, t, :], z[:, u, t, :], fac[:, 1, t:t + 1],
                                                                x[:, u, t, :], ALU.mult, ALU.add))
                            c.wait()
                        dve.sem_inc(s_o, 1)
                        dve.sem_inc(s_free, 1)
                        c.close()

            @block.scalar
            def _(act):
                with act.Fori(0, B // 2) as i:
                    for u in range(2):
                        b = i * 2 + u
                        act.wait_ge(s_o, b + 1)
                        act.dma_start(ho[b], o[:, u]).then_inc(s_out[u], 16)
                for u in range(2):
                    act.wait_ge(s_out[u], B // 2 * 16)


def stage_l3_attention(nc, A, h_in, h_out):
    E = 8
    NG = NT + E
    y = nc.dram_tensor("d_l3_y", (T, D), F32).ap()
    res = nc.dram_tensor("d_l3_res", (T, D), F32).ap()
    z = nc.dram_tensor("d_l3_z", (T, D), F32).ap()
    xs = nc.dram_tensor("d_l3_xs", (NG * P, D), F32).ap()
    ys = nc.dram_tensor("d_l3_ys", (NG * P, D), F32).ap()
    eid = nc.dram_tensor("d_l3_eid", (1, NG), I32).ap()
    tok = nc.dram_tensor("d_l3_tok", (P, 3, NT), F32).ap()
    l3_token_attention_stage(nc, A, h_in, y)
    router_stage(nc, A, "l3r", E, h_in, res, z, xs, eid, tok, A["L3_attn_Wg"], NG,
                 moe=(y, A["L3_attn_ln2_g"], A["L3_attn_ln2_b"], A["L3_attn_bg"]))
    grouped_ffn_stage(nc, A, "l3m", xs, ys, eid, A["L3_attn_W1"], A["L3_attn_W2"], A["L3_attn_b1"], A["L3_attn_b2"],
                      ACT.Gelu, NG, 1)
    gather_stage(nc, A, "l3g", res, ys, tok, h_out)


def stage_l3_ffn(nc, A, h_in, h_out):
    E = 16
    NG = NT + E
    res = nc.dram_tensor("d_l4_res", (T, D), F32).ap()
    z = nc.dram_tensor("d_l4_z", (T, D), F32).ap()
    xs = nc.dram_tensor("d_l4_xs", (NG * P, D), F32).ap()
    ys = nc.dram_tensor("d_l4_ys", (NG * P, D), F32).ap()
    eid = nc.dram_tensor("d_l4_eid", (1, NG), I32).ap()
    tok = nc.dram_tensor("d_l4_tok", (P, 3, NT), F32).ap()
    router_stage(nc, A, "l4r", E, h_in, res, z, xs, eid, tok, A["L3_ffn_w_router"], NG, cap=64,
                 switch=(A["L3_ffn_ln_w"],))
    grouped_ffn_stage(nc, A, "l4m", xs, ys, eid, A["L3_ffn_wi"], A["L3_ffn_wo"], None, None, ACT.Relu, NG, 1)
    gather_stage(nc, A, "l4g", res, ys, tok, h_out, z)


def stage_l0_attention(nc, A, h_in, h_out):
    xT = nc.dram_tensor("d_l0a_xT", (B, KP, KC, S), F32).ap()
    wq = nc.dram_tensor("d_l0a_wqkv", (KP, KC, 2304), F32).ap()
    wo = nc.dram_tensor("d_l0a_wout", (P, 6, D), F32).ap()
    att = nc.dram_tensor("d_l0a_att", (T, 768), F32).ap()
    ternary_stage(nc, A, "l0t", [(A["L0_attn_w_qkv"].rearrange("p k n -> p (k n)"), wq.rearrange("p k n -> p (k n)")),
                                 (A["L0_attn_w_out"].rearrange("p k n -> p (k n)"), wo.rearrange("p k n -> p (k n)"))])
    attention_inputs_stage(nc, A, "l0i", h_in, xT, (A["L0_attn_gamma"], A["L0_attn_beta"]), A["L0_attn_sparsity"])
    attention_stage(nc, A, "l0a", xT, wq, att)
    attention_output_stage(nc, A, "l0o", att, wo, A["L0_attn_b_out"], h_in, h_out, A["L0_attn_sparsity"])


def stage_l2_attention(nc, A, h_in, h_out):
    xT = nc.dram_tensor("d_l2a_xT", (B, KP, KC, S), F32).ap()
    att = nc.dram_tensor("d_l2a_att", (T, 768), F32).ap()
    attention_inputs_stage(nc, A, "l2i", h_in, xT)
    attention_stage(nc, A, "l2a", xT, A["L2_attn_qkv_w"], att, A["L2_attn_qkv_b"])
    attention_output_stage(nc, A, "l2o", att, A["L2_attn_proj_w"], A["L2_attn_proj_b"], h_in, h_out)


STAGES = {7: stage_l3_attention, 8: stage_l3_ffn, 4: stage_l1_ffn, 6: stage_l2_ffn, 0: embedding_stage, 3: stage_l1_attention, 1: stage_l0_attention, 2: quant_linear_stage, 5: stage_l2_attention}


def build_tower(nc, A, out, first=0, last=8):
    h = A["h_start"] if first else None
    for n in range(first, last + 1):
        to = out if n == last else nc.dram_tensor(f"d_h{n}", (T, D), F32).ap()
        STAGES[n](nc, A, h, to)
        h = to


def shape_constants():
    row, col = np.arange(KP)[:, None], np.arange(6 * 64)[None, :]
    half = np.where(row // 16 == col // 64, -0.5, 0.0)
    row, col = np.arange(P)[:, None], np.arange(34)[None, :]
    kvmask = np.where(row // 64 == col // 17, 1 / 64, 0.0)
    rank = np.broadcast_to(16.0 - np.arange(16), (P, 16))
    upper = np.arange(P)[:, None] < np.arange(P)[None, :]
    count = np.broadcast_to(np.arange(NT + 16), (P, NT + 16))
    inv_freq = (1.0 / 10000.0 ** (np.arange(0, 16, 2, dtype=np.float32) / 16)).astype(np.float32)
    angle = np.arange(S, dtype=np.float32)[:, None] * inv_freq[None, :]
    angle = angle.reshape(TB, P, 8).transpose(1, 0, 2)
    return {"c_upper": upper.astype(np.float32), "c_count": count.astype(np.float32),
            "c_cos": np.cos(angle).astype(np.float32), "c_sin": np.sin(angle).astype(np.float32),
            "c_rank": rank.astype(np.float32), "c_half": half.astype(np.float32), "c_kvmask": kvmask.astype(np.float32)}


def declare_inputs(nc, inputs):
    def rows(p):
        return lambda a: a.reshape(-1, p, a.shape[-1]).transpose(1, 0, 2)

    layout = {
        "L0_attn_w_qkv": lambda a: rows(KP)(a.T), "L0_attn_w_out": lambda a: rows(P)(a.T),
        "L2_attn_qkv_w": lambda a: rows(KP)(a.T), "L2_attn_proj_w": lambda a: rows(P)(a.T),
        "L0_attn_sparsity": lambda a: a.reshape(1),
        "L0_ffn_weight_t": lambda a: a.view(np.int32),
        "L1_attn_W_qkv": rows(KP), "L1_attn_W_proj": rows(KP), "L1_attn_random_features": lambda a: a.T,
    }
    def expert_rows(p):
        return lambda a: a.reshape(a.shape[0], -1, p, a.shape[-1]).transpose(2, 0, 1, 3)

    def by_expert(p):
        return lambda a: a.reshape(a.shape[0], -1, p, a.shape[-1]).transpose(0, 2, 1, 3)

    def bias_rows(a):
        return a.reshape(a.shape[0], -1, P).transpose(0, 2, 1)

    layout.update({
        "L1_ffn_shared_gate": rows(KP), "L1_ffn_shared_up": rows(KP), "L1_ffn_shared_down": rows(P),
        "L1_ffn_routed_gate": expert_rows(KP), "L1_ffn_routed_up": expert_rows(KP),
        "L1_ffn_routed_down": expert_rows(P), "L1_ffn_router_w": rows(KP),
        "L2_ffn_Wg": lambda a: rows(KP)(a.T), "L2_ffn_W1": by_expert(KP), "L2_ffn_W2": by_expert(P),
        "L2_ffn_b1": bias_rows,
        "L3_attn_Wq": rows(KP), "L3_attn_Wk": rows(KP), "L3_attn_Wv": rows(KP), "L3_attn_Wg": rows(KP),
        "L3_attn_W1": by_expert(KP), "L3_attn_W2": by_expert(P), "L3_attn_b1": bias_rows,
        "L3_ffn_w_router": rows(KP), "L3_ffn_wi": by_expert(KP), "L3_ffn_wo": by_expert(P),
    })
    inputs = dict(inputs, **shape_constants())
    arrays, A = {}, {}
    for name, a in inputs.items():
        a = np.ascontiguousarray(layout.get(name, lambda a: a)(np.asarray(a)))
        arrays[f"in_{name}_dram"] = a
        A[name] = nc.dram_tensor(f"in_{name}_dram", a.shape, mybir.dt.from_np(a.dtype), kind="ExternalInput").ap()
    return arrays, A


def kernel(**inputs):
    import concourse.bacc as bacc
    from concourse.bass_utils import run_bass_kernel_spmd as run

    nc = bacc.Bacc("TRN2", target_bir_lowering=False, num_devices=1)
    arrays, A = declare_inputs(nc, inputs)
    out = nc.dram_tensor("out_0_dram", (T, D), F32, kind="ExternalOutput").ap()
    build_tower(nc, A, out)
    r = run(nc, [arrays], core_ids=[0])
    return r.results[0]["out_0_dram"].reshape(B, S, D)
```

```python
from contextlib import ExitStack

import numpy as np

import concourse.bass as bass
from concourse import mybir

F32 = mybir.dt.float32
F32R = mybir.dt.float32r
BF16 = mybir.dt.bfloat16
I32 = mybir.dt.int32
U32 = mybir.dt.uint32
I8 = mybir.dt.int8
ALU = mybir.AluOpType
ACT = mybir.ActivationFunctionType
AX = mybir.AxisListType

P = 128
B, S, D = 8, 512, 192
T = B * S
NT = T // P
TB = S // P
KC, KP = 2, D // 2
ROUND = 1.5 * 2 ** 23


class Chain:

    def __init__(self, eng, sem):
        self.eng, self.sem, self.n = eng, sem, 0

    def mark(self, ins):
        ins.then_inc(self.sem, 1)
        self.n += 1
        return self.n

    def wait(self, n=None):
        self.eng.wait_ge(self.sem, self.n if n is None else n)

    def close(self):
        self.wait()
        self.eng.sem_clear(self.sem)

    def link(self, ins):
        self.mark(ins)
        self.wait()


class Stage:

    def __init__(self, nc, ctx, name):
        self.nc, self.ctx, self.name, self.sems = nc, ctx, name, []
        ctx.callback(self.end)

    def sb(self, name, shape, dt=F32):
        return self.ctx.enter_context(self.nc.sbuf_tensor(f"{self.name}_{name}", shape, dt))

    def ps(self, name, shape, dt=F32):
        return self.ctx.enter_context(self.nc.psum_tensor(f"{self.name}_{name}", shape, dt))

    def sem(self, name):
        self.sems.append(self.nc.alloc_semaphore(f"{self.name}_{name}"))
        return self.sems[-1]

    def end(self):
        self.nc.clear_and_free_semaphores(self.sems)
        self.nc.all_engine_barrier()


def split(eng, c, hi, lo, x):
    c.link(eng.tensor_copy(hi, x))
    return eng.tensor_tensor(lo, x, hi.bitcast(F32), ALU.subtract)


def batch_tiles(h):
    return h.rearrange("(b t p) d -> b p t d", t=TB, p=P)


def bcast(ap, shape):
    return ap.broadcast_to(shape)


def make_identity(pool, chain, ident):
    chain.link(pool.memset(ident, 0.0))
    return pool.affine_select(out=ident, in_=ident, compare_op=ALU.not_equal, fill=1.0, base=0,
                              pattern=[[-1, ident.shape[1]]], channel_multiplier=1)


def norm_stats(dve, c, x, stats, mv, eps, veps):
    n = x.shape[1]
    for t in range(n):
        c.mark(dve.bn_stats(stats[:, t, :], x[:, t, :]))
    c.wait()
    for t in range(n):
        c.mark(dve.bn_aggr(mv[:, t, :], stats[:, t, :]))
    c.wait()
    return dve.tensor_scalar(veps, mv[:, :, 1], eps, None, ALU.add)


def norm_apply(dve, c, out, x, mv, rstd):
    for t in range(x.shape[1]):
        c.mark(dve.tensor_scalar(out[:, t, :], x[:, t, :], mv[:, t, 0:1], rstd[:, t:t + 1],
                                 ALU.subtract, ALU.mult))


def quant_linear_stage(nc, A, h_in, h_out):
    with ExitStack() as ctx:
        st = Stage(nc, ctx, "l0f")
        x = st.sb("x", [P, 2, TB, D])
        y = st.sb("y", [P, TB, D])
        q = st.sb("q", [P, TB, D], BF16)
        qT = st.sb("qT", [KP, KC, S], BF16)
        w8 = st.sb("w8", [KP, KC, D // 4], I32)
        w = st.sb("w", [KP, KC, D], BF16)
        bias = st.sb("bias", [P, D])
        o = st.sb("o", [P, 2, TB, D])
        ident = st.sb("ident", [P, P], BF16)
        stats = st.sb("stats", [P, TB, 6])
        mv = st.sb("mv", [P, TB, 2])
        veps = st.sb("veps", [P, TB])
        rstd = st.sb("rstd", [P, TB])
        mhalf = st.sb("mhalf", [P, TB])
        psT = st.ps("psT", [P, KC, 1024], BF16)
        psO = st.ps("psO", [P, TB, 512])
        s_x, s_out = [st.sem(f"x{u}") for u in range(2)], [st.sem(f"out{u}") for u in range(2)]
        s_w = st.sem("w")
        s_xfree, s_var, s_rstd, s_q, s_T, s_qT, s_y, s_o = (
            st.sem(n) for n in ("xfree", "var", "rstd", "q", "T", "qT", "y", "o"))
        s_ident, s_wb, s_dve, s_pool = st.sem("ident"), st.sem("wb"), st.sem("dve"), st.sem("pool")
        hi, ho = batch_tiles(h_in), batch_tiles(h_out)
        with nc.Block() as block:

            @block.sync
            def _(sp):
                sp.dma_start(w8[:], A["L0_ffn_weight_t"].rearrange("(c p) n -> p c n", p=KP)).then_inc(s_w, 16)
                sp.dma_start(bias[:], A["L0_ffn_bias"].partition_broadcast(P)).then_inc(s_w, 16)
                with sp.Fori(0, B // 2) as i:
                    for u in range(2):
                        b = i * 2 + u
                        sp.wait_ge(s_xfree, b + 1)
                        sp.dma_start(x[:, u], hi[b]).then_inc(s_x[u], 16)

            @block.gpsimd
            def _(pool):
                c = Chain(pool, s_pool)
                make_identity(pool, c, ident[:]).then_inc(s_ident, 1)
                c.link(pool.memset(mhalf[:], -0.5))
                with pool.Fori(0, B // 2) as i:
                    for u in range(2):
                        b = i * 2 + u
                        pool.wait_ge(s_var, b + 1)
                        pool.tensor_tensor(rstd[:], veps[:], mhalf[:], ALU.pow).then_inc(s_rstd, 1)

            @block.vector
            def _(dve):
                dve.sem_inc(s_xfree, 2)
                dve.wait_ge(s_w, 32)
                dve.tensor_copy(w[:], w8[:].bitcast(I8)).then_inc(s_wb, 1)
                with dve.Fori(0, B // 2) as i:
                    for u in range(2):
                        b = i * 2 + u
                        c = Chain(dve, s_dve)
                        xb, ob = x[:, u], o[:, u]
                        dve.wait_ge(s_x[u], (i + 1) * 16)
                        norm_stats(dve, c, xb, stats, mv, 1e-5, veps[:]).then_inc(s_var, 1)
                        dve.wait_ge(s_rstd, b + 1)
                        norm_apply(dve, c, y, xb, mv, rstd)
                        c.wait()
                        c.link(dve.tensor_scalar(y[:], y[:], 50.0, None, ALU.mult))
                        c.link(dve.tensor_scalar(y[:], y[:], ROUND, None, ALU.add))
                        c.link(dve.tensor_scalar(y[:], y[:], ROUND, -128.0, ALU.subtract, ALU.max))
                        dve.tensor_scalar(q[:], y[:], 127.0, None, ALU.min).then_inc(s_q, 1)
                        for k in range(KC):
                            dve.wait_ge(s_T, b * KC + k + 1)
                            dve.tensor_copy(qT[:, k, :], psT[0:KP, k, 0:S]).then_inc(s_qT, 1)
                        dve.wait_ge(s_y, b + 1)
                        dve.wait_ge(s_out[u], i * 16)
                        c.link(dve.tensor_scalar(ob, psO[:, :, 0:D], 0.02 * 0.01, None, ALU.mult))
                        c.link(dve.tensor_tensor(ob, ob, bcast(bias[:].unsqueeze(1), [P, TB, D]), ALU.add))
                        dve.tensor_tensor(ob, ob, xb, ALU.add).then_inc(s_o, 1)
                        dve.wait_ge(s_o, b + 1)
                        dve.sem_inc(s_xfree, 1)
                        c.close()

            @block.tensor
            def _(pe):
                pe.wait_ge(s_ident, 1)
                pe.wait_ge(s_wb, 1)
                with pe.Fori(0, B // 2) as i:
                    for u in range(2):
                        b = i * 2 + u
                        pe.wait_ge(s_q, b + 1)
                        for k in range(KC):
                            for t in range(TB):
                                m = pe.transpose(psT[0:KP, k, t * P:(t + 1) * P],
                                                 q[:, t, k * KP:(k + 1) * KP], ident[:])
                            m.then_inc(s_T, 1)
                        pe.wait_ge(s_qT, (b + 1) * KC)
                        for t in range(TB):
                            for k in range(KC):
                                m = pe.matmul(psO[:, t, 0:D], qT[:, k, t * P:(t + 1) * P], w[:, k, :],
                                              start=(k == 0), stop=(k == KC - 1))
                        m.then_inc(s_y, 1)

            @block.scalar
            def _(act):
                with act.Fori(0, B // 2) as i:
                    for u in range(2):
                        b = i * 2 + u
                        act.wait_ge(s_o, b + 1)
                        act.dma_start(ho[b], o[:, u]).then_inc(s_out[u], 16)
                for u in range(2):
                    act.wait_ge(s_out[u], B // 2 * 16)


SPLITS = 24


def move_up(pool, c, w, at, split):
    lo, wide, cnt, take = (w[k] for k in ("lo", "wide", "cnt", "take"))
    left, right = slice(at.start, split), slice(split, at.stop)
    c.link(pool.tensor_tensor(take[:, at], cnt[:, at], w["one"][:, at], ALU.mult))
    c.mark(pool.tensor_scalar(take[:, left], take[:, left], w["K"][:], None, ALU.is_ge))
    c.link(pool.tensor_scalar(take[:, right], take[:, right], w["nK"][:], None, ALU.is_le))
    c.link(pool.tensor_tensor(take[:, at], take[:, at], wide[:, at], ALU.mult))
    c.mark(pool.tensor_scalar(wide[:, at], wide[:, at], 0.5, None, ALU.mult))
    c.link(pool.tensor_tensor(lo[:, at], lo[:, at], take[:, at], ALU.add))
    c.link(pool.tensor_tensor(w["mid"][:, at], lo[:, at], wide[:, at], ALU.add))


def count_dve(dve, w, ax, t):
    return dve.tensor_scalar(w["junk"][:, t], ax[:, t, :], w["mid"][:, t:t + 1], None, ALU.is_ge, ALU.add,
                             accum_out=w["cnt"][:, t:t + 1])


def count_act(act, w, ax, t):
    return act.activation(w["junk"][:, t], ax[:, t, :], ACT.Sign, bias=w["mid"][:, t:t + 1], scale=-1.0,
                          accum_out=w["cnt"][:, t:t + 1])


def kept_count(dve, c, w, n):
    sp, r, g, K, nK = (w[k][:] for k in ("sp", "kr", "kg", "K", "nK"))
    c.link(dve.tensor_scalar(sp, sp, float(n - 1), None, ALU.mult))
    c.link(dve.tensor_scalar(r, sp, ROUND, None, ALU.add))
    c.link(dve.tensor_scalar(r, r, ROUND, None, ALU.subtract))
    c.link(dve.tensor_tensor(g, sp, r, ALU.is_gt))
    c.link(dve.tensor_tensor(r, r, g, ALU.add))
    c.mark(dve.tensor_scalar(K, r, -1.0, float(n), ALU.mult, ALU.add))
    c.link(dve.tensor_scalar(nK, r, 2.0, -float(n), ALU.mult, ALU.add))


def select_buffers(st, tiles, width):
    w = {"junk": st.sb("junk", [P, tiles, width], BF16)}
    for k in ("wide", "lo", "mid", "cnt", "take", "one"):
        w[k] = st.sb(k, [P, tiles])
    for k in ("sp", "kr", "kg", "K", "nK"):
        w[k] = st.sb(k, [P, 1])
    return w


def attention_inputs_stage(nc, A, name, h_in, xT_d):
    with ExitStack() as ctx:
        st = Stage(nc, ctx, name)
        x = st.sb("x", [P, 2, TB, D])
        y = st.sb("y", [P, TB, D])
        xT = st.sb("xT", [KP, KC, S])
        ident = st.sb("ident", [P, P])
        stats, mv = st.sb("stats", [P, TB, 6]), st.sb("mv", [P, TB, 2])
        veps, rstd, mhalf = st.sb("veps", [P, TB]), st.sb("rstd", [P, TB]), st.sb("mhalf", [P, TB])
        ps_t = st.ps("ps_t", [P, KC, S])
        s_x = [st.sem(f"x{u}") for u in range(2)]
        s_xfree, s_var, s_rstd, s_y, s_t, s_xT, s_out, s_ident, s_dve, s_pool = (
            st.sem(n) for n in ("xfree", "var", "rstd", "y", "t", "xT", "out", "ident", "dve", "pool"))
        hi = batch_tiles(h_in)
        with nc.Block() as block:

            @block.sync
            def _(sp):
                with sp.Fori(0, B // 2) as i:
                    for u in range(2):
                        sp.wait_ge(s_xfree, i * 2 + u + 1)
                        sp.dma_start(x[:, u], hi[i * 2 + u]).then_inc(s_x[u], 16)

            @block.gpsimd
            def _(pool):
                c = Chain(pool, s_pool)
                make_identity(pool, c, ident[:]).then_inc(s_ident, 1)
                c.link(pool.memset(mhalf[:], -0.5))
                with pool.Fori(0, B) as i:
                    pool.wait_ge(s_var, i + 1)
                    pool.tensor_tensor(rstd[:], veps[:], mhalf[:], ALU.pow).then_inc(s_rstd, 1)

            @block.vector
            def _(dve):
                dve.sem_inc(s_xfree, 2)
                with dve.Fori(0, B // 2) as i:
                    for u in range(2):
                        b = i * 2 + u
                        c = Chain(dve, s_dve)
                        dve.wait_ge(s_x[u], (i + 1) * 16)
                        norm_stats(dve, c, x[:, u], stats, mv, 1e-5, veps[:]).then_inc(s_var, 1)
                        dve.wait_ge(s_rstd, b + 1)
                        dve.wait_ge(s_t, b)
                        norm_apply(dve, c, y, x[:, u], mv, rstd)
                        c.wait()
                        dve.sem_inc(s_xfree, 1)
                        dve.sem_inc(s_y, 1)
                        dve.wait_ge(s_t, b + 1)
                        dve.wait_ge(s_out, b * 16)
                        dve.tensor_copy(xT[:], ps_t[0:KP, :, :]).then_inc(s_xT, 1)
                        c.close()

            @block.tensor
            def _(pe):
                pe.wait_ge(s_ident, 1)
                with pe.Fori(0, B) as b:
                    pe.wait_ge(s_y, b + 1)
                    pe.wait_ge(s_xT, b)
                    for k in range(KC):
                        for t in range(TB):
                            m = pe.transpose(ps_t[0:KP, k, t * P:(t + 1) * P], y[:, t, k * KP:(k + 1) * KP], ident[:])
                    m.then_inc(s_t, 1)

            @block.scalar
            def _(act):
                with act.Fori(0, B) as b:
                    act.wait_ge(s_xT, b + 1)
                    act.dma_start(xT_d[b], xT[:]).then_inc(s_out, 16)
                act.wait_ge(s_out, B * 16)


def sparse_inputs_stage(nc, A, name, h_in, xT_d, gamma, beta, sparsity):
    with ExitStack() as ctx:
        st = Stage(nc, ctx, name)
        y = st.sb("y", [P, NT, D])
        mag = st.sb("mag", [P, NT, D])
        xT = st.sb("xT", [KP, 2, KC, S])
        gb = st.sb("gb", [P, 2, D])
        ident = st.sb("ident", [P, P])
        stats, mv = st.sb("stats", [P, 2, TB, 6]), st.sb("mv", [P, 2, TB, 2])
        veps, rstd, mhalf = st.sb("veps", [P, 2, TB]), st.sb("rstd", [P, 2, TB]), st.sb("mhalf", [P, TB])
        w = select_buffers(st, NT, D)
        lo, wide = w["lo"], w["wide"]
        ps_t = st.ps("ps_t", [P, 2, KC, S])
        s_x = [st.sem(f"x{b}") for b in range(B)]
        s_out = [st.sem(f"out{u}") for u in range(2)]
        (s_c, s_var, s_rstd, s_mag, s_kept, s_mid, s_cd, s_ca, s_y, s_t, s_xT, s_ident, s_dve, s_pool,
         s_absd) = (st.sem(n) for n in ("c", "var", "rstd", "mag", "kept", "mid", "cd", "ca", "y", "t", "xT",
                                       "ident", "dve", "pool", "absd"))
        hi = batch_tiles(h_in)
        GROUP, SHARE = NT // 2, 9
        with nc.Block() as block:

            @block.sync
            def _(sp):
                for b in range(B):
                    sp.dma_start(y[:, b * TB:(b + 1) * TB], hi[b]).then_inc(s_x[b], 16)
                    if b == 0:
                        sp.dma_start(gb[:, 0, :], gamma.partition_broadcast(P)).then_inc(s_c, 16)
                        sp.dma_start(gb[:, 1, :], beta.partition_broadcast(P)).then_inc(s_c, 16)
                        sp.dma_start(w["sp"][:], sparsity.partition_broadcast(P)).then_inc(s_c, 16)

            @block.gpsimd
            def _(pool):
                c = Chain(pool, s_pool)
                make_identity(pool, c, ident[:]).then_inc(s_ident, 1)
                c.link(pool.memset(mhalf[:], -0.5))
                with pool.Fori(0, B) as i:
                    for norm in range(2):
                        pool.wait_ge(s_var, i * 2 + norm + 1)
                        pool.tensor_tensor(rstd[:, norm], veps[:, norm], mhalf[:], ALU.pow).then_inc(s_rstd, 1)
                c.mark(pool.memset(lo[:], 0.0))
                c.mark(pool.memset(w["one"][:], 1.0))
                pool.wait_ge(s_mag, 1)
                pool.wait_ge(s_kept, 1)
                c.wait()
                c.link(pool.tensor_tensor(w["mid"][:], lo[:], wide[:], ALU.add))
                c.close()
                pool.sem_inc(s_mid, 2)
                with pool.Fori(0, SPLITS) as i:
                    for g in range(2):
                        c = Chain(pool, s_pool)
                        pool.wait_ge(s_cd, i * 2 + g + 1)
                        pool.wait_ge(s_ca, i * 2 + g + 1)
                        move_up(pool, c, w, slice(g * GROUP, (g + 1) * GROUP), g * GROUP + SHARE)
                        c.close()
                        pool.sem_inc(s_mid, 1)

            @block.vector
            def _(dve):
                dve.wait_ge(s_c, 48)
                c = Chain(dve, s_dve)
                kept_count(dve, c, w, D)
                c.close()
                dve.sem_inc(s_kept, 1)


                def stats_of(b, norm):
                    x = y[:, b * TB:(b + 1) * TB]
                    c = Chain(dve, s_dve)
                    if norm == 0:
                        dve.wait_ge(s_x[b], 16)
                    norm_stats(dve, c, x, stats[:, norm], mv[:, norm], 1e-5, veps[:, norm]).then_inc(s_var, 1)
                    c.close()

                def apply_norm(b, norm, done):
                    x = y[:, b * TB:(b + 1) * TB]
                    c = Chain(dve, s_dve)
                    dve.wait_ge(s_rstd, done)
                    norm_apply(dve, c, x, x, mv[:, norm], rstd[:, norm])
                    if norm == 1:
                        c.wait()
                        c.link(dve.tensor_tensor(x, x, bcast(gb[:, 0:1, :], [P, TB, D]), ALU.mult))
                        c.link(dve.tensor_tensor(x, x, bcast(gb[:, 1:2, :], [P, TB, D]), ALU.add))
                        dve.tensor_reduce(wide[:, b * TB:(b + 1) * TB], x, AX.X, ALU.max,
                                          apply_absolute_value=True).then_inc(s_y, 1)
                    c.close()

                stats_of(0, 0)
                for b in range(B):
                    apply_norm(b, 0, 2 * b + 1)
                    stats_of(b, 1)
                    if b + 1 < B:
                        stats_of(b + 1, 0)
                    apply_norm(b, 1, 2 * b + 2)
                dve.wait_ge(s_y, B)
                dve.wait_ge(s_absd, B)
                dve.tensor_scalar(wide[:], wide[:], 0.5, None, ALU.mult).then_inc(s_mag, 1)
                with dve.Fori(0, SPLITS) as i:
                    for g in range(2):
                        dve.wait_ge(s_mid, i * 2 + g + 1)
                        for t in range(g * GROUP, g * GROUP + SHARE):
                            m = count_dve(dve, w, mag, t)
                        m.then_inc(s_cd, 1)
                dve.wait_ge(s_mid, 2 * SPLITS + 2)
                for t in range(NT):
                    dve.scalar_tensor_tensor(y[:, t, :], mag[:, t, :], lo[:, t:t + 1], y[:, t, :],
                                             ALU.is_ge, ALU.mult).then_inc(s_kept, 1)

            @block.tensor
            def _(pe):
                pe.wait_ge(s_ident, 1)
                for b in range(B):
                    pe.wait_ge(s_kept, (b + 1) * TB + 1)
                    if b >= 2:
                        pe.wait_ge(s_xT, b - 1)
                    for k in range(KC):
                        for t in range(TB):
                            m = pe.transpose(ps_t[0:KP, b % 2, k, t * P:(t + 1) * P],
                                             y[:, b * TB + t, k * KP:(k + 1) * KP], ident[:])
                    m.then_inc(s_t, 1)

            @block.scalar
            def _(act):
                act.wait_ge(s_ident, 1)
                act.activation(w["junk"][:, 0, 0:P], ident[:], ACT.Sign)
                for b in range(B):
                    act.wait_ge(s_y, b + 1)
                    act.activation(mag[:, b * TB:(b + 1) * TB], y[:, b * TB:(b + 1) * TB], ACT.Abs).then_inc(s_absd, 1)
                with act.Fori(0, SPLITS) as i:
                    for g in range(2):
                        act.wait_ge(s_mid, i * 2 + g + 1)
                        for t in range(g * GROUP + SHARE, (g + 1) * GROUP):
                            m = count_act(act, w, mag, t)
                        m.then_inc(s_ca, 1)
                for b in range(B):
                    act.wait_ge(s_t, b + 1)
                    if b >= 2:
                        act.wait_ge(s_out[b % 2], b // 2 * 16)
                    act.activation(xT[:, b % 2], ps_t[0:KP, b % 2], ACT.Copy).then_inc(s_xT, 1)
                    act.wait_ge(s_xT, b + 1)
                    act.dma_start(xT_d[b], xT[:, b % 2]).then_inc(s_out[b % 2], 16)
                for u in range(2):
                    act.wait_ge(s_out[u], B // 2 * 16)


def ternary_stage(nc, A, name, pairs):
    with ExitStack() as ctx:
        st = Stage(nc, ctx, name)
        s_w, s_p, s_sum, s_out, s_dve, s_ones = (st.sem(n) for n in ("w", "p", "sum", "out", "dve", "ones"))
        work = []
        for k, (src, dst) in enumerate(pairs):
            p, n = src.shape
            work.append((st.sb(f"w{k}", [p, n]), st.sb(f"part{k}", [p, 1]), st.sb(f"s{k}", [p, 2]),
                         st.ps(f"sum{k}", [p, 1]), p, n))
        ones = st.sb("ones", [P, P])
        with nc.Block() as block:

            @block.sync
            def _(sp):
                for k, (src, dst) in enumerate(pairs):
                    sp.dma_start(work[k][0][:], src).then_inc(s_w, 16)
                    sp.wait_ge(s_w, 16 * (k + 1))

            @block.vector
            def _(dve):
                c = Chain(dve, s_dve)
                dve.memset(ones[:], 1.0).then_inc(s_ones, 1)
                for k, (w, part, sc, total, p, n) in enumerate(work):
                    dve.wait_ge(s_w, 16 * (k + 1))
                    dve.tensor_reduce(part[:], w[:], AX.X, ALU.add, apply_absolute_value=True).then_inc(s_p, 1)
                    dve.wait_ge(s_sum, k + 1)
                    c.link(dve.tensor_scalar(sc[:, 0:1], total[:], 1.0 / (p * n), None, ALU.mult))
                    c.link(dve.tensor_scalar(sc[:, 1:2], sc[:, 0:1], 1e-8, None, ALU.add))
                    c.link(dve.reciprocal(sc[:, 1:2], sc[:, 1:2]))
                    c.link(dve.tensor_scalar(w[:], w[:], sc[:, 1:2], None, ALU.mult))
                    c.link(dve.tensor_scalar(w[:], w[:], ROUND, None, ALU.add))
                    c.link(dve.tensor_scalar(w[:], w[:], ROUND, -1.0, ALU.subtract, ALU.max))
                    c.link(dve.tensor_scalar(w[:], w[:], 1.0, sc[:, 0:1], ALU.min, ALU.mult))

            @block.tensor
            def _(pe):
                pe.wait_ge(s_ones, 1)
                for k, (w, part, sc, total, p, n) in enumerate(work):
                    pe.wait_ge(s_p, k + 1)
                    pe.matmul(total[:], ones[0:p, 0:p], part[:], start=True, stop=True).then_inc(s_sum, 1)

            @block.scalar
            def _(act):
                for k, (src, dst) in enumerate(pairs):
                    act.wait_ge(s_dve, 7 * (k + 1))
                    act.dma_start(dst, work[k][0][:]).then_inc(s_out, 16)
                act.wait_ge(s_out, 16 * len(pairs))


def attention_stage(nc, A, name, xT_d, w_d, att_d, qkv_bias=None, thr_d=None, sparsity=None):
    H, DH = 12, 64
    NPAIR, INNER = H // 2, H * DH
    G = 2 * TB
    STEPS = NPAIR * G
    COPIES = (3, 7) if sparsity is not None else ()
    FIRST = 3
    counts = [[] for s in range(STEPS)]
    if sparsity is not None:
        start = [FIRST + i * (STEPS - FIRST) // SPLITS for i in range(SPLITS + 1)]
        for i in range(SPLITS):
            counts[start[i]].append((i, 0))
            counts[start[i + 1] - 1].append((i, 1))
    with ExitStack() as ctx:
        st = Stage(nc, ctx, name)
        W = st.sb("W", [KP, KC, 3 * INNER])
        xT = st.sb("xT", [KP, 2, KC, S])
        qk = st.sb("qk", [P, 2, 2, S])
        v = st.sb("v", [P, 2, TB, P])
        prob = st.sb("prob", [P, 2, S])
        probT = st.sb("probT", [P, 2, S])
        o = st.sb("o", [P, 2, TB, INNER])
        nmax = st.sb("nmax", [P, 2])
        rsum = st.sb("rsum", [P, 2, TB, 2])
        rinv = st.sb("rinv", [P, TB])
        ident = st.sb("ident", [P, P])
        bqk = st.sb("bqk", [P, 2, NPAIR])
        bv = st.sb("bv", [P, INNER])
        ps_qv, ps_k = st.ps("ps_qv", [P, S]), st.ps("ps_k", [P, S])
        ps_s, ps_t = st.ps("ps_s", [P, 2, S]), st.ps("ps_t", [P, 2, S])
        ps_o = st.ps("ps_o", [P, 2, TB, P])
        s_w, s_bias, s_bq, s_ident, s_pool = (st.sem(n) for n in ("w", "bias", "bq", "ident", "pool"))
        s_q, s_k, s_qc, s_kc, s_v, s_vc = (st.sem(n) for n in ("q", "k", "qc", "kc", "v", "vc"))
        s_s, s_max, s_exp, s_t, s_tc, s_pv, s_o, s_dve = (
            st.sem(n) for n in ("s", "max", "exp", "t", "tc", "pv", "o", "dve"))
        s_x, s_out = [st.sem(f"x{u}") for u in range(2)], [st.sem(f"out{u}") for u in range(2)]
        if sparsity is not None:
            w = select_buffers(st, TB, INNER)
            ax = st.sb("ax", [P, 2, TB, INNER])
            thr = st.sb("thr", [P, 2, TB])
            pmax, smax = st.sb("pmax", [P, TB, NPAIR]), st.sb("smax", [P, 2, TB])
            s_sp, s_kept, s_smax, s_abs, s_sel, s_mid, s_cd, s_ca = (
                st.sem(n) for n in ("sp", "kept", "smax", "abs", "sel", "mid", "cd", "ca"))
            s_thr = [st.sem(f"thr{u}") for u in range(2)]
        s_tca = st.sem("tca")
        att = att_d.rearrange("b (t p) f -> b p t f", p=P)
        with nc.Block() as block:

            @block.sync
            def _(sp):

                def store(b, u):
                    sp.wait_ge(s_o, (b + 1) * NPAIR * 2 + 1)
                    sp.dma_start(att[b + 1], o[:, u]).then_inc(s_out[u], 16)

                def store_thresholds(b, u):
                    sp.wait_ge(s_sel, b + 2)
                    sp.dma_start(thr_d[b + 1], thr[:, u]).then_inc(s_thr[u], 16)

                sp.dma_start(W[:], w_d).then_inc(s_w, 16)
                if qkv_bias is not None:
                    sp.dma_start(bqk[:], qkv_bias[0:2 * INNER].rearrange("(a n p) -> p a n", a=2, p=P),
                                 allow_slow_non_contiguous=True).then_inc(s_bias, 16)
                    sp.dma_start(bv[:], qkv_bias[2 * INNER:].partition_broadcast(P)).then_inc(s_bias, 16)
                if sparsity is not None:
                    sp.dma_start(w["sp"][:], sparsity.partition_broadcast(P)).then_inc(s_sp, 16)
                for u in range(2):
                    sp.dma_start(xT[:, u], xT_d[u]).then_inc(s_x[u], 16)
                sp.wait_ge(s_ident, 2)
                with sp.Fori(0, B // 2) as i:
                    for u in range(2):
                        b = i * 2 + u
                        store(b - 1, 1 - u)
                        sp.wait_ge(s_v, (b + 1) * NPAIR)
                        sp.dma_start(xT[:, u], xT_d[(b + 2) % B]).then_inc(s_x[u], 16)
                        if sparsity is not None:
                            store_thresholds(b - 1, 1 - u)
                store(B - 1, 1)
                if sparsity is not None:
                    store_thresholds(B - 1, 1)
                    sp.wait_ge(s_thr[0], B // 2 * 16)
                    sp.wait_ge(s_thr[1], (B // 2 + 1) * 16)
                sp.wait_ge(s_out[0], B // 2 * 16)
                sp.wait_ge(s_out[1], (B // 2 + 1) * 16)
                for u in range(2):
                    sp.wait_ge(s_x[u], (B // 2 + 1) * 16)

            @block.gpsimd
            def _(pool):
                c = Chain(pool, s_pool)
                make_identity(pool, c, ident[:]).then_inc(s_ident, 1)
                pool.memset(o[:, 1], 0.0).then_inc(s_ident, 1)
                if sparsity is None:
                    return
                pool.memset(ax[:, 1], 0.0).then_inc(s_ident, 1)
                pool.memset(w["one"][:], 1.0).then_inc(s_ident, 1)
                pool.wait_ge(s_ident, 4)
                c.close()
                pool.wait_ge(s_kept, 1)

                def select(b, u):
                    lo, wide, mid = w["lo"], w["wide"], w["mid"]
                    c = Chain(pool, s_pool)
                    pool.wait_ge(s_abs, (b + 1) * NPAIR + 1)
                    pool.wait_ge(s_smax, b + 2)
                    c.link(pool.tensor_tensor(wide[:], smax[:, u], w["one"][:], ALU.mult))
                    c.mark(pool.tensor_scalar(wide[:], wide[:], 0.5, None, ALU.mult))
                    c.link(pool.memset(lo[:], 0.0))
                    c.link(pool.tensor_tensor(mid[:], lo[:], wide[:], ALU.add))
                    c.close()
                    pool.sem_inc(s_mid, 1)
                    with pool.Fori(0, SPLITS) as i:
                        c = Chain(pool, s_pool)
                        pool.wait_ge(s_cd, ((b + 1) * SPLITS + i + 1) * 2)
                        pool.wait_ge(s_ca, ((b + 1) * SPLITS + i + 1) * 2)
                        move_up(pool, c, w, slice(0, TB), TB // 2)
                        c.close()
                        pool.sem_inc(s_mid, 1)
                    c = Chain(pool, s_pool)
                    pool.wait_ge(s_thr[u], ((b + 1) // 2 if isinstance(b, int) else stored[0]) * 16)
                    c.link(pool.tensor_tensor(thr[:, u], lo[:], w["one"][:], ALU.mult))
                    c.close()
                    pool.sem_inc(s_sel, 1)

                stored = [None]
                with pool.Fori(0, B // 2) as i:
                    for u in range(2):
                        stored[0] = i
                        select(i * 2 + u - 1, 1 - u)
                select(B - 1, 1)

            @block.tensor
            def _(pe):

                def project(j, n, g, x):
                    if g < 4:
                        a, k = g // 2, g % 2
                        if g == 0:
                            pe.wait_ge(s_vc, j)
                        m = pe.matmul((ps_qv, ps_k)[a][:], W[:, k, a * INNER + n * P:a * INNER + (n + 1) * P],
                                      x[:, k, :], start=(k == 0), stop=(k == KC - 1))
                        if k == KC - 1:
                            m.then_inc((s_q, s_k)[a], 1)
                    elif g < 6:
                        if g == 4:
                            pe.wait_ge(s_qc, j + 1)
                        for t in range((g - 4) * TB // 2, (g - 3) * TB // 2):
                            for k in range(KC):
                                m = pe.matmul(ps_qv[:, t * P:(t + 1) * P], x[:, k, t * P:(t + 1) * P],
                                              W[:, k, 2 * INNER + n * P:2 * INNER + (n + 1) * P],
                                              start=(k == 0), stop=(k == KC - 1))
                        if g == 5:
                            m.then_inc(s_v, 1)

                own = [g for g in range(G) if g not in COPIES]

                def score(n, g):
                    rows, q = slice(g // TB * DH, (g // TB + 1) * DH), g % TB
                    pe.matmul(ps_s[:, g % 2], qk[rows, n % 2, 0, q * P:(q + 1) * P], qk[rows, n % 2, 1, :],
                              start=True, stop=True).then_inc(s_s, 1)

                pe.wait_ge(s_w, 16)
                pe.wait_ge(s_ident, 2)
                pe.wait_ge(s_x[0], 16)
                for g in range(6):
                    project(0, 0, g, xT[:, 0])
                pe.wait_ge(s_kc, 1)
                score(0, 0)
                score(0, 1)
                with pe.Fori(0, B // 2) as i:
                    for u in range(2):
                        b = i * 2 + u
                        for n in range(NPAIR):
                            j = b * NPAIR + n
                            for g in range(G):
                                step = j * G + g
                                pe.wait_ge(s_exp, step + 1)
                                for k in range(TB):
                                    m = pe.transpose(ps_t[:, g % 2, k * P:(k + 1) * P],
                                                     prob[:, g % 2, k * P:(k + 1) * P], ident[:])
                                m.then_inc(s_t, 1)
                                if g == G - 2:
                                    pe.wait_ge(s_kc, j + 2)
                                score((n if g + 2 < G else n + 1) % NPAIR, (g + 2) % G)
                                if n == NPAIR - 1 and g == 0:
                                    pe.wait_ge(s_x[1 - u], (i + 1 + u) * 16)
                                project(j + 1, (n + 1) % NPAIR, g, xT[:, u if n + 1 < NPAIR else 1 - u])
                                if g in COPIES:
                                    pe.wait_ge(s_tca, j * len(COPIES) + COPIES.index(g) + 1)
                                else:
                                    pe.wait_ge(s_tc, j * (G - len(COPIES)) + own.index(g) + 1)
                                if g == 0:
                                    pe.wait_ge(s_vc, j + 1)
                                if g % TB == 0:
                                    pe.wait_ge(s_o, j * 2 + g // TB)
                                for k in range(TB):
                                    m = pe.matmul(ps_o[:, g // TB, g % TB, :], probT[:, g % 2, k * P:(k + 1) * P],
                                                  v[:, n % 2, k, :], start=(k == 0), stop=(k == TB - 1))
                                m.then_inc(s_pv, 1)

            @block.scalar
            def _(act):

                def copy_q(j, n):
                    act.wait_ge(s_q, j + 1)
                    if qkv_bias is None:
                        m = act.activation(qk[:, n % 2, 0, :], ps_qv[:], ACT.Copy, scale=DH ** -0.5)
                    else:
                        m = act.activation(qk[:, n % 2, 0, :], ps_qv[:], ACT.Identity, scale=DH ** -0.5,
                                           bias=bqk[:, 0, n:n + 1])
                    m.then_inc(s_qc, 1)

                def copy_k(j, n):
                    act.wait_ge(s_k, j + 1)
                    if qkv_bias is None:
                        m = act.activation(qk[:, n % 2, 1, :], ps_k[:], ACT.Copy)
                    else:
                        m = act.activation(qk[:, n % 2, 1, :], ps_k[:], ACT.Identity, bias=bqk[:, 1, n:n + 1])
                    m.then_inc(s_kc, 1)

                def copy_v(j, n):
                    act.wait_ge(s_v, j + 1)
                    act.activation(v[:, n % 2].rearrange("p t f -> p (t f)"), ps_qv[:], ACT.Copy).then_inc(s_vc, 1)

                def exponentials(step, n, g):
                    act.wait_ge(s_max, step + 1)
                    act.activation(prob[:, g % 2], ps_s[:, g % 2], ACT.Exp, bias=nmax[:, g % 2:g % 2 + 1],
                                   accum_out=rsum[:, n % 2, g % TB, g // TB:g // TB + 1]).then_inc(s_exp, 1)

                def count(sel, u, halving, k):
                    act.wait_ge(s_mid, sel * (SPLITS + 1) + halving + 1)
                    count_act(act, w, ax[:, u], 2 + k).then_inc(s_ca, 1)

                def magnitudes(j, n, u):
                    act.wait_ge(s_o, j * 2 + 3)
                    act.activation(ax[:, u, :, n * P:(n + 1) * P], o[:, u, :, n * P:(n + 1) * P],
                                   ACT.Abs).then_inc(s_abs, 1)

                if sparsity is not None:
                    act.wait_ge(s_ident, 3)
                    act.activation(w["junk"][:, 2, 0:P], ident[:], ACT.Sign)
                if qkv_bias is not None:
                    act.wait_ge(s_bq, 1)
                copy_q(0, 0)
                copy_k(0, 0)
                if sparsity is not None:
                    copy_v(0, 0)
                exponentials(0, 0, 0)
                with act.Fori(0, B // 2) as i:
                    for u in range(2):
                        b = i * 2 + u
                        for n in range(NPAIR):
                            j = b * NPAIR + n
                            for g in range(G):
                                step = j * G + g
                                if g == G - 1:
                                    act.wait_ge(s_o, j * 2 + 1)
                                act.wait_ge(s_t, step)
                                exponentials(step + 1, (n if g + 1 < G else n + 1), (g + 1) % G)
                                if g == 2:
                                    copy_q(j + 1, (n + 1) % NPAIR)
                                if g == 4:
                                    copy_k(j + 1, (n + 1) % NPAIR)
                                if g in COPIES:
                                    act.wait_ge(s_t, step + 1)
                                    act.activation(probT[:, g % 2], ps_t[:, g % 2], ACT.Copy).then_inc(s_tca, 1)
                                if g == 1 and sparsity is not None:
                                    magnitudes(j - 1, (n - 1) % NPAIR, u if n else 1 - u)
                                if g == 6 and sparsity is not None:
                                    copy_v(j + 1, (n + 1) % NPAIR)
                                for halving, k in counts[n * G + g]:
                                    count(b, 1 - u, halving, k)
                if sparsity is not None:
                    magnitudes(B * NPAIR - 1, NPAIR - 1, 1)
                    with act.Fori(0, SPLITS) as i:
                        act.wait_ge(s_mid, i + (B * (SPLITS + 1) + 1))
                        for t in (2, 3):
                            count_act(act, w, ax[:, 1], t).then_inc(s_ca, 1)

            @block.vector
            def _(dve):

                def maximum(step, g):
                    dve.wait_ge(s_s, step + 1)
                    dve.tensor_reduce(nmax[:, g % 2:g % 2 + 1], ps_s[:, g % 2], AX.X, ALU.max,
                                      negate=True).then_inc(s_max, 1)

                def copy_v(j, n):
                    dve.wait_ge(s_v, j + 1)
                    if qkv_bias is None:
                        dve.tensor_copy(v[:, n % 2].rearrange("p t f -> p (t f)"), ps_qv[:]).then_inc(s_vc, 1)
                    else:
                        dve.tensor_tensor(v[:, n % 2], ps_qv[:].rearrange("p (t f) -> p t f", t=TB),
                                          bcast(bv[:, n * P:(n + 1) * P].unsqueeze(1), [P, TB, P]),
                                          ALU.add).then_inc(s_vc, 1)

                def normalise(j, n, head, u, stored):
                    c = Chain(dve, s_dve)
                    dve.wait_ge(s_pv, j * G + (head + 1) * TB)
                    c.link(dve.reciprocal(rinv[:], rsum[:, n % 2, :, head]))
                    if n == 0 and head == 0:
                        dve.wait_ge(s_out[u], stored * 16)
                    c.link(dve.tensor_tensor(o[:, u, :, n * P + head * DH:n * P + (head + 1) * DH],
                                             ps_o[:, head, :, head * DH:(head + 1) * DH],
                                             bcast(rinv[:].unsqueeze(2), [P, TB, DH]), ALU.mult))
                    dve.sem_inc(s_o, 1)
                    c.close()

                def largest(n, u):
                    c = Chain(dve, s_dve)
                    c.mark(dve.tensor_reduce(pmax[:, :, n], o[:, u, :, n * P:(n + 1) * P], AX.X, ALU.max,
                                             apply_absolute_value=True))
                    if n == NPAIR - 1:
                        c.wait()
                        c.link(dve.tensor_reduce(smax[:, u], pmax[:], AX.X, ALU.max))
                        dve.sem_inc(s_smax, 1)
                    c.close()

                def count(sel, u, halving, k):
                    dve.wait_ge(s_mid, sel * (SPLITS + 1) + halving + 1)
                    count_dve(dve, w, ax[:, u], k).then_inc(s_cd, 1)

                if qkv_bias is not None:
                    dve.wait_ge(s_bias, 32)
                    dve.tensor_scalar(bqk[:, 0, :], bqk[:, 0, :], DH ** -0.5, None, ALU.mult).then_inc(s_bq, 1)
                if sparsity is not None:
                    dve.wait_ge(s_sp, 16)
                    c = Chain(dve, s_dve)
                    kept_count(dve, c, w, INNER)
                    c.close()
                    dve.sem_inc(s_kept, 1)
                dve.memset(ps_o[:, 1], 0.0)
                dve.memset(rsum[:, 1], 1.0)
                if sparsity is not None:
                    dve.memset(pmax[:], 1.0)
                dve.wait_ge(s_ident, 2)
                maximum(0, 0)
                if sparsity is None:
                    copy_v(0, 0)
                with dve.Fori(0, B // 2) as i:
                    for u in range(2):
                        b = i * 2 + u
                        for n in range(NPAIR):
                            j = b * NPAIR + n
                            for g in range(G):
                                step = j * G + g
                                dve.wait_ge(s_exp, step)
                                maximum(step + 1, (g + 1) % G)
                                if g not in COPIES:
                                    dve.wait_ge(s_t, step + 1)
                                    dve.tensor_copy(probT[:, g % 2], ps_t[:, g % 2]).then_inc(s_tc, 1)
                                if g == 6 and sparsity is None:
                                    copy_v(j + 1, (n + 1) % NPAIR)
                                before = (n - 1) % NPAIR
                                if g == 0:
                                    normalise(j - 1, before, 1, u if n else 1 - u, 0)
                                if g == TB:
                                    normalise(j, n, 0, u, i + u)
                                if g == 1 and sparsity is not None:
                                    largest(before, u if n else 1 - u)
                                for halving, k in counts[n * G + g]:
                                    count(b, 1 - u, halving, k)
                normalise(B * NPAIR - 1, NPAIR - 1, 1, 1, 0)
                if sparsity is not None:
                    largest(NPAIR - 1, 1)
                    with dve.Fori(0, SPLITS) as i:
                        dve.wait_ge(s_mid, i + (B * (SPLITS + 1) + 1))
                        for t in range(2):
                            count_dve(dve, w, ax[:, 1], t).then_inc(s_cd, 1)


def attention_output_stage(nc, A, name, att_d, w_d, bias, h_in, h_out, thr_d=None):
    INNER = att_d.shape[2]
    C = INNER // P
    with ExitStack() as ctx:
        st = Stage(nc, ctx, name)
        a = st.sb("a", [P, 2, TB, INNER])
        hx = st.sb("hx", [P, 2, TB, D])
        W = st.sb("W", [P, C, D])
        bo = st.sb("bo", [P, D])
        aT = st.sb("aT", [P, 2, C * P])
        o = st.sb("o", [P, 2, TB, D])
        ident = st.sb("ident", [P, P])
        ax = st.sb("ax", [P, 2, TB, INNER])
        thr = st.sb("thr", [P, 2, TB])
        s_abs, s_cut = st.sem("abs"), st.sem("cut")
        LOADS = 48 if thr_d is not None else 32
        ps_t = st.ps("ps_t", [P, 2, 2, S])
        ps_o = st.ps("ps_o", [P, TB, S])
        s_a = [st.sem(f"a{u}") for u in range(2)]
        s_out = [st.sem(f"out{u}") for u in range(2)]
        s_w, s_afree, s_t, s_tc, s_y, s_o, s_ident, s_dve, s_pool = (
            st.sem(n) for n in ("w", "afree", "t", "tc", "y", "o", "ident", "dve", "pool"))
        ai = att_d.rearrange("b (t p) f -> b p t f", p=P)
        hi, ho = batch_tiles(h_in), batch_tiles(h_out)
        HC = C * P // 2
        with nc.Block() as block:

            @block.sync
            def _(sp):
                sp.dma_start(W[:], w_d).then_inc(s_w, 16)
                sp.dma_start(bo[:], bias.partition_broadcast(P)).then_inc(s_w, 16)

                def load(b, u):
                    sp.dma_start(a[:, u], ai[b % B + 1]).then_inc(s_a[u], 16)
                    sp.dma_start(hx[:, u], hi[b % B]).then_inc(s_a[u], 16)
                    if thr_d is not None:
                        sp.dma_start(thr[:, u], thr_d[b % B + 1]).then_inc(s_a[u], 16)

                load(0, 0)
                load(1, 1)
                with sp.Fori(0, B // 2) as i:
                    for u in range(2):
                        sp.wait_ge(s_afree, i * 2 + u + 1)
                        load(i * 2 + u + 2, u)
                for u in range(2):
                    sp.wait_ge(s_a[u], (B // 2 + 1) * LOADS)

            @block.gpsimd
            def _(pool):
                c = Chain(pool, s_pool)
                make_identity(pool, c, ident[:]).then_inc(s_ident, 1)

            @block.vector
            def _(dve):
                dve.wait_ge(s_w, 32)

                def cut(k, u):
                    dve.wait_ge(s_abs, k + 1)
                    for t in range(TB):
                        m = dve.scalar_tensor_tensor(a[:, u, t, :], ax[:, u, t, :], thr[:, u, t:t + 1], a[:, u, t, :],
                                                     ALU.is_ge, ALU.mult)
                        m.then_inc(s_cut, 1)

                if thr_d is not None:
                    cut(0, 0)
                with dve.Fori(0, B // 2) as i:
                    for u in range(2):
                        b = i * 2 + u
                        c = Chain(dve, s_dve)
                        dve.wait_ge(s_a[u], (i + 1) * LOADS)
                        for t in range(TB):
                            dve.wait_ge(s_t, b * TB + t + 1)
                            dve.tensor_copy(aT[:, t % 2].rearrange("p (a f) -> p a f", a=2),
                                            ps_t[:, t % 2, :, 0:HC]).then_inc(s_tc, 1)
                        if thr_d is not None:
                            cut(b + 1, 1 - u)
                        c.mark(dve.tensor_tensor(hx[:, u], hx[:, u], bcast(bo[:].unsqueeze(1), [P, TB, D]), ALU.add))
                        c.wait()
                        dve.wait_ge(s_y, b + 1)
                        dve.wait_ge(s_out[u], i * 16)
                        dve.tensor_tensor(o[:, u], ps_o[:, :, 0:D], hx[:, u], ALU.add).then_inc(s_o, 1)
                        dve.wait_ge(s_o, b + 1)
                        dve.sem_inc(s_afree, 1)
                        c.close()

            @block.tensor
            def _(pe):
                pe.wait_ge(s_ident, 1)
                pe.wait_ge(s_w, 32)
                with pe.Fori(0, B // 2) as i:
                    for u in range(2):
                        b = i * 2 + u
                        if thr_d is None:
                            pe.wait_ge(s_a[u], (i + 1) * LOADS)
                        else:
                            pe.wait_ge(s_cut, (b + 1) * TB)

                        def turn(t):
                            for k in range(C):
                                m = pe.transpose(ps_t[:, t % 2, k * P // HC, k * P % HC:k * P % HC + P],
                                                 a[:, u, t, k * P:(k + 1) * P], ident[:])
                            m.then_inc(s_t, 1)

                        turn(0)
                        for t in range(TB):
                            if t + 1 < TB:
                                turn(t + 1)
                            pe.wait_ge(s_tc, b * TB + t + 1)
                            if t == 0:
                                pe.wait_ge(s_o, b)
                            for k in range(C):
                                m = pe.matmul(ps_o[:, t, 0:D], aT[:, t % 2, k * P:(k + 1) * P], W[:, k, :],
                                              start=(k == 0), stop=(k == C - 1))
                        m.then_inc(s_y, 1)

            @block.scalar
            def _(act):

                def magnitudes(u, loads):
                    act.wait_ge(s_a[u], loads * LOADS)
                    act.activation(ax[:, u], a[:, u], ACT.Abs).then_inc(s_abs, 1)

                if thr_d is not None:
                    magnitudes(0, 1)
                with act.Fori(0, B // 2) as i:
                    for u in range(2):
                        b = i * 2 + u
                        if thr_d is not None:
                            magnitudes(1 - u, i + 1 + u)
                        act.wait_ge(s_o, b + 1)
                        act.dma_start(ho[b], o[:, u]).then_inc(s_out[u], 16)
                for u in range(2):
                    act.wait_ge(s_out[u], B // 2 * 16)


def embedding_stage(nc, A, h_in, h_out):
    V_WORD, V_MODAL, V_SEG, V_NPI, V_POS = 8000, 16, 4, 2500, 512
    WORD, NPI, POS, SEG, MODAL = range(5)
    IDS = [("x", V_WORD), ("itok_BS_0_9999", V_NPI), ("itok_BS_0_2047", V_POS), ("itok_BS_0_3", V_SEG),
           ("itok_BS_0_15", V_MODAL)]
    TWO_PI_HI = 6.28125
    TWO_PI_LO = 2 * np.pi - TWO_PI_HI
    PI = float(np.float32(np.pi)) * (1 - 2.0 ** -23)
    combined = nc.dram_tensor("d_seg_modal", (V_SEG * V_MODAL, D), F32).ap()
    tables = [A["L0_tok_word_table"], A["L0_tok_npi_table"], A["L0_tok_posi_table"], combined]
    NG = NT // TB
    with ExitStack() as ctx:
        st = Stage(nc, ctx, "emb")
        ids = st.sb("ids", [P, 5, NT], I32)
        idf = st.sb("idf", [P, 5, NT])
        neg = st.sb("neg", [P, 5, NT])
        rows = st.sb("rows", [P, 4, NT], I32)
        row = st.sb("row", [P, 2, 4, TB], I32)
        tau = st.sb("tau", [P, 2, NT])
        tg = st.sb("tg", [P, 2, TB])
        wb = st.sb("wb", [P, 2, 2, D])
        seg = st.sb("seg", [V_SEG * V_MODAL, D])
        modal = st.sb("modal", [V_SEG * V_MODAL, D])
        g = st.sb("g", [P, 2, 4, TB, D])
        arg = st.sb("arg", [P, TB, 2, D])
        turns = st.sb("turns", [P, TB, 2, D])
        wave = st.sb("wave", [P, TB, 2, D])
        e = st.sb("e", [P, TB, D])
        o = st.sb("o", [P, 2, TB, D])
        gb = st.sb("gb", [P, 2, D])
        stats, mv = st.sb("stats", [P, TB, 6]), st.sb("mv", [P, TB, 2])
        veps, rstd, mhalf = st.sb("veps", [P, TB]), st.sb("rstd", [P, TB]), st.sb("mhalf", [P, TB])
        s_g = [st.sem(f"g{u}") for u in range(2)]
        s_out = [st.sem(f"out{u}") for u in range(2)]
        s_c, s_cmb, s_cst, s_rows, s_gfree, s_arg, s_turns, s_red, s_wave, s_var, s_rstd, s_o, s_dve, s_pool, s_act = (
            st.sem(n) for n in ("c", "cmb", "cst", "rows", "gfree", "arg", "turns", "red", "wave", "var", "rstd", "o",
                                "dve", "pool", "act"))
        ho = h_out.rearrange("(p g t) d -> g p t d", p=P, t=TB)
        with nc.Block() as block:

            @block.sync
            def _(sp):
                for k, (name, _) in enumerate(IDS):
                    sp.dma_start(ids[:, k, :], A[name].rearrange("b (q t) -> (b q) t", t=NT)).then_inc(s_c, 16)
                for k, (tau_name, part) in enumerate((("fside_BS_age_tau", "age"), ("fside_BS_delays_tau", "delay"))):
                    sp.dma_start(tau[:, k, :], A[tau_name].rearrange("b (q t) -> (b q) t", t=NT)).then_inc(s_c, 16)
                    for a, name in enumerate(("w", "b")):
                        v = A[f"L0_tok_{part}_{name}"]
                        v0 = A[f"L0_tok_{part}_{name}0"]
                        v = v[0] if a == 0 else v
                        v0 = v0[0] if a == 0 else v0
                        sp.dma_start(wb[:, k, a, 0:D - 1], v.partition_broadcast(P)).then_inc(s_c, 16)
                        sp.dma_start(wb[:, k, a, D - 1:D], v0.partition_broadcast(P)).then_inc(s_c, 16)
                sp.dma_start(gb[:, 0, :], A["L0_tok_ln_gamma"].partition_broadcast(P)).then_inc(s_c, 16)
                sp.dma_start(gb[:, 1, :], A["L0_tok_ln_beta"].partition_broadcast(P)).then_inc(s_c, 16)
                for k in range(V_SEG):
                    sp.dma_start(seg[k * V_MODAL:(k + 1) * V_MODAL, :],
                                 A["L0_tok_seg_table"][k].partition_broadcast(V_MODAL)).then_inc(s_c, 16)
                    sp.dma_start(modal[k * V_MODAL:(k + 1) * V_MODAL, :],
                                 A["L0_tok_modalities_table"]).then_inc(s_c, 16)
                sp.wait_ge(s_cmb, 1)
                sp.dma_start(combined, seg[:]).then_inc(s_cst, 16)

            @block.gpsimd
            def _(pool):
                c = Chain(pool, s_pool)
                c.link(pool.memset(mhalf[:], -0.5))
                c.close()
                pool.wait_ge(s_rows, 1)
                pool.wait_ge(s_cst, 16)

                def gather(i, u):
                    c = Chain(pool, s_pool)
                    pool.wait_ge(s_gfree, i * 2 + u + 1)
                    c.link(pool.tensor_copy(row[:, u], rows[:, :, bass.ds((i * 2 + u) * TB, TB)]))
                    for k in range(4):
                        for t in range(TB):
                            pool.indirect_dma_start(
                                out=g[:, u, k, t, :], out_offset=None, in_=tables[k],
                                in_offset=bass.IndirectOffsetOnAxis(ap=row[:, u, k, t:t + 1], axis=0)).then_inc(s_g[u], 16)
                    c.close()

                gather(0, 0)
                with pool.Fori(0, NG // 2) as i:
                    for u in range(2):
                        if u == 0:
                            gather(i, 1)
                        else:
                            c = Chain(pool, s_pool)
                            pool.wait_ge(s_gfree, i * 2 + 3)
                            c.link(pool.tensor_copy(row[:, 0], rows[:, :, bass.ds((i * 2 + 2) % NG * TB, TB)]))
                            for k in range(4):
                                for t in range(TB):
                                    pool.indirect_dma_start(
                                        out=g[:, 0, k, t, :], out_offset=None, in_=tables[k],
                                        in_offset=bass.IndirectOffsetOnAxis(ap=row[:, 0, k, t:t + 1],
                                                                            axis=0)).then_inc(s_g[0], 16)
                            c.close()
                        pool.wait_ge(s_var, i * 2 + u + 1)
                        pool.tensor_tensor(rstd[:], veps[:], mhalf[:], ALU.pow).then_inc(s_rstd, 1)
                pool.wait_ge(s_g[0], (NG // 2 + 1) * 4 * TB * 16)

            @block.scalar
            def _(act):
                with act.Fori(0, NG // 2) as i:
                    for u in range(2):
                        n = i * 2 + u
                        c = Chain(act, s_act)
                        act.wait_ge(s_arg, n + 1)
                        c.link(act.activation(turns[:], arg[:], ACT.Copy, scale=float(1 / (2 * np.pi)), bias=ROUND))
                        act.activation(turns[:], turns[:], ACT.Copy, bias=-ROUND).then_inc(s_turns, 1)
                        act.wait_ge(s_red, n + 1)
                        act.activation(wave[:, :, :, 0:D - 1], turns[:, :, :, 0:D - 1], ACT.Sin).then_inc(s_wave, 1)
                        act.activation(wave[:, :, :, D - 1:D], arg[:, :, :, D - 1:D], ACT.Copy).then_inc(s_wave, 1)
                        c.close()
                        act.wait_ge(s_o, n + 1)
                        act.dma_start(ho[n], o[:, u]).then_inc(s_out[u], 16)
                for u in range(2):
                    act.wait_ge(s_out[u], NG // 2 * 16)

            @block.vector
            def _(dve):
                c = Chain(dve, s_dve)
                dve.wait_ge(s_c, 16 * 25)
                c.link(dve.tensor_copy(idf[:], ids[:]))
                for k, (_, size) in enumerate(IDS):
                    c.mark(dve.tensor_scalar(neg[:, k], idf[:, k], 0.0, float(size), ALU.is_lt, ALU.mult))
                c.wait()
                c.link(dve.tensor_tensor(idf[:], idf[:], neg[:], ALU.add))
                for k, (_, size) in enumerate(IDS):
                    c.mark(dve.tensor_scalar(idf[:, k], idf[:, k], 0.0, float(size - 1), ALU.max, ALU.min))
                c.wait()
                c.link(dve.scalar_tensor_tensor(idf[:, SEG], idf[:, SEG], float(V_MODAL), idf[:, MODAL], ALU.mult, ALU.add))
                c.link(dve.tensor_copy(rows[:], idf[:, 0:4]))
                dve.sem_inc(s_rows, 1)
                c.link(dve.tensor_tensor(seg[:], seg[:], modal[:], ALU.add))
                dve.sem_inc(s_cmb, 1)
                dve.sem_inc(s_gfree, 2)
                c.close()
                with dve.Fori(0, NG // 2) as i:
                    for u in range(2):
                        n = i * 2 + u
                        c = Chain(dve, s_dve)
                        c.link(dve.tensor_copy(tg[:], tau[:, :, bass.ds(n * TB, TB)]))
                        for k in range(2):
                            for t in range(TB):
                                c.mark(dve.scalar_tensor_tensor(arg[:, t, k, :], wb[:, k, 0, :], tg[:, k, t:t + 1],
                                                                wb[:, k, 1, :], ALU.mult, ALU.add))
                        c.wait()
                        dve.sem_inc(s_arg, 1)
                        ob, gu = o[:, u], g[:, u]
                        dve.wait_ge(s_g[u], (i + 1) * 4 * TB * 16)
                        dve.wait_ge(s_out[u], i * 16)
                        c.mark(dve.tensor_tensor(e[:], gu[:, WORD], gu[:, SEG], ALU.add))
                        c.link(dve.tensor_tensor(ob, gu[:, NPI], gu[:, POS], ALU.add))
                        dve.sem_inc(s_gfree, 1)
                        c.mark(dve.tensor_tensor(e[:], e[:], ob, ALU.add))
                        dve.wait_ge(s_turns, n + 1)
                        c.link(dve.scalar_tensor_tensor(wave[:], turns[:], -TWO_PI_HI, arg[:], ALU.mult, ALU.add))
                        c.link(dve.scalar_tensor_tensor(wave[:], turns[:], -TWO_PI_LO, wave[:], ALU.mult, ALU.add))
                        c.link(dve.tensor_scalar(turns[:], wave[:], PI, -PI, ALU.min, ALU.max))
                        dve.sem_inc(s_red, 1)
                        dve.wait_ge(s_wave, 2 * n + 2)
                        c.link(dve.tensor_tensor(e[:], e[:], wave[:, :, 0, :], ALU.add))
                        c.link(dve.tensor_tensor(e[:], e[:], wave[:, :, 1, :], ALU.add))
                        norm_stats(dve, c, e, stats, mv, 1e-12, veps[:]).then_inc(s_var, 1)
                        dve.wait_ge(s_rstd, n + 1)
                        norm_apply(dve, c, ob, e, mv, rstd)
                        c.wait()
                        c.link(dve.tensor_tensor(ob, ob, bcast(gb[:, 0:1, :], [P, TB, D]), ALU.mult))
                        c.link(dve.tensor_tensor(ob, ob, bcast(gb[:, 1:2, :], [P, TB, D]), ALU.add))
                        dve.sem_inc(s_o, 1)
                        c.close()


def stage_l1_attention(nc, A, h_in, h_out):
    H, DH, M = 12, 16, 64
    NP = H // 2
    HC = H // KC
    V1 = DH + 1
    with ExitStack() as ctx:
        st = Stage(nc, ctx, "l1a")
        x = st.sb("x", [P, 2, TB, D])
        y = st.sb("y", [P, 2, TB, D])
        xT = st.sb("xT", [KP, KC, S])
        aT = st.sb("aT", [KP, KC, S])
        W = st.sb("W", [KP, KC, 3 * D])
        Wp = st.sb("Wp", [KP, KC, D])
        gb = st.sb("gb", [P, 3, D])
        feat = st.sb("feat", [KP, HC * M])
        half = st.sb("half", [KP, HC * M])
        kvmask = st.sb("kvmask", [P, 2 * V1])
        t1 = st.sb("t1", [KP, 2, KC, S])
        t2 = st.sb("t2", [KP, 2, KC, S])
        v1 = st.sb("v1", [P, TB, H, V1])
        kp = st.sb("kp", [P, TB, H * M])
        qp = st.sb("qp", [P, NP, S])
        kv = st.sb("kv", [P, NP, 2 * V1])
        den = st.sb("den", [P, TB, H])
        att = st.sb("att", [P, TB, H, DH])
        o = st.sb("o", [P, 2, TB, D])
        ident = st.sb("ident", [P, P])
        stats, mv = st.sb("stats", [P, TB, 6]), st.sb("mv", [P, TB, 2])
        veps, rstd, mhalf = st.sb("veps", [P, TB]), st.sb("rstd", [P, TB]), st.sb("mhalf", [P, TB])
        ps_t = st.ps("ps_t", [P, KC, S])
        ps_q = st.ps("ps_q", [P, KC, S])
        ps_e = st.ps("ps_e", [P, 2, S])
        ps_m = st.ps("ps_m", [P, 2, 256])
        ps_o = st.ps("ps_o", [P, 2, 256])
        s_x = [st.sem(f"x{u}") for u in range(2)]
        s_out = [st.sem(f"out{u}") for u in range(2)]
        names = ("c var rstd y t tc q qc sq v vc e ec kv kvc num att proj o dve pool ident ones pr").split()
        (s_c, s_var, s_rstd, s_y, s_t, s_tc, s_q, s_qc, s_sq, s_v, s_vc, s_e, s_ec, s_kv, s_kvc, s_num,
         s_att, s_proj, s_o, s_dve, s_pool, s_ident, s_ones, s_pr) = (st.sem(n) for n in names)
        hi, ho = batch_tiles(h_in), batch_tiles(h_out)
        NE = 2 * TB + NP
        with nc.Block() as block:

            @block.sync
            def _(sp):
                loads = [(W[:], A["L1_attn_W_qkv"]), (Wp[:], A["L1_attn_W_proj"]),
                         (gb[:, 0, :], A["L1_attn_gamma"].partition_broadcast(P)),
                         (gb[:, 1, :], A["L1_attn_beta"].partition_broadcast(P)),
                         (gb[:, 2, :], A["L1_attn_b_proj"].partition_broadcast(P)),
                         (half[:], A["c_half"]), (kvmask[:], A["c_kvmask"])]
                for to, src in loads:
                    sp.dma_start(to, src).then_inc(s_c, 16)
                sp.wait_ge(s_ones, 1)
                for n in range(HC):
                    sp.dma_start(feat[n * DH:(n + 1) * DH, n * M:(n + 1) * M], A["L1_attn_random_features"]).then_inc(s_c, 16)
                for u in range(2):
                    sp.dma_start(x[:, u], hi[u]).then_inc(s_x[u], 16)
                with sp.Fori(0, B // 2) as i:
                    for u in range(2):
                        b = i * 2 + u
                        sp.wait_ge(s_o, b + 1)
                        sp.dma_start(ho[b], o[:, u]).then_inc(s_out[u], 16)
                        sp.dma_start(x[:, u], hi[(b + 2) % B]).then_inc(s_x[u], 16)
                for u in range(2):
                    sp.wait_ge(s_out[u], B // 2 * 16)
                    sp.wait_ge(s_x[u], (B // 2 + 1) * 16)

            @block.gpsimd
            def _(pool):
                c = Chain(pool, s_pool)
                make_identity(pool, c, ident[:]).then_inc(s_ident, 1)
                c.link(pool.memset(mhalf[:], -0.5))
                with pool.Fori(0, B * 2 + 1) as i:
                    pool.wait_ge(s_var, i + 1)
                    pool.tensor_tensor(rstd[:], veps[:], mhalf[:], ALU.pow).then_inc(s_rstd, 1)

            @block.tensor
            def _(pe):
                pe.wait_ge(s_ident, 1)
                pe.wait_ge(s_c, 16 * (7 + HC))

                def turn(src):
                    for k in range(KC):
                        for t in range(TB):
                            m = pe.transpose(ps_t[0:KP, k, t * P:(t + 1) * P], src(t, k), ident[:])
                    m.then_inc(s_t, 1)

                def project(b, a):
                    pe.wait_ge(s_qc, 2 * b + a)
                    for c in range(KC):
                        for k in range(KC):
                            m = pe.matmul(ps_q[0:KP, c, :], W[:, k, a * D + c * KP:a * D + (c + 1) * KP], xT[:, k, :],
                                          start=(k == 0), stop=(k == KC - 1))
                    m.then_inc(s_q, 1)

                def project_v(b):
                    for r in range(2):
                        if r == 1:
                            pe.wait_ge(s_vc, 2 * b + 1)
                        for t in range(2):
                            for k in range(KC):
                                m = pe.matmul(ps_m[:, t, 0:D], xT[:, k, (2 * r + t) * P:(2 * r + t + 1) * P],
                                              W[:, k, 2 * D:3 * D], start=(k == 0), stop=(k == KC - 1))
                        m.then_inc(s_v, 1)

                pe.wait_ge(s_y, 1)
                turn(lambda t, k: y[:, 0, t, k * KP:(k + 1) * KP])
                pe.wait_ge(s_tc, 1)
                project(0, 0)
                project(0, 1)
                project_v(0)
                with pe.Fori(0, B // 2) as i:
                    for u in range(2):
                        b = i * 2 + u
                        pe.wait_ge(s_qc, 2 * b + 2)
                        pe.wait_ge(s_sq, 2 * b + 2)
                        for n in range(2 * TB):
                            t, c = n // 2, n % 2
                            if n > 0:
                                pe.wait_ge(s_ec, b * NE + n - 1)
                            pe.matmul(ps_e[:, n % 2, 0:HC * M], t1[:, 1, c, t * P:(t + 1) * P], feat[:],
                                      start=True, stop=False)
                            pe.matmul(ps_e[:, n % 2, 0:HC * M], t2[:, 1, c, t * P:(t + 1) * P], half[:], start=False,
                                      stop=True).then_inc(s_e, 1)
                        for p in range(NP):
                            c, cols = p // 3, slice(p % 3 * P, (p % 3 + 1) * P)
                            n = 2 * TB + p
                            pe.wait_ge(s_ec, b * NE + n - 1)
                            pe.matmul(ps_e[:, n % 2, :], feat[:, cols], t1[:, 0, c, :], start=True, stop=False)
                            pe.matmul(ps_e[:, n % 2, :], half[:, cols], t2[:, 0, c, :], start=False,
                                      stop=True).then_inc(s_e, 1)
                        pe.wait_ge(s_y, b + 2)
                        pe.wait_ge(s_tc, 2 * b + 1)
                        turn(lambda t, k: y[:, 1 - u, t, k * KP:(k + 1) * KP])
                        pe.wait_ge(s_vc, 2 * b + 2)
                        pe.wait_ge(s_proj, 2 * b)
                        for p in range(NP):
                            for t in range(TB):
                                m = pe.matmul(ps_m[:].rearrange("p a f -> p (a f)")[:, p * 2 * V1:(p + 1) * 2 * V1],
                                              kp[:, t, p * P:(p + 1) * P],
                                              v1[:, t, 2 * p:2 * p + 2, :].rearrange("p a f -> p (a f)"),
                                              start=(t == 0), stop=(t == TB - 1))
                        m.then_inc(s_kv, 1)
                        pe.wait_ge(s_tc, 2 * b + 2)
                        project(b + 1, 0)
                        pe.wait_ge(s_kvc, b + 1)
                        pe.wait_ge(s_ec, (b + 1) * NE)
                        for r in range(2):
                            pe.wait_ge(s_att, 2 * b + r)
                            for t in range(2):
                                for p in range(NP):
                                    m = pe.matmul(ps_o[:, t, p * 2 * V1:(p + 1) * 2 * V1],
                                                  qp[:, p, (2 * r + t) * P:(2 * r + t + 1) * P], kv[:, p, :],
                                                  start=True, stop=True)
                            m.then_inc(s_num, 1)
                            if r == 0:
                                project(b + 1, 1)
                        project_v(b + 1)
                        pe.wait_ge(s_att, 2 * b + 2)
                        turn(lambda t, k: att[:, t, k * HC:(k + 1) * HC, :].rearrange("p h d -> p (h d)"))
                        pe.wait_ge(s_tc, 2 * b + 3)
                        pe.wait_ge(s_vc, 2 * b + 4)
                        for r in range(2):
                            if r == 1:
                                pe.wait_ge(s_proj, 2 * b + 1)
                            for t in range(2):
                                for k in range(KC):
                                    m = pe.matmul(ps_m[:, t, 0:D], aT[:, k, (2 * r + t) * P:(2 * r + t + 1) * P],
                                                  Wp[:, k, :], start=(k == 0), stop=(k == KC - 1))
                            m.then_inc(s_pr, 1)

            @block.scalar
            def _(act):

                def squares(b):
                    for a in range(2):
                        act.wait_ge(s_qc, 2 * b + a + 1)
                        act.activation(t2[:, a], t1[:, a], ACT.Square).then_inc(s_sq, 1)

                squares(0)
                with act.Fori(0, B) as b:
                    for n in range(2 * TB):
                        act.wait_ge(s_e, b * NE + n + 1)
                        act.activation(kp[:, n // 2, n % 2 * HC * M:(n % 2 + 1) * HC * M], ps_e[:, n % 2, 0:HC * M],
                                       ACT.Exp).then_inc(s_ec, 1)
                    for p in range(NP):
                        n = 2 * TB + p
                        act.wait_ge(s_e, b * NE + n + 1)
                        act.activation(qp[:, p, :], ps_e[:, n % 2, :], ACT.Exp).then_inc(s_ec, 1)
                    squares(b + 1)

            @block.vector
            def _(dve):
                c = Chain(dve, s_dve)
                c.link(dve.memset(feat[:], 0.0))
                c.link(dve.memset(v1[:], 1.0))
                dve.sem_inc(s_ones, 1)
                c.close()
                dve.wait_ge(s_c, 16 * (7 + HC))

                def first_norm(u, loads, roots):
                    c = Chain(dve, s_dve)
                    dve.wait_ge(s_x[u], loads * 16)
                    norm_stats(dve, c, x[:, u], stats, mv, 1e-5, veps[:]).then_inc(s_var, 1)
                    dve.wait_ge(s_rstd, roots)
                    norm_apply(dve, c, y[:, u], x[:, u], mv, rstd)
                    c.wait()
                    dve.sem_inc(s_y, 1)
                    c.close()

                def copy_xT(u, turns):
                    c = Chain(dve, s_dve)
                    dve.wait_ge(s_t, turns)
                    dve.tensor_copy(xT[:], ps_t[0:KP]).then_inc(s_tc, 1)
                    c.link(dve.tensor_tensor(y[:, u], y[:, u], bcast(gb[:, 2:3, :], [P, TB, D]), ALU.add))
                    c.close()

                def copy_qk(b, a):
                    dve.wait_ge(s_q, 2 * b + a + 1)
                    dve.tensor_copy(t1[:, a], ps_q[0:KP]).then_inc(s_qc, 1)

                def copy_v(b):
                    for r in range(2):
                        dve.wait_ge(s_v, 2 * b + r + 1)
                        dve.tensor_copy(v1[:, 2 * r:2 * r + 2, :, 0:DH],
                                        ps_m[:, :, 0:D].rearrange("p t (h d) -> p t h d", h=H)).then_inc(s_vc, 1)

                first_norm(0, 1, 1)
                copy_xT(0, 1)
                copy_qk(0, 0)
                copy_qk(0, 1)
                copy_v(0)
                with dve.Fori(0, B // 2) as i:
                    for u in range(2):
                        b = i * 2 + u
                        xb, yb, ob = x[:, u], y[:, u], o[:, u]
                        first_norm(1 - u, i + 1 + u, 2 * b + 2)
                        copy_xT(1 - u, 2 * b + 2)
                        dve.wait_ge(s_kv, b + 1)
                        dve.tensor_tensor(kv[:], ps_m[:].rearrange("p a f -> p (a f)")[:, 0:NP * 2 * V1]
                                          .rearrange("p (n f) -> p n f", n=NP),
                                          bcast(kvmask[:].unsqueeze(1), [P, NP, 2 * V1]), ALU.mult).then_inc(s_kvc, 1)
                        copy_qk(b + 1, 0)
                        c = Chain(dve, s_dve)
                        for r in range(2):
                            dve.wait_ge(s_num, 2 * b + r + 1)
                            frac = ps_o[:, :, 0:H * V1].rearrange("p t (h f) -> p t h f", h=H)
                            dn = den[:, 2 * r:2 * r + 2, :]
                            c.link(dve.tensor_scalar(dn, frac[:, :, :, DH], 1e-6, None, ALU.add))
                            c.link(dve.reciprocal(dn, dn))
                            dve.tensor_tensor(att[:, 2 * r:2 * r + 2], frac[:, :, :, 0:DH],
                                              bcast(dn.unsqueeze(3), [P, 2, H, DH]), ALU.mult).then_inc(s_att, 1)
                            if r == 0:
                                copy_qk(b + 1, 1)
                        copy_v(b + 1)
                        dve.wait_ge(s_t, 2 * b + 3)
                        dve.tensor_copy(aT[:], ps_t[0:KP]).then_inc(s_tc, 1)
                        for r in range(2):
                            dve.wait_ge(s_pr, 2 * b + r + 1)
                            c.link(dve.tensor_tensor(yb[:, 2 * r:2 * r + 2], yb[:, 2 * r:2 * r + 2], ps_m[:, :, 0:D],
                                                     ALU.add))
                            dve.sem_inc(s_proj, 1)
                        norm_stats(dve, c, yb, stats, mv, 1e-5, veps[:]).then_inc(s_var, 1)
                        dve.wait_ge(s_rstd, 2 * b + 3)
                        dve.wait_ge(s_out[u], i * 16)
                        norm_apply(dve, c, ob, yb, mv, rstd)
                        c.wait()
                        c.link(dve.tensor_tensor(ob, ob, bcast(gb[:, 0:1, :], [P, TB, D]), ALU.mult))
                        c.link(dve.tensor_tensor(ob, ob, bcast(gb[:, 1:2, :], [P, TB, D]), ALU.add))
                        c.link(dve.tensor_tensor(ob, ob, xb, ALU.add))
                        dve.sem_inc(s_o, 1)
                        c.close()


def stage_l1_ffn(nc, A, h_in, h_out):
    E, I = 4, 384
    C = I // P
    N = E * C
    R = 3
    with ExitStack() as ctx:
        st = Stage(nc, ctx, "l1f")
        x = st.sb("x", [P, 2, TB, D])
        y = st.sb("y", [P, TB, D])
        xT = st.sb("xT", [KP, 2, KC, S])
        Wg, Wu = st.sb("Wg", [KP, E, KC, I]), st.sb("Wu", [KP, E, KC, I])
        gate, up = ([st.sb(f"{n}{part}", [KP, E, KC, I], F32R) for part in ("hi", "lo")] for n in ("gate", "up"))
        xh, xl = st.sb("xh", [KP, 2, KC, S], F32R), st.sb("xl", [KP, 2, KC, S], F32R)
        Wd = st.sb("Wd", [P, E, C, D])
        Wr = st.sb("Wr", [KP, KC, R])
        rb = st.sb("rb", [P, R])
        sg = st.sb("sg", [P, 2, S])
        hT = st.sb("hT", [P, 2, C, S])
        pr = st.sb("pr", [P, TB, R])
        cmp = st.sb("cmp", [P, 3, TB])
        keep = st.sb("keep", [P, TB, R])
        tot = st.sb("tot", [P, TB])
        o = st.sb("o", [P, 2, TB, D])
        ident = st.sb("ident", [P, P])
        stats, mv = st.sb("stats", [P, TB, 6]), st.sb("mv", [P, TB, 2])
        veps, rstd, mhalf = st.sb("veps", [P, TB]), st.sb("rstd", [P, TB]), st.sb("mhalf", [P, TB])
        ps_t = st.ps("ps_t", [P, KC, S])
        ps_g, ps_u = st.ps("ps_g", [P, 2, S]), st.ps("ps_u", [P, 2, S])
        ps_d = st.ps("ps_d", [P, TB, 256])
        s_ws = st.sem("ws")
        s_x = [st.sem(f"x{u}") for u in range(2)]
        s_out = [st.sem(f"out{u}") for u in range(2)]
        names = "c xfree var rstd y t tc r rl p g u sg h d acc o dve pool ident".split()
        (s_c, s_xfree, s_var, s_rstd, s_y, s_t, s_tc, s_r, s_rl, s_p, s_g, s_u, s_sg, s_h, s_d, s_acc, s_o,
         s_dve, s_pool, s_ident) = (st.sem(n) for n in names)
        hi, ho = batch_tiles(h_in), batch_tiles(h_out)
        with nc.Block() as block:

            @block.sync
            def _(sp):
                loads = [(Wg[:, 0], A["L1_ffn_shared_gate"]), (Wu[:, 0], A["L1_ffn_shared_up"]),
                         (Wg[:, 1:], A["L1_ffn_routed_gate"]), (Wu[:, 1:], A["L1_ffn_routed_up"]),
                         (Wd[:, 0], A["L1_ffn_shared_down"]), (Wd[:, 1:], A["L1_ffn_routed_down"]),
                         (Wr[:], A["L1_ffn_router_w"]), (rb[:], A["L1_ffn_routing_bias"].partition_broadcast(P))]
                sp.dma_start(x[:, 0], hi[0]).then_inc(s_x[0], 16)
                for to, src in loads:
                    sp.dma_start(to, src).then_inc(s_c, 16)
                with sp.Fori(0, B // 2) as i:
                    for u in range(2):
                        b = i * 2 + u
                        sp.wait_ge(s_xfree, b + 1)
                        sp.dma_start(x[:, 1 - u], hi[(b + 1) % B]).then_inc(s_x[1 - u], 16)

            @block.gpsimd
            def _(pool):
                c = Chain(pool, s_pool)
                make_identity(pool, c, ident[:]).then_inc(s_ident, 1)
                c.link(pool.memset(mhalf[:], -0.5))
                c.wait()
                pool.wait_ge(s_var, 1)
                c.link(pool.tensor_tensor(rstd[:], veps[:], mhalf[:], ALU.pow))
                pool.sem_inc(s_rstd, 1)
                pool.wait_ge(s_c, 16 * 8)
                split(pool, c, up[0][:], up[1][:], Wu[:]).then_inc(s_ws, 1)
                with pool.Fori(1, B + 1) as i:
                    pool.wait_ge(s_var, i + 1)
                    pool.tensor_tensor(rstd[:], veps[:], mhalf[:], ALU.pow).then_inc(s_rstd, 1)

            @block.tensor
            def _(pe):

                def turn(b, u):
                    pe.wait_ge(s_y, b + 1)
                    for k in range(KC):
                        for t in range(TB):
                            m = pe.transpose(ps_t[0:KP, k, t * P:(t + 1) * P], y[:, t, k * KP:(k + 1) * KP], ident[:])
                    m.then_inc(s_t, 1)

                def down(b, e):
                    pe.wait_ge(s_h, b * N + (e + 1) * C)
                    pe.wait_ge(s_acc, b * E + e)
                    if e == 0:
                        pe.wait_ge(s_rl, b + 1)
                    for t in range(TB):
                        for k in range(C):
                            m = pe.matmul(ps_d[:, t, 0:D], hT[:, e % 2, k, t * P:(t + 1) * P], Wd[:, e, k, :],
                                          start=(k == 0), stop=(k == C - 1))
                    m.then_inc(s_d, 1)

                pe.wait_ge(s_ident, 1)
                turn(0, 0)
                pe.wait_ge(s_c, 16 * 8)
                pe.wait_ge(s_ws, 2)
                with pe.Fori(0, B // 2) as i:
                    for u in range(2):
                        b = i * 2 + u
                        pe.wait_ge(s_tc, b + 1)
                        pe.wait_ge(s_acc, b * E)
                        for t in range(TB):
                            for k in range(KC):
                                m = pe.matmul(ps_d[:, t, D:D + R], xT[:, u, k, t * P:(t + 1) * P], Wr[:, k, :],
                                              start=(k == 0), stop=(k == KC - 1))
                        m.then_inc(s_r, 1)
                        for n in range(N):
                            e, c = n // C, n % C
                            cols = slice(c * P, (c + 1) * P)
                            pe.wait_ge(s_h, b * N + n - 1) if n else None
                            for (wh, wl), bank in ((gate, ps_g), (up, ps_u)):
                                for k in range(KC):
                                    pe.matmul(bank[:, n % 2], wh[:, e, k, cols], xh[:, u, k, :], start=(k == 0), stop=False)
                                    pe.matmul(bank[:, n % 2], wh[:, e, k, cols], xl[:, u, k, :], start=False, stop=False)
                                    m = pe.matmul(bank[:, n % 2], wl[:, e, k, cols], xh[:, u, k, :],
                                                  start=False, stop=(k == KC - 1))
                                m.then_inc(s_g if bank is ps_g else s_u, 1)
                            if c == 1 and e:
                                down(b, e - 1)
                        turn(b + 1, 1 - u)
                        down(b, E - 1)

            @block.scalar
            def _(act):
                with act.Fori(0, B // 2) as i:
                    for u in range(2):
                        b = i * 2 + u
                        act.wait_ge(s_rl, b + 1)
                        act.activation(pr[:], pr[:], ACT.Sigmoid).then_inc(s_p, 1)
                        for n in range(N):
                            act.wait_ge(s_g, b * N + n + 1)
                            act.wait_ge(s_h, b * N + n - 1) if n else None
                            act.activation(sg[:, n % 2], ps_g[:, n % 2], ACT.Silu).then_inc(s_sg, 1)
                        act.wait_ge(s_o, b + 1)
                        act.dma_start(ho[b], o[:, u]).then_inc(s_out[u], 16)
                for u in range(2):
                    act.wait_ge(s_out[u], B // 2 * 16)

            @block.vector
            def _(dve):

                def norm(c, b, i, u):
                    dve.wait_ge(s_x[u], (i + 1) * 16)
                    norm_stats(dve, c, x[:, u], stats, mv, 1e-5, veps[:]).then_inc(s_var, 1)
                    dve.wait_ge(s_rstd, b + 1)
                    norm_apply(dve, c, y, x[:, u], mv, rstd)
                    c.wait()
                    dve.sem_inc(s_y, 1)

                def weights(c):
                    p0, p1, p2 = (pr[:, :, e] for e in range(R))
                    c20, c21, c10 = (cmp[:, k, :] for k in range(3))
                    k0, k1, k2 = (keep[:, :, e] for e in range(R))
                    c.mark(dve.tensor_tensor(c20, p2, p0, ALU.is_gt))
                    c.mark(dve.tensor_tensor(c21, p2, p1, ALU.is_gt))
                    c.link(dve.tensor_tensor(c10, p1, p0, ALU.is_gt))
                    c.mark(dve.tensor_tensor(k2, c20, c21, ALU.max))
                    c.mark(dve.tensor_tensor(k1, c21, c21, ALU.mult))
                    c.mark(dve.tensor_tensor(k0, c20, c10, ALU.mult))
                    c.wait()
                    c.link(dve.tensor_scalar(k1, k1, -1.0, 1.0, ALU.mult, ALU.add))
                    c.mark(dve.tensor_tensor(k1, k1, c10, ALU.max))
                    c.link(dve.tensor_scalar(k0, k0, -1.0, 1.0, ALU.mult, ALU.add))
                    c.link(dve.tensor_tensor(pr[:], pr[:], keep[:], ALU.mult))
                    c.link(dve.tensor_reduce(tot[:], pr[:], AX.X, ALU.add))
                    c.link(dve.reciprocal(tot[:], tot[:]))
                    c.link(dve.tensor_tensor(pr[:], pr[:], bcast(tot[:].unsqueeze(2), [P, TB, R]), ALU.mult))

                def accumulate(c, b, e, i, u):
                    dve.wait_ge(s_d, b * E + e + 1)
                    if e == 0:
                        dve.wait_ge(s_out[u], i * 16)
                        c.link(dve.tensor_tensor(o[:, u], ps_d[:, :, 0:D], x[:, u], ALU.add))
                    else:
                        for t in range(TB):
                            c.mark(dve.scalar_tensor_tensor(o[:, u, t, :], ps_d[:, t, 0:D], pr[:, t, e - 1:e],
                                                            o[:, u, t, :], ALU.mult, ALU.add))
                        c.wait()
                    dve.sem_inc(s_acc, 1)

                def copy_x(c, b, u):
                    dve.wait_ge(s_t, b + 1)
                    c.mark(dve.tensor_copy(xT[:, u], ps_t[0:KP]))
                    c.mark(split(dve, c, xh[:, u], xl[:, u], ps_t[0:KP]))
                    c.wait()
                    dve.sem_inc(s_tc, 1)

                dve.sem_inc(s_xfree, 1)
                c = Chain(dve, s_dve)
                norm(c, 0, 0, 0)
                copy_x(c, 0, 0)
                dve.wait_ge(s_c, 16 * 8)
                split(dve, c, gate[0][:], gate[1][:], Wg[:]).then_inc(s_ws, 1)
                c.close()
                with dve.Fori(0, B // 2) as i:
                    for u in range(2):
                        b = i * 2 + u
                        c = Chain(dve, s_dve)
                        dve.wait_ge(s_r, b + 1)
                        c.link(dve.tensor_tensor(pr[:], ps_d[:, :, D:D + R], bcast(rb[:].unsqueeze(1), [P, TB, R]), ALU.add))
                        dve.sem_inc(s_rl, 1)
                        for n in range(N):
                            e = n // C
                            dve.wait_ge(s_sg, b * N + n + 1)
                            dve.wait_ge(s_u, b * N + n + 1)
                            dve.tensor_tensor(hT[:, e % 2, n % C, :], sg[:, n % 2], ps_u[:, n % 2], ALU.mult).then_inc(s_h, 1)
                            if n == 1:
                                dve.wait_ge(s_p, b + 1)
                                weights(c)
                            if n % C == 2 and e:
                                accumulate(c, b, e - 1, i, u)
                            if n == 6:
                                norm(c, b + 1, (i if u == 0 else i + 1), 1 - u)
                        copy_x(c, b + 1, 1 - u)
                        accumulate(c, b, E - 1, i, u)
                        dve.sem_inc(s_o, 1)
                        dve.sem_inc(s_xfree, 1)
                        c.close()


def top1(dve, act_turn, c, logits, shape, m, oh, val, rank, best, ex, prob):
    N, E = shape
    full = [P, N, E]
    c.link(dve.tensor_reduce(m[:], logits, AX.X, ALU.max))
    c.mark(dve.tensor_tensor(ex[:], logits, bcast(m[:].unsqueeze(2), full), ALU.subtract))
    c.link(dve.tensor_tensor(oh[:], logits, bcast(m[:].unsqueeze(2), full), ALU.is_ge))
    act_turn()
    c.link(dve.tensor_tensor(val[:], oh[:], bcast(rank[:, 0:E].unsqueeze(1), full), ALU.mult))
    c.link(dve.tensor_reduce(best[:], val[:], AX.X, ALU.max))
    c.link(dve.tensor_tensor(oh[:], val[:], bcast(best[:].unsqueeze(2), full), ALU.is_equal))
    c.link(dve.tensor_reduce(prob[:], ex[:], AX.X, ALU.add))
    c.link(dve.reciprocal(prob[:], prob[:]))


def grouped_ffn_stage(nc, A, name, xs_d, ys_d, eid_d, w1_d, w2_d, b1_d, b2_d, func, NG, TG):
    F, C = 768, 6
    NB, AHEAD = 4, 3
    assert NG % NB == 0
    N = TG * P
    with ExitStack() as ctx:
        st = Stage(nc, ctx, name)
        eid = st.sb("eid", [1, NG + AHEAD], I32)
        w1 = st.sb("w1", [KP, NB, KC, F])
        w2 = st.sb("w2", [P, NB, C, D])
        b1 = st.sb("b1", [P, NB, C])
        b2 = st.sb("b2", [P, NB, D])
        x = st.sb("x", [P, NB, TG, D])
        xT = st.sb("xT", [KP, 2, KC, N])
        hT = st.sb("hT", [P, 2, C, N])
        o = st.sb("o", [P, 2, TG, D])
        ident = st.sb("ident", [P, P])
        ps_t = st.ps("ps_t", [P, KC, S])
        ps_h = st.ps("ps_h", [P, 3, S])
        ps_y = st.ps("ps_y", [P, 2 if TG == 4 else 1, S])
        s_w = [st.sem(f"w{u}") for u in range(NB)]
        s_x = [st.sem(f"x{u}") for u in range(NB)]
        s_out = [st.sem(f"out{u}") for u in range(2)]
        names = "e t tc h hc y o pool ident".split()
        s_e, s_t, s_tc, s_h, s_hc, s_y, s_o, s_pool, s_ident = (st.sem(n) for n in names)
        xi = xs_d.rearrange("(g t p) d -> g p t d", t=TG, p=P)
        yo = ys_d.rearrange("(g t p) d -> g p t d", t=TG, p=P)
        nw = 2 + (b1_d is not None) * 2

        def y_bank(t):
            return ps_y[:, t // 2, t % 2 * 256:t % 2 * 256 + D]

        with nc.Block() as block:

            @block.sync
            def _(sp):

                def load(g, u):
                    e = sp.value_load(eid[0:1, bass.ds(g, 1)], min_val=0, max_val=w1_d.shape[0] - 1)
                    sp.dma_start(x[:, u], xi[g % NG]).then_inc(s_x[u], 16)
                    sp.dma_start(w1[:, u], w1_d[e]).then_inc(s_w[u], 16)
                    sp.dma_start(w2[:, u], w2_d[e]).then_inc(s_w[u], 16)
                    if b1_d is not None:
                        sp.dma_start(b1[:, u], b1_d[e]).then_inc(s_w[u], 16)
                        sp.dma_start(b2[:, u], b2_d[e].partition_broadcast(P)).then_inc(s_w[u], 16)

                sp.dma_start(eid[0:1, 0:NG], eid_d[0:1, 0:NG]).then_inc(s_e, 16)
                sp.dma_start(eid[0:1, NG:NG + AHEAD], eid_d[0:1, 0:AHEAD]).then_inc(s_e, 16)
                sp.wait_ge(s_e, 32)
                for g in range(AHEAD):
                    load(g, g)
                with sp.Fori(0, NG // NB) as i:
                    for u in range(NB):
                        g = i * NB + u
                        sp.wait_ge(s_o, g)
                        load(g + AHEAD, (u + AHEAD) % NB)
                for u in range(NB):
                    n = NG // NB + (u < AHEAD)
                    sp.wait_ge(s_x[u], n * 16)
                    sp.wait_ge(s_w[u], n * 16 * nw)

            @block.gpsimd
            def _(pool):
                c = Chain(pool, s_pool)
                make_identity(pool, c, ident[:]).then_inc(s_ident, 1)

            @block.tensor
            def _(pe):

                def turn(g, i, u):
                    pe.wait_ge(s_x[u], (i + 1) * 16)
                    pe.wait_ge(s_tc, g)
                    for k in range(KC):
                        for t in range(TG):
                            m = pe.transpose(ps_t[0:KP, k, t * P:(t + 1) * P], x[:, u, t, k * KP:(k + 1) * KP], ident[:])
                    m.then_inc(s_t, 1)

                def first_product(g, i, u):
                    pe.wait_ge(s_w[u], (i + 1) * 16 * nw)
                    pe.wait_ge(s_tc, g + 1)
                    for c in range(C):
                        if not isinstance(g, int) or c >= 3:
                            pe.wait_ge(s_hc, g * C + c - 2)
                        for k in range(KC):
                            m = pe.matmul(ps_h[:, c % 3, 0:N], w1[:, u, k, c * P:(c + 1) * P], xT[:, u % 2, k, :],
                                          start=(k == 0), stop=(k == KC - 1))
                        m.then_inc(s_h, 1)

                pe.wait_ge(s_ident, 1)
                turn(0, 0, 0)
                turn(1, 0, 1)
                first_product(0, 0, 0)
                with pe.Fori(0, NG // NB) as i:
                    for u in range(NB):
                        g = i * NB + u
                        turn(g + 2, i + (u + 2) // NB, (u + 2) % NB)
                        first_product(g + 1, i + (u + 1) // NB, (u + 1) % NB)
                        pe.wait_ge(s_hc, (g + 1) * C)
                        pe.wait_ge(s_o, g)
                        for t in range(TG):
                            for c in range(C):
                                m = pe.matmul(y_bank(t), hT[:, u % 2, c, t * P:(t + 1) * P], w2[:, u, c, :],
                                              start=(c == 0), stop=(c == C - 1))
                        m.then_inc(s_y, 1)

            @block.scalar
            def _(act):

                def between(g, i, u):
                    act.wait_ge(s_w[u], (i + 1) * 16 * nw)
                    for c in range(C):
                        act.wait_ge(s_h, g * C + c + 1)
                        bias = 0.0 if b1_d is None else b1[:, u, c:c + 1]
                        act.activation(hT[:, u % 2, c, :], ps_h[:, c % 3, 0:N], func, bias=bias).then_inc(s_hc, 1)

                between(0, 0, 0)
                with act.Fori(0, NG // NB) as i:
                    for u in range(NB):
                        g = i * NB + u
                        between(g + 1, i + (u + 1) // NB, (u + 1) % NB)
                        act.wait_ge(s_o, g + 1)
                        act.dma_start(yo[g], o[:, u % 2]).then_inc(s_out[u % 2], 16)
                for u in range(2):
                    act.wait_ge(s_out[u], NG // 2 * 16)

            @block.vector
            def _(dve):

                def copy_x(g, u):
                    dve.wait_ge(s_t, g + 1)
                    dve.tensor_copy(xT[:, u], ps_t[0:KP, :, 0:N]).then_inc(s_tc, 1)

                copy_x(0, 0)
                copy_x(1, 1)
                with dve.Fori(0, NG // NB) as i:
                    for u in range(NB):
                        g = i * NB + u
                        copy_x(g + 2, u % 2)
                        dve.wait_ge(s_y, g + 1)
                        dve.wait_ge(s_out[u % 2], (i * 2 + u // 2) * 16)
                        view = ps_y[:].rearrange("p a (b f) -> p (a b) f", b=2)[:, 0:TG, 0:D]
                        if b2_d is None:
                            dve.tensor_copy(o[:, u % 2], view).then_inc(s_o, 1)
                        else:
                            dve.tensor_tensor(o[:, u % 2], view, bcast(b2[:, u:u + 1, :], [P, TG, D]),
                                              ALU.add).then_inc(s_o, 1)


def l2_gate_stage(nc, A, h_in, xs_d, eid_d, prob_d):
    E = 3
    with ExitStack() as ctx:
        st = Stage(nc, ctx, "l2g")
        x = st.sb("x", [P, 2, TB, D])
        y = st.sb("y", [P, 2, TB, D])
        Wg = st.sb("Wg", [KP, KC, E])
        rank = st.sb("rank", [P, 16])
        mean = st.sb("mean", [KP, KC, P])
        ones = st.sb("ones", [P, P])
        lg, ex, oh, val = (st.sb(n, [P, B, E]) for n in ("lg", "ex", "oh", "val"))
        m, best, prob = (st.sb(n, [P, B]) for n in ("m", "best", "prob"))
        eid = st.sb("eid", [P, B], I32)
        stats, mv = st.sb("stats", [P, TB, 6]), st.sb("mv", [P, TB, 2])
        veps, rstd, mhalf = st.sb("veps", [P, TB]), st.sb("rstd", [P, TB]), st.sb("mhalf", [P, TB])
        ps_m, ps_l = st.ps("ps_m", [P, KC]), st.ps("ps_l", [P, E])
        s_x = [st.sem(f"x{u}") for u in range(2)]
        s_out = [st.sem(f"out{u}") for u in range(2)]
        names = "c xfree var rstd y m mc l lc ex exd fin pool dve fout".split()
        (s_c, s_xfree, s_var, s_rstd, s_y, s_m, s_mc, s_l, s_lc, s_ex, s_exd, s_fin, s_pool, s_dve,
         s_fout) = (st.sem(n) for n in names)
        hi, ho = batch_tiles(h_in), batch_tiles(xs_d)
        with nc.Block() as block:

            @block.sync
            def _(sp):
                sp.dma_start(Wg[:], A["L2_ffn_Wg"]).then_inc(s_c, 16)
                sp.dma_start(rank[:], A["c_rank"]).then_inc(s_c, 16)
                with sp.Fori(0, B // 2) as i:
                    for u in range(2):
                        sp.wait_ge(s_xfree, i * 2 + u + 1)
                        sp.dma_start(x[:, u], hi[i * 2 + u]).then_inc(s_x[u], 16)
                sp.wait_ge(s_fin, 1)
                sp.dma_start(eid_d, eid[0:1, :]).then_inc(s_fout, 16)
                sp.dma_start(prob_d, prob[:]).then_inc(s_fout, 16)
                sp.wait_ge(s_fout, 32)

            @block.gpsimd
            def _(pool):
                c = Chain(pool, s_pool)
                c.link(pool.memset(mhalf[:], -0.5))
                with pool.Fori(0, B) as i:
                    pool.wait_ge(s_var, i + 1)
                    pool.tensor_tensor(rstd[:], veps[:], mhalf[:], ALU.pow).then_inc(s_rstd, 1)

            @block.tensor
            def _(pe):
                pe.wait_ge(s_c, 32)
                with pe.Fori(0, B // 2) as i:
                    for u in range(2):
                        b = i * 2 + u
                        pe.wait_ge(s_y, b + 1)
                        for k in range(KC):
                            for t in range(TB):
                                mm = pe.matmul(ps_m[0:KP, k:k + 1], y[:, u, t, k * KP:(k + 1) * KP], ones[:, 0:1],
                                               start=(t == 0), stop=(t == TB - 1))
                        mm.then_inc(s_m, 1)
                        pe.wait_ge(s_mc, b + 1)
                        for k in range(KC):
                            mm = pe.matmul(ps_l[:], mean[:, k, :], Wg[:, k, :], start=(k == 0), stop=(k == KC - 1))
                        mm.then_inc(s_l, 1)

            @block.scalar
            def _(act):
                with act.Fori(0, B // 2) as i:
                    for u in range(2):
                        b = i * 2 + u
                        act.wait_ge(s_y, b + 1)
                        act.dma_start(ho[b], y[:, u]).then_inc(s_out[u], 16)
                act.wait_ge(s_ex, 1)
                act.activation(ex[:], ex[:], ACT.Exp).then_inc(s_exd, 1)
                for u in range(2):
                    act.wait_ge(s_out[u], B // 2 * 16)

            @block.vector
            def _(dve):
                c = Chain(dve, s_dve)
                c.link(dve.memset(ones[:], 1.0))
                dve.sem_inc(s_xfree, 2)
                c.close()
                dve.wait_ge(s_c, 32)
                with dve.Fori(0, B // 2) as i:
                    for u in range(2):
                        b = i * 2 + u
                        c = Chain(dve, s_dve)
                        dve.wait_ge(s_x[u], (i + 1) * 16)
                        norm_stats(dve, c, x[:, u], stats, mv, 1e-5, veps[:]).then_inc(s_var, 1)
                        dve.wait_ge(s_rstd, b + 1)
                        dve.wait_ge(s_out[u], i * 16)
                        norm_apply(dve, c, y[:, u], x[:, u], mv, rstd)
                        c.wait()
                        dve.sem_inc(s_y, 1)
                        dve.sem_inc(s_xfree, 1)
                        dve.wait_ge(s_m, b + 1)
                        c.mark(dve.tensor_scalar(mean[:], bcast(ps_m[0:KP].unsqueeze(2), [KP, KC, P]), 1.0 / S, None, ALU.mult))
                        c.wait()
                        dve.sem_inc(s_mc, 1)
                        dve.wait_ge(s_l, b + 1)
                        c.link(dve.tensor_copy(lg[:, bass.ds(b, 1), :], ps_l[:].unsqueeze(1)))
                        c.close()
                c = Chain(dve, s_dve)

                def act_turn():
                    dve.sem_inc(s_ex, 1)
                    dve.wait_ge(s_exd, 1)

                top1(dve, act_turn, c, lg[:], (B, E), m, oh, val, rank, best, ex, prob)
                c.link(dve.tensor_scalar(eid[:], best[:], -1.0, 16.0, ALU.mult, ALU.add))
                dve.sem_inc(s_fin, 1)
                c.close()


def l2_add_stage(nc, A, h_in, ys_d, prob_d, h_out):
    with ExitStack() as ctx:
        st = Stage(nc, ctx, "l2s")
        x, ys, o = (st.sb(n, [P, 2, TB, D]) for n in ("x", "ys", "o"))
        prob = st.sb("prob", [P, B])
        pb = st.sb("pb", [P, 1])
        s_x = [st.sem(f"x{u}") for u in range(2)]
        s_out = [st.sem(f"out{u}") for u in range(2)]
        s_c, s_free, s_o, s_dve = (st.sem(n) for n in ("c", "free", "o", "dve"))
        hi, yi, ho = batch_tiles(h_in), batch_tiles(ys_d), batch_tiles(h_out)
        with nc.Block() as block:

            @block.sync
            def _(sp):
                sp.dma_start(prob[:], prob_d).then_inc(s_c, 16)
                with sp.Fori(0, B // 2) as i:
                    for u in range(2):
                        b = i * 2 + u
                        sp.wait_ge(s_free, b + 1)
                        sp.dma_start(x[:, u], hi[b]).then_inc(s_x[u], 16)
                        sp.dma_start(ys[:, u], yi[b]).then_inc(s_x[u], 16)

            @block.vector
            def _(dve):
                dve.sem_inc(s_free, 2)
                dve.wait_ge(s_c, 16)
                with dve.Fori(0, B // 2) as i:
                    for u in range(2):
                        c = Chain(dve, s_dve)
                        c.link(dve.tensor_copy(pb[:], prob[:, bass.ds(i * 2 + u, 1)]))
                        dve.wait_ge(s_x[u], (i + 1) * 32)
                        dve.wait_ge(s_out[u], i * 16)
                        c.link(dve.scalar_tensor_tensor(o[:, u], ys[:, u], pb[:, 0:1], x[:, u], ALU.mult, ALU.add))
                        dve.sem_inc(s_o, 1)
                        dve.sem_inc(s_free, 1)
                        c.close()

            @block.scalar
            def _(act):
                with act.Fori(0, B // 2) as i:
                    for u in range(2):
                        b = i * 2 + u
                        act.wait_ge(s_o, b + 1)
                        act.dma_start(ho[b], o[:, u]).then_inc(s_out[u], 16)
                for u in range(2):
                    act.wait_ge(s_out[u], B // 2 * 16)


def stage_l2_ffn(nc, A, h_in, h_out):
    xs = nc.dram_tensor("d_l2f_xs", (T, D), F32).ap()
    ys = nc.dram_tensor("d_l2f_ys", (T, D), F32).ap()
    eid = nc.dram_tensor("d_l2f_eid", (1, B), I32).ap()
    prob = nc.dram_tensor("d_l2f_prob", (P, B), F32).ap()
    l2_gate_stage(nc, A, h_in, xs, eid, prob)
    grouped_ffn_stage(nc, A, "l2f", xs, ys, eid, A["L2_ffn_W1"], A["L2_ffn_W2"], A["L2_ffn_b1"], A["L2_ffn_b2"],
                      ACT.Gelu, B, TB)
    l2_add_stage(nc, A, h_in, ys, prob, h_out)


def l3_token_attention_stage(nc, A, h_in, x2_d):
    H, DH = 12, 16
    HF = DH // 2
    NQ = D + 2 * DH
    with ExitStack() as ctx:
        st = Stage(nc, ctx, "l3i")
        x = st.sb("x", [P, 2, TB, D])
        y = st.sb("y", [P, 2, TB, D])
        z = st.sb("z", [P, TB, D])
        o = st.sb("o", [P, 2, TB, D])
        zT = st.sb("zT", [KP, KC, S])
        W = st.sb("W", [KP, KC, NQ])
        bias = st.sb("bias", [P, NQ])
        gb = st.sb("gb", [P, 2, D])
        qkv = st.sb("qkv", [P, TB, NQ])
        cos, sin, cosq, sinq = (st.sb(n, [P, TB, HF]) for n in ("cos", "sin", "cosq", "sinq"))
        ta, tb = st.sb("ta", [P, TB, H, HF]), st.sb("tb", [P, TB, H, HF])
        qr = st.sb("qr", [P, TB, H, DH])
        kr = st.sb("kr", [P, TB, DH])
        sc, mx, ex = (st.sb(n, [P, TB, H]) for n in ("sc", "mx", "ex"))
        ident = st.sb("ident", [P, P])
        stats, mv = st.sb("stats", [P, TB, 6]), st.sb("mv", [P, TB, 2])
        veps, rstd, mhalf = st.sb("veps", [P, TB]), st.sb("rstd", [P, TB]), st.sb("mhalf", [P, TB])
        ps_t = st.ps("ps_t", [P, KC, S])
        ps_p = st.ps("ps_p", [P, TB, 256])
        s_x = [st.sem(f"x{u}") for u in range(2)]
        s_out = [st.sem(f"out{u}") for u in range(2)]
        names = "c xfree var rstd z t tc p sc ex o dve pool ident".split()
        (s_c, s_xfree, s_var, s_rstd, s_z, s_t, s_tc, s_p, s_sc, s_ex, s_o, s_dve, s_pool,
         s_ident) = (st.sem(n) for n in names)
        hi, ho = batch_tiles(h_in), batch_tiles(x2_d)
        with nc.Block() as block:

            @block.sync
            def _(sp):
                loads = [(W[:, :, 0:D], A["L3_attn_Wq"]), (W[:, :, D:D + DH], A["L3_attn_Wk"]),
                         (W[:, :, D + DH:], A["L3_attn_Wv"]),
                         (bias[:, 0:D], A["L3_attn_bq"].partition_broadcast(P)),
                         (bias[:, D:D + DH], A["L3_attn_bk"].partition_broadcast(P)),
                         (bias[:, D + DH:], A["L3_attn_bv"].partition_broadcast(P)),
                         (gb[:, 0, :], A["L3_attn_ln1_g"].partition_broadcast(P)),
                         (gb[:, 1, :], A["L3_attn_ln1_b"].partition_broadcast(P)),
                         (cos[:], A["c_cos"]), (sin[:], A["c_sin"])]
                for to, src in loads:
                    sp.dma_start(to, src).then_inc(s_c, 16)
                sp.dma_start(x[:, 0], hi[0]).then_inc(s_x[0], 16)
                with sp.Fori(0, B // 2) as i:
                    for u in range(2):
                        k = i * 2 + u + 1
                        sp.wait_ge(s_xfree, k)
                        sp.dma_start(x[:, 1 - u], hi[k % B]).then_inc(s_x[1 - u], 16)

            @block.gpsimd
            def _(pool):
                c = Chain(pool, s_pool)
                make_identity(pool, c, ident[:]).then_inc(s_ident, 1)
                c.link(pool.memset(mhalf[:], -0.5))
                with pool.Fori(0, 2 * B + 2) as i:
                    pool.wait_ge(s_var, i + 1)
                    pool.tensor_tensor(rstd[:], veps[:], mhalf[:], ALU.pow).then_inc(s_rstd, 1)

            @block.tensor
            def _(pe):
                pe.wait_ge(s_ident, 1)
                pe.wait_ge(s_c, 160)

                def project(b):
                    pe.wait_ge(s_z, b + 1)
                    for k in range(KC):
                        for t in range(TB):
                            m = pe.transpose(ps_t[0:KP, k, t * P:(t + 1) * P], z[:, t, k * KP:(k + 1) * KP], ident[:])
                    m.then_inc(s_t, 1)
                    pe.wait_ge(s_tc, b + 1)
                    for t in range(TB):
                        for k in range(KC):
                            m = pe.matmul(ps_p[:, t, 0:NQ], zT[:, k, t * P:(t + 1) * P], W[:, k, :],
                                          start=(k == 0), stop=(k == KC - 1))
                    m.then_inc(s_p, 1)

                project(0)
                with pe.Fori(0, B) as b:
                    project(b + 1)

            @block.scalar
            def _(act):
                with act.Fori(0, B // 2) as i:
                    for u in range(2):
                        b = i * 2 + u
                        act.wait_ge(s_sc, b + 1)
                        act.activation(ex[:], sc[:], ACT.Exp).then_inc(s_ex, 1)
                        act.wait_ge(s_o, b + 1)
                        act.dma_start(ho[b], o[:, u]).then_inc(s_out[u], 16)
                for u in range(2):
                    act.wait_ge(s_out[u], B // 2 * 16)

            @block.vector
            def _(dve):
                c = Chain(dve, s_dve)
                dve.sem_inc(s_xfree, 1)
                dve.wait_ge(s_c, 160)
                c.mark(dve.tensor_scalar(cosq[:], cos[:], DH ** -0.5, None, ALU.mult))
                c.mark(dve.tensor_scalar(sinq[:], sin[:], DH ** -0.5, None, ALU.mult))
                c.close()
                hf = [P, TB, H, HF]

                def norms(u, loads, roots):
                    c = Chain(dve, s_dve)
                    yu = y[:, u]
                    dve.wait_ge(s_x[u], loads * 16)
                    norm_stats(dve, c, x[:, u], stats, mv, 1e-5, veps[:]).then_inc(s_var, 1)
                    dve.wait_ge(s_rstd, roots + 1)
                    norm_apply(dve, c, yu, x[:, u], mv, rstd)
                    c.wait()
                    dve.sem_inc(s_xfree, 1)
                    norm_stats(dve, c, yu, stats, mv, 1e-5, veps[:]).then_inc(s_var, 1)
                    dve.wait_ge(s_rstd, roots + 2)
                    norm_apply(dve, c, z, yu, mv, rstd)
                    c.wait()
                    c.link(dve.tensor_tensor(z[:], z[:], bcast(gb[:, 0:1, :], [P, TB, D]), ALU.mult))
                    c.link(dve.tensor_tensor(z[:], z[:], bcast(gb[:, 1:2, :], [P, TB, D]), ALU.add))
                    dve.sem_inc(s_z, 1)
                    c.close()

                def copy_z(b):
                    dve.wait_ge(s_t, b + 1)
                    dve.tensor_copy(zT[:], ps_t[0:KP]).then_inc(s_tc, 1)

                norms(0, 1, 0)
                copy_z(0)
                with dve.Fori(0, B // 2) as i:
                    for u in range(2):
                        b = i * 2 + u
                        c = Chain(dve, s_dve)
                        dve.wait_ge(s_p, b + 1)
                        c.link(dve.tensor_tensor(qkv[:], ps_p[:, :, 0:NQ], bcast(bias[:].unsqueeze(1), [P, TB, NQ]), ALU.add))
                        c.close()
                        norms(1 - u, i + 1 + u, 2 * b + 2)
                        c = Chain(dve, s_dve)
                        q = qkv[:, :, 0:D].rearrange("p t (h a f) -> p t h a f", h=H, a=2)
                        k = qkv[:, :, D:D + DH].rearrange("p t (a f) -> p t a f", a=2)
                        q1, q2, k1, k2 = q[:, :, :, 0, :], q[:, :, :, 1, :], k[:, :, 0, :], k[:, :, 1, :]
                        cq, sq = (bcast(w[:].unsqueeze(2), hf) for w in (cosq, sinq))
                        c.mark(dve.tensor_tensor(ta[:], q1, cq, ALU.mult))
                        c.link(dve.tensor_tensor(tb[:], q2, sq, ALU.mult))
                        c.link(dve.tensor_tensor(qr[:, :, :, 0:HF], ta[:], tb[:], ALU.subtract))
                        c.mark(dve.tensor_tensor(ta[:], q2, cq, ALU.mult))
                        c.link(dve.tensor_tensor(tb[:], q1, sq, ALU.mult))
                        c.link(dve.tensor_tensor(qr[:, :, :, HF:DH], ta[:], tb[:], ALU.add))
                        c.mark(dve.tensor_tensor(ta[:, :, 0, :], k1, cos[:], ALU.mult))
                        c.link(dve.tensor_tensor(tb[:, :, 0, :], k2, sin[:], ALU.mult))
                        c.link(dve.tensor_tensor(kr[:, :, 0:HF], ta[:, :, 0, :], tb[:, :, 0, :], ALU.subtract))
                        c.mark(dve.tensor_tensor(ta[:, :, 0, :], k2, cos[:], ALU.mult))
                        c.link(dve.tensor_tensor(tb[:, :, 0, :], k1, sin[:], ALU.mult))
                        c.link(dve.tensor_tensor(kr[:, :, HF:DH], ta[:, :, 0, :], tb[:, :, 0, :], ALU.add))
                        copy_z(b + 1)
                        c.link(dve.tensor_tensor(qr[:], qr[:], bcast(kr[:].unsqueeze(2), [P, TB, H, DH]), ALU.mult))
                        c.link(dve.tensor_reduce(sc[:], qr[:], AX.X, ALU.add))
                        c.link(dve.tensor_tensor(mx[:], sc[:], sc[:], ALU.max))
                        c.link(dve.tensor_tensor(sc[:], sc[:], mx[:], ALU.subtract))
                        dve.sem_inc(s_sc, 1)
                        dve.wait_ge(s_ex, b + 1)
                        c.link(dve.tensor_scalar(mx[:], ex[:], float(H), None, ALU.mult))
                        c.link(dve.reciprocal(mx[:], mx[:]))
                        c.link(dve.scalar_tensor_tensor(sc[:], ex[:], float(H), mx[:], ALU.mult, ALU.mult))
                        dve.wait_ge(s_out[u], i * 16)
                        v = qkv[:, :, D + DH:]
                        full = [P, TB, H, DH]
                        c.link(dve.tensor_tensor(qr[:], bcast(v.unsqueeze(2), full), bcast(sc[:].unsqueeze(3), full), ALU.mult))
                        c.link(dve.tensor_tensor(o[:, u], qr[:].rearrange("p t h d -> p t (h d)"), y[:, u], ALU.add))
                        dve.sem_inc(s_o, 1)
                        c.close()


def router_stage(nc, A, name, E, h_in, res_d, z_d, xs_d, eid_d, tok_d, w_router, NG, cap=None,
                 moe=None, switch=None):
    with ExitStack() as ctx:
        st = Stage(nc, ctx, name)
        x, o = st.sb("x", [P, 2, TB, D]), st.sb("o", [P, 2, TB, D])
        y = st.sb("y", [P, 2, TB, D])
        z = st.sb("z", [P, NT, D])
        zT = st.sb("zT", [KP, KC, S])
        sq = st.sb("sq", [P, TB, D])
        gb = st.sb("gb", [P, 2, D])
        rb = st.sb("rb", [P, E])
        Wr = st.sb("Wr", [KP, KC, E])
        rank, upper = st.sb("rank", [P, 16]), st.sb("upper", [P, P])
        count = st.sb("count", [P, NG])
        ones, ident = st.sb("ones", [P, P]), st.sb("ident", [P, P])
        zeros = st.sb("zeros", [P, D])
        lg, ex, oh, val, tot, before, run = (st.sb(n, [P, NT, E]) for n in ("lg", "ex", "oh", "val", "tot", "before", "run"))
        m, best = st.sb("m", [P, NT]), st.sb("best", [P, NT])
        tok = st.sb("tok", [P, 3, NT])
        pos = st.sb("pos", [P, NT], I32)
        ntile, start, swap = (st.sb(n, [P, E]) for n in ("ntile", "start", "swap"))
        ge = st.sb("ge", [P, NG, E])
        gsum = st.sb("gsum", [P, NG])
        eid = st.sb("eid", [P, NG], I32)
        stats, mv = st.sb("stats", [P, TB, 6]), st.sb("mv", [P, TB, 2])
        veps, rstd, mhalf = st.sb("veps", [P, TB]), st.sb("rstd", [P, TB]), st.sb("mhalf", [P, TB])
        ps_t = st.ps("ps_t", [P, KC, S])
        ps_l = st.ps("ps_l", [P, TB, E])
        ps_in, ps_tot = st.ps("ps_in", [P, NT, E]), st.ps("ps_tot", [P, NT, E])
        s_x = [st.sem(f"x{u}") for u in range(2)]
        s_out = [st.sem(f"out{u}") for u in range(2)]
        names = "c xfree var rstd z t tc l ex exd oh cnt pos fin zero zd sc dve pool ident fout".split()
        (s_c, s_xfree, s_var, s_rstd, s_z, s_t, s_tc, s_l, s_ex, s_exd, s_oh, s_cnt, s_pos, s_fin, s_zero, s_zd, s_sc,
         s_dve, s_pool, s_ident, s_fout) = (st.sem(n) for n in names)
        hi, ro, zo = batch_tiles(h_in), batch_tiles(res_d), batch_tiles(z_d)
        loads = [(Wr[:], w_router), (rank[:], A["c_rank"]), (upper[:], A["c_upper"]), (count[:], A["c_count"][:, 0:NG])]
        if moe:
            y_d, gamma, beta, bias = moe
            loads += [(gb[:, 0, :], gamma.partition_broadcast(P)), (gb[:, 1, :], beta.partition_broadcast(P)),
                      (rb[:], bias.partition_broadcast(P))]
            yi = batch_tiles(y_d)
        else:
            loads += [(gb[:, 0, :], switch[0].partition_broadcast(P))]
        nx = 2 if moe else 1
        norms = 1 if moe else 2
        with nc.Block() as block:

            @block.sync
            def _(sp):
                for to, src in loads:
                    sp.dma_start(to, src).then_inc(s_c, 16)
                with sp.Fori(0, B // 2) as i:
                    for u in range(2):
                        b = i * 2 + u
                        sp.wait_ge(s_xfree, b + 1)
                        sp.dma_start(x[:, u], hi[b]).then_inc(s_x[u], 16)
                        if moe:
                            sp.dma_start(y[:, u], yi[b]).then_inc(s_x[u], 16)
                sp.wait_ge(s_zero, 1)
                sp.dma_start(xs_d.rearrange("(g p) d -> p g d", p=P),
                             bcast(zeros[:].unsqueeze(1), [P, NG, D])).then_inc(s_zd, 16)
                sp.wait_ge(s_fin, 1)
                sp.dma_start(eid_d[0:1, 0:NG], eid[0:1, :]).then_inc(s_fout, 16)
                sp.dma_start(tok_d, tok[:]).then_inc(s_fout, 16)
                sp.wait_ge(s_fout, 32)

            @block.gpsimd
            def _(pool):
                c = Chain(pool, s_pool)
                make_identity(pool, c, ident[:]).then_inc(s_ident, 1)
                c.link(pool.memset(mhalf[:], -0.5))
                with pool.Fori(0, B * norms) as i:
                    pool.wait_ge(s_var, i + 1)
                    pool.tensor_tensor(rstd[:], veps[:], mhalf[:], ALU.pow).then_inc(s_rstd, 1)
                c.close()
                pool.wait_ge(s_pos, 1)
                pool.wait_ge(s_zd, 16)
                for t in range(NT):
                    pool.indirect_dma_start(out=xs_d, out_offset=bass.IndirectOffsetOnAxis(ap=pos[:, t:t + 1], axis=0),
                                            in_=z[:, t, :], in_offset=None).then_inc(s_sc, 16)
                pool.wait_ge(s_sc, NT * 16)

            @block.tensor
            def _(pe):
                pe.wait_ge(s_ident, 1)
                pe.wait_ge(s_c, 16 * len(loads))
                for b in range(B):
                    pe.wait_ge(s_z, b + 1)
                    for k in range(KC):
                        for t in range(TB):
                            mm = pe.transpose(ps_t[0:KP, k, t * P:(t + 1) * P], z[:, b * TB + t, k * KP:(k + 1) * KP],
                                              ident[:])
                    mm.then_inc(s_t, 1)
                    pe.wait_ge(s_tc, b + 1)
                    for t in range(TB):
                        for k in range(KC):
                            mm = pe.matmul(ps_l[:, t, :], zT[:, k, t * P:(t + 1) * P], Wr[:, k, :],
                                           start=(k == 0), stop=(k == KC - 1))
                    mm.then_inc(s_l, 1)
                pe.wait_ge(s_oh, 1)
                flat = oh[:].rearrange("p t e -> p (t e)")
                pe.matmul(ps_in[:].rearrange("p t e -> p (t e)"), upper[:], flat, start=True, stop=True)
                pe.matmul(ps_tot[:].rearrange("p t e -> p (t e)"), ones[:], flat, start=True, stop=True).then_inc(s_cnt, 1)

            @block.scalar
            def _(act):
                with act.Fori(0, B // 2) as i:
                    for u in range(2):
                        b = i * 2 + u
                        act.wait_ge(s_z, b + 1)
                        act.dma_start(zo[b], z[:, bass.ds(b * TB, TB)]).then_inc(s_out[u], 16)
                        act.dma_start(ro[b], o[:, u]).then_inc(s_out[u], 16)
                for u in range(2):
                    act.wait_ge(s_out[u], B // 2 * 32)
                act.wait_ge(s_ex, 1)
                act.activation(ex[:], ex[:], ACT.Exp).then_inc(s_exd, 1)

            @block.vector
            def _(dve):
                c = Chain(dve, s_dve)
                c.mark(dve.memset(ones[:], 1.0))
                c.link(dve.memset(zeros[:], 0.0))
                dve.sem_inc(s_zero, 1)
                dve.sem_inc(s_xfree, 2)
                dve.wait_ge(s_c, 16 * len(loads))
                c.close()
                full = [P, TB, D]

                def logits(b):
                    c = Chain(dve, s_dve)
                    dve.wait_ge(s_l, b + 1)
                    to = lg[:, b * TB:(b + 1) * TB, :]
                    if moe:
                        c.link(dve.tensor_tensor(to, ps_l[:], bcast(rb[:].unsqueeze(1), [P, TB, E]), ALU.add))
                    else:
                        c.link(dve.tensor_copy(to, ps_l[:]))
                    c.close()

                for i in range(B // 2):
                    for u in range(2):
                        b = i * 2 + u
                        xb, yb, zb, ob = x[:, u], y[:, u], z[:, b * TB:(b + 1) * TB], o[:, u]
                        c = Chain(dve, s_dve)
                        dve.wait_ge(s_x[u], (i + 1) * 16 * nx)
                        dve.wait_ge(s_out[u], i * 32)
                        if moe:
                            norm_stats(dve, c, yb, stats, mv, 1e-5, veps[:]).then_inc(s_var, 1)
                            c.mark(dve.tensor_tensor(ob, xb, yb, ALU.add))
                            dve.wait_ge(s_rstd, b + 1)
                            norm_apply(dve, c, zb, yb, mv, rstd)
                            c.wait()
                            c.link(dve.tensor_tensor(zb, zb, bcast(gb[:, 0:1, :], full), ALU.mult))
                            c.link(dve.tensor_tensor(zb, zb, bcast(gb[:, 1:2, :], full), ALU.add))
                        else:
                            norm_stats(dve, c, xb, stats, mv, 1e-5, veps[:]).then_inc(s_var, 1)
                            dve.wait_ge(s_rstd, 2 * b + 1)
                            norm_apply(dve, c, yb, xb, mv, rstd)
                            c.wait()
                            c.mark(dve.tensor_tensor(ob, xb, yb, ALU.add))
                            c.link(dve.tensor_tensor(sq[:], yb, yb, ALU.mult))
                            c.link(dve.tensor_reduce(veps[:], sq[:], AX.X, ALU.add))
                            dve.tensor_scalar(veps[:], veps[:], 1.0 / D, 1e-6, ALU.mult, ALU.add).then_inc(s_var, 1)
                            dve.wait_ge(s_rstd, 2 * b + 2)
                            for t in range(TB):
                                c.mark(dve.tensor_scalar(zb[:, t, :], yb[:, t, :], rstd[:, t:t + 1], None, ALU.mult))
                            c.wait()
                            c.link(dve.tensor_tensor(zb, zb, bcast(gb[:, 0:1, :], full), ALU.mult))
                        dve.sem_inc(s_z, 1)
                        dve.sem_inc(s_xfree, 1)
                        c.close()
                        if b > 0:
                            logits(b - 1)
                        dve.wait_ge(s_t, b + 1)
                        dve.tensor_copy(zT[:], ps_t[0:KP]).then_inc(s_tc, 1)
                logits(B - 1)
                c = Chain(dve, s_dve)

                def act_turn():
                    dve.sem_inc(s_ex, 1)
                    dve.wait_ge(s_exd, 1)

                top1(dve, act_turn, c, lg[:], (NT, E), m, oh, val, rank, best, ex, tok[:, 1, :])
                dve.sem_inc(s_oh, 1)
                dve.wait_ge(s_cnt, 1)
                c.mark(dve.tensor_copy(tot[:], ps_tot[:]))
                c.link(dve.tensor_copy(run[:], ps_tot[:]))
                src, dst, s = run, before, 1
                while s < NT:
                    c.mark(dve.tensor_tensor(dst[:, s:, :], src[:, s:, :], src[:, 0:NT - s, :], ALU.add))
                    c.link(dve.tensor_copy(dst[:, 0:s, :], src[:, 0:s, :]))
                    src, dst, s = dst, src, 2 * s
                c.link(dve.tensor_copy(ntile[:], src[:, NT - 1, :]))
                c.link(dve.tensor_tensor(dst[:], src[:], tot[:], ALU.subtract))
                bef = dst
                c.link(dve.tensor_scalar(ntile[:], ntile[:], 1.0 / P, 0.5 - 1.0 / (2 * P), ALU.mult, ALU.add))
                c.link(dve.tensor_scalar(ntile[:], ntile[:], ROUND, None, ALU.add))
                c.link(dve.tensor_scalar(ntile[:], ntile[:], ROUND, None, ALU.subtract))
                c.link(dve.tensor_copy(start[:], ntile[:]))
                a, d, s = start, swap, 1
                while s < E:
                    c.mark(dve.tensor_tensor(d[:, s:], a[:, s:], a[:, 0:E - s], ALU.add))
                    c.link(dve.tensor_copy(d[:, 0:s], a[:, 0:s]))
                    a, d, s = d, a, 2 * s
                c.link(dve.tensor_tensor(ge[:], bcast(a[:].unsqueeze(1), [P, NG, E]),
                                         bcast(count[:].unsqueeze(2), [P, NG, E]), ALU.is_le))
                c.link(dve.tensor_reduce(gsum[:], ge[:], AX.X, ALU.add))
                c.link(dve.tensor_scalar(gsum[:], gsum[:], float(E - 1), None, ALU.min))
                c.link(dve.tensor_copy(eid[:], gsum[:]))
                c.link(dve.tensor_tensor(d[:], a[:], ntile[:], ALU.subtract))
                c.link(dve.tensor_scalar(d[:], d[:], float(P), None, ALU.mult))
                c.link(dve.tensor_tensor(tot[:], bef[:], ps_in[:], ALU.add))
                c.link(dve.tensor_tensor(val[:], tot[:], bcast(d[:].unsqueeze(1), [P, NT, E]), ALU.add))
                c.link(dve.tensor_tensor(val[:], val[:], oh[:], ALU.mult))
                c.link(dve.tensor_reduce(tok[:, 0, :], val[:], AX.X, ALU.add))
                c.link(dve.tensor_copy(pos[:], tok[:, 0, :]))
                dve.sem_inc(s_pos, 1)
                if cap is None:
                    c.link(dve.memset(tok[:, 2, :], 1.0))
                else:
                    by_batch = [P, B, TB, E]
                    tb = tot[:].rearrange("p (b t) e -> p b t e", t=TB)
                    bb = bef[:].rearrange("p (b t) e -> p b t e", t=TB)
                    vb = val[:].rearrange("p (b t) e -> p b t e", t=TB)
                    c.link(dve.tensor_tensor(vb, tb, bcast(bb[:, :, 0:1, :], by_batch), ALU.subtract))
                    c.link(dve.tensor_tensor(val[:], val[:], oh[:], ALU.mult))
                    c.link(dve.tensor_reduce(m[:], val[:], AX.X, ALU.add))
                    c.link(dve.tensor_scalar(tok[:, 2, :], m[:], float(cap), None, ALU.is_lt))
                dve.sem_inc(s_fin, 1)
                c.close()


def gather_stage(nc, A, name, res_d, ys_d, tok_d, h_out, z_d=None):
    with ExitStack() as ctx:
        st = Stage(nc, ctx, name)
        x, ys, z, o = (st.sb(n, [P, 2, TB, D]) for n in ("x", "ys", "z", "o"))
        tok = st.sb("tok", [P, 3, NT])
        cut = st.sb("cut", [P, 2, NT])
        pos = st.sb("pos", [P, NT], I32)
        row = st.sb("row", [P, 2, TB], I32)
        fac = st.sb("fac", [P, 2, TB])
        s_x = [st.sem(f"x{u}") for u in range(2)]
        s_g = [st.sem(f"g{u}") for u in range(2)]
        s_out = [st.sem(f"out{u}") for u in range(2)]
        s_c, s_pos, s_free, s_o, s_dve, s_pool = (st.sem(n) for n in ("c", "pos", "free", "o", "dve", "pool"))
        ri, ho = batch_tiles(res_d), batch_tiles(h_out)
        zi = batch_tiles(z_d) if z_d is not None else None
        nx = 1 if z_d is None else 2
        with nc.Block() as block:

            @block.sync
            def _(sp):
                sp.dma_start(tok[:], tok_d).then_inc(s_c, 16)
                with sp.Fori(0, B // 2) as i:
                    for u in range(2):
                        b = i * 2 + u
                        sp.wait_ge(s_free, b + 1)
                        sp.dma_start(x[:, u], ri[b]).then_inc(s_x[u], 16)
                        if z_d is not None:
                            sp.dma_start(z[:, u], zi[b]).then_inc(s_x[u], 16)

            @block.gpsimd
            def _(pool):
                pool.wait_ge(s_pos, 1)
                with pool.Fori(0, B // 2) as i:
                    for u in range(2):
                        b = i * 2 + u
                        c = Chain(pool, s_pool)
                        pool.wait_ge(s_free, b + 1)
                        c.link(pool.tensor_copy(row[:, u], pos[:, bass.ds(b * TB, TB)]))
                        for t in range(TB):
                            pool.indirect_dma_start(out=ys[:, u, t, :], out_offset=None, in_=ys_d,
                                                    in_offset=bass.IndirectOffsetOnAxis(ap=row[:, u, t:t + 1], axis=0)
                                                    ).then_inc(s_g[u], 16)
                        c.close()

            @block.vector
            def _(dve):
                c = Chain(dve, s_dve)
                dve.wait_ge(s_c, 16)
                c.link(dve.tensor_copy(pos[:], tok[:, 0, :]))
                dve.sem_inc(s_pos, 1)
                dve.sem_inc(s_free, 2)
                c.link(dve.tensor_tensor(cut[:, 0, :], tok[:, 1, :], tok[:, 2, :], ALU.mult))
                c.link(dve.tensor_tensor(cut[:, 1, :], tok[:, 1, :], cut[:, 0, :], ALU.subtract))
                c.close()
                with dve.Fori(0, B // 2) as i:
                    for u in range(2):
                        b = i * 2 + u
                        c = Chain(dve, s_dve)
                        dve.wait_ge(s_x[u], (i + 1) * 16 * nx)
                        dve.wait_ge(s_g[u], (i + 1) * 16 * TB)
                        dve.wait_ge(s_out[u], i * 16)
                        if z_d is None:
                            c.link(dve.tensor_tensor(o[:, u], x[:, u], ys[:, u], ALU.add))
                        else:
                            c.link(dve.tensor_copy(fac[:], cut[:, :, bass.ds(b * TB, TB)]))
                            for t in range(TB):
                                c.mark(dve.scalar_tensor_tensor(x[:, u, t, :], ys[:, u, t, :], fac[:, 0, t:t + 1],
                                                                x[:, u, t, :], ALU.mult, ALU.add))
                            c.wait()
                            for t in range(TB):
                                c.mark(dve.scalar_tensor_tensor(o[:, u, t, :], z[:, u, t, :], fac[:, 1, t:t + 1],
                                                                x[:, u, t, :], ALU.mult, ALU.add))
                            c.wait()
                        dve.sem_inc(s_o, 1)
                        dve.sem_inc(s_free, 1)
                        c.close()

            @block.scalar
            def _(act):
                with act.Fori(0, B // 2) as i:
                    for u in range(2):
                        b = i * 2 + u
                        act.wait_ge(s_o, b + 1)
                        act.dma_start(ho[b], o[:, u]).then_inc(s_out[u], 16)
                for u in range(2):
                    act.wait_ge(s_out[u], B // 2 * 16)


def stage_l3_attention(nc, A, h_in, h_out):
    E = 8
    NG = NT + E
    y = nc.dram_tensor("d_l3_y", (T, D), F32).ap()
    res = nc.dram_tensor("d_l3_res", (T, D), F32).ap()
    z = nc.dram_tensor("d_l3_z", (T, D), F32).ap()
    xs = nc.dram_tensor("d_l3_xs", (NG * P, D), F32).ap()
    ys = nc.dram_tensor("d_l3_ys", (NG * P, D), F32).ap()
    eid = nc.dram_tensor("d_l3_eid", (1, NG), I32).ap()
    tok = nc.dram_tensor("d_l3_tok", (P, 3, NT), F32).ap()
    l3_token_attention_stage(nc, A, h_in, y)
    router_stage(nc, A, "l3r", E, h_in, res, z, xs, eid, tok, A["L3_attn_Wg"], NG,
                 moe=(y, A["L3_attn_ln2_g"], A["L3_attn_ln2_b"], A["L3_attn_bg"]))
    grouped_ffn_stage(nc, A, "l3m", xs, ys, eid, A["L3_attn_W1"], A["L3_attn_W2"], A["L3_attn_b1"], A["L3_attn_b2"],
                      ACT.Gelu, NG, 1)
    gather_stage(nc, A, "l3g", res, ys, tok, h_out)


def stage_l3_ffn(nc, A, h_in, h_out):
    E = 16
    NG = NT + E
    res = nc.dram_tensor("d_l4_res", (T, D), F32).ap()
    z = nc.dram_tensor("d_l4_z", (T, D), F32).ap()
    xs = nc.dram_tensor("d_l4_xs", (NG * P, D), F32).ap()
    ys = nc.dram_tensor("d_l4_ys", (NG * P, D), F32).ap()
    eid = nc.dram_tensor("d_l4_eid", (1, NG), I32).ap()
    tok = nc.dram_tensor("d_l4_tok", (P, 3, NT), F32).ap()
    router_stage(nc, A, "l4r", E, h_in, res, z, xs, eid, tok, A["L3_ffn_w_router"], NG, cap=64,
                 switch=(A["L3_ffn_ln_w"],))
    grouped_ffn_stage(nc, A, "l4m", xs, ys, eid, A["L3_ffn_wi"], A["L3_ffn_wo"], None, None, ACT.Relu, NG, 1)
    gather_stage(nc, A, "l4g", res, ys, tok, h_out, z)


def stage_l0_attention(nc, A, h_in, h_out):
    xT = nc.dram_tensor("d_l0a_xT", (B, KP, KC, S), F32).ap()
    wq = nc.dram_tensor("d_l0a_wqkv", (KP, KC, 2304), F32).ap()
    wo = nc.dram_tensor("d_l0a_wout", (P, 6, D), F32).ap()
    att = nc.dram_tensor("d_l0a_att", (B + 1, S, 768), F32).ap()
    thr = nc.dram_tensor("d_l0a_thr", (B + 1, P, TB), F32).ap()
    ternary_stage(nc, A, "l0t", [(A["L0_attn_w_qkv"].rearrange("p k n -> p (k n)"), wq.rearrange("p k n -> p (k n)")),
                                 (A["L0_attn_w_out"].rearrange("p k n -> p (k n)"), wo.rearrange("p k n -> p (k n)"))])
    sparse_inputs_stage(nc, A, "l0i", h_in, xT, A["L0_attn_gamma"], A["L0_attn_beta"], A["L0_attn_sparsity"])
    attention_stage(nc, A, "l0a", xT, wq, att, thr_d=thr, sparsity=A["L0_attn_sparsity"])
    attention_output_stage(nc, A, "l0o", att, wo, A["L0_attn_b_out"], h_in, h_out, thr)


def stage_l2_attention(nc, A, h_in, h_out):
    xT = nc.dram_tensor("d_l2a_xT", (B, KP, KC, S), F32).ap()
    att = nc.dram_tensor("d_l2a_att", (B + 1, S, 768), F32).ap()
    attention_inputs_stage(nc, A, "l2i", h_in, xT)
    attention_stage(nc, A, "l2a", xT, A["L2_attn_qkv_w"], att, A["L2_attn_qkv_b"])
    attention_output_stage(nc, A, "l2o", att, A["L2_attn_proj_w"], A["L2_attn_proj_b"], h_in, h_out)


STAGES = {7: stage_l3_attention, 8: stage_l3_ffn, 4: stage_l1_ffn, 6: stage_l2_ffn, 0: embedding_stage, 3: stage_l1_attention, 1: stage_l0_attention, 2: quant_linear_stage, 5: stage_l2_attention}


def build_tower(nc, A, out, first=0, last=8):
    h = A["h_start"] if first else None
    for n in range(first, last + 1):
        to = out if n == last else nc.dram_tensor(f"d_h{n}", (T, D), F32).ap()
        STAGES[n](nc, A, h, to)
        h = to


def shape_constants():
    row, col = np.arange(KP)[:, None], np.arange(6 * 64)[None, :]
    half = np.where(row // 16 == col // 64, -0.5, 0.0)
    row, col = np.arange(P)[:, None], np.arange(34)[None, :]
    kvmask = np.where(row // 64 == col // 17, 1 / 64, 0.0)
    rank = np.broadcast_to(16.0 - np.arange(16), (P, 16))
    upper = np.arange(P)[:, None] < np.arange(P)[None, :]
    count = np.broadcast_to(np.arange(NT + 16), (P, NT + 16))
    inv_freq = (1.0 / 10000.0 ** (np.arange(0, 16, 2, dtype=np.float32) / 16)).astype(np.float32)
    angle = np.arange(S, dtype=np.float32)[:, None] * inv_freq[None, :]
    angle = angle.reshape(TB, P, 8).transpose(1, 0, 2)
    return {"c_upper": upper.astype(np.float32), "c_count": count.astype(np.float32),
            "c_cos": np.cos(angle).astype(np.float32), "c_sin": np.sin(angle).astype(np.float32),
            "c_rank": rank.astype(np.float32), "c_half": half.astype(np.float32), "c_kvmask": kvmask.astype(np.float32)}


def declare_inputs(nc, inputs):
    def rows(p):
        return lambda a: a.reshape(-1, p, a.shape[-1]).transpose(1, 0, 2)

    layout = {
        "L0_attn_w_qkv": lambda a: rows(KP)(a.T), "L0_attn_w_out": lambda a: rows(P)(a.T),
        "L2_attn_qkv_w": lambda a: rows(KP)(a.T), "L2_attn_proj_w": lambda a: rows(P)(a.T),
        "L0_attn_sparsity": lambda a: a.reshape(1),
        "L0_ffn_weight_t": lambda a: a.view(np.int32),
        "L1_attn_W_qkv": rows(KP), "L1_attn_W_proj": rows(KP), "L1_attn_random_features": lambda a: a.T,
    }
    def expert_rows(p):
        return lambda a: a.reshape(a.shape[0], -1, p, a.shape[-1]).transpose(2, 0, 1, 3)

    def by_expert(p):
        return lambda a: a.reshape(a.shape[0], -1, p, a.shape[-1]).transpose(0, 2, 1, 3)

    def bias_rows(a):
        return a.reshape(a.shape[0], -1, P).transpose(0, 2, 1)

    layout.update({
        "L1_ffn_shared_gate": rows(KP), "L1_ffn_shared_up": rows(KP), "L1_ffn_shared_down": rows(P),
        "L1_ffn_routed_gate": expert_rows(KP), "L1_ffn_routed_up": expert_rows(KP),
        "L1_ffn_routed_down": expert_rows(P), "L1_ffn_router_w": rows(KP),
        "L2_ffn_Wg": lambda a: rows(KP)(a.T), "L2_ffn_W1": by_expert(KP), "L2_ffn_W2": by_expert(P),
        "L2_ffn_b1": bias_rows,
        "L3_attn_Wq": rows(KP), "L3_attn_Wk": rows(KP), "L3_attn_Wv": rows(KP), "L3_attn_Wg": rows(KP),
        "L3_attn_W1": by_expert(KP), "L3_attn_W2": by_expert(P), "L3_attn_b1": bias_rows,
        "L3_ffn_w_router": rows(KP), "L3_ffn_wi": by_expert(KP), "L3_ffn_wo": by_expert(P),
    })
    inputs = dict(inputs, **shape_constants())
    arrays, A = {}, {}
    for name, a in inputs.items():
        a = np.ascontiguousarray(layout.get(name, lambda a: a)(np.asarray(a)))
        arrays[f"in_{name}_dram"] = a
        A[name] = nc.dram_tensor(f"in_{name}_dram", a.shape, mybir.dt.from_np(a.dtype), kind="ExternalInput").ap()
    return arrays, A


def kernel(**inputs):
    import concourse.bacc as bacc
    from concourse.bass_utils import run_bass_kernel_spmd as run

    nc = bacc.Bacc("TRN2", target_bir_lowering=False, num_devices=1)
    arrays, A = declare_inputs(nc, inputs)
    out = nc.dram_tensor("out_0_dram", (T, D), F32, kind="ExternalOutput").ap()
    build_tower(nc, A, out)
    r = run(nc, [arrays], core_ids=[0])
    return r.results[0]["out_0_dram"].reshape(B, S, D)
```
